# Optimizing a Trainium2 kernel written in Bass

```python
import numpy as np
import jax
import jax.numpy as jnp

def _softmax(x, axis=-1):
    return jax.nn.softmax(x, axis=axis)

def _gelu(x):
    return jax.nn.gelu(x, approximate=True)

def _silu(x):
    return jax.nn.silu(x)

def _sigmoid(x):
    return jax.nn.sigmoid(x)

def _layernorm(x, axis=-1, eps=1e-05):
    m = jnp.mean(x, axis=axis, keepdims=True)
    v = jnp.var(x, axis=axis, keepdims=True)
    return (x - m) / jnp.sqrt(v + eps)

def _scatter_add(tgt, idx, src, axis=0):
    return tgt.at[idx].add(src)

def _segment_sum(src, seg, n):
    return jax.ops.segment_sum(src, seg, n)
kernel_name = 'mk_prb_d2_jaxref_r8_5e99e5'

def setup_inputs(seed: int=0):
    np.random.seed(seed)
    _w = jnp.asarray

    def _L0_attn_setup():
        import jax, jax.numpy as jnp
        import numpy as np
        B, L, D, H, W = (2, 512, 128, 16, 128)
        E = D // H

        def _ln(x, g, b):
            m = jnp.mean(x, axis=-1, keepdims=True)
            v = jnp.mean((x - m) ** 2, axis=-1, keepdims=True)
            return (x - m) / jnp.sqrt(v + 1e-05) * g + b

        def _swa(xn, Wqkv, bqkv, Wp, bp):
            b_, l_, d_ = xn.shape
            nb = l_ // W
            qkv = xn @ Wqkv + bqkv
            q, k, v = jnp.split(qkv, 3, axis=-1)

            def heads(t):
                return t.reshape(b_, l_, H, E).transpose(0, 2, 1, 3)
            q, k, v = (heads(q), heads(k), heads(v))

            def blk(t):
                return t.reshape(b_, H, nb, W, E)
            qb, kb, vb = (blk(q), blk(k), blk(v))
            kprev = jnp.pad(kb, ((0, 0), (0, 0), (1, 0), (0, 0), (0, 0)))[:, :, :nb]
            vprev = jnp.pad(vb, ((0, 0), (0, 0), (1, 0), (0, 0), (0, 0)))[:, :, :nb]
            kc = jnp.concatenate([kprev, kb], axis=3)
            vc = jnp.concatenate([vprev, vb], axis=3)
            scores = jnp.einsum('bhnre,bhnse->bhnrs', qb, kc) / np.float32(np.sqrt(E))
            r = jnp.arange(W)[:, None]
            s = jnp.arange(2 * W)[None, :]
            band = (s >= r + 1) & (s <= r + W)
            first = band & (s >= W)
            mask = jnp.concatenate([first[None], jnp.broadcast_to(band, (nb - 1, W, 2 * W))], axis=0)
            scores = jnp.where(mask[None, None], scores, jnp.float32(-1e+30))
            attn = jax.nn.softmax(scores, axis=-1)
            out = jnp.einsum('bhnrs,bhnse->bhnre', attn, vc)
            out = out.reshape(b_, H, l_, E).transpose(0, 2, 1, 3).reshape(b_, l_, d_)
            return out @ Wp + bp

        def _linattn(xn, Wqkv, bqkv, Wo, bo):
            b_, l_, d_ = xn.shape
            C = 128
            nc = l_ // C
            qkv = xn @ Wqkv + bqkv
            q, k, v = jnp.split(qkv, 3, axis=-1)
            q = q.reshape(b_, l_, H, E)
            k = k.reshape(b_, l_, H, E)
            v = v.reshape(b_, l_, H, E)
            q = jax.nn.elu(q * np.float32(E ** (-0.5))) + np.float32(1.0001)
            k = jax.nn.elu(k) + np.float32(1.0001)

            def chunks(t):
                return t.reshape(b_, nc, C, H, E).transpose(1, 0, 3, 2, 4)
            qc, kc, vc = (chunks(q), chunks(k), chunks(v))
            tril = jnp.tril(jnp.ones((C, C), jnp.float32))

            def step(carry, inp):
                S, z = carry
                qi, ki, vi = inp
                A = jnp.einsum('bhce,bhde->bhcd', qi, ki) * tril
                num = jnp.einsum('bhce,bhef->bhcf', qi, S) + jnp.einsum('bhcd,bhdf->bhcf', A, vi)
                den = jnp.einsum('bhce,bhe->bhc', qi, z) + A.sum(-1)
                o = num / (den[..., None] + 1e-06)
                S = S + jnp.einsum('bhce,bhcf->bhef', ki, vi)
                z = z + ki.sum(2)
                return ((S, z), o)
            S0 = jnp.zeros((b_, H, E, E), jnp.float32)
            z0 = jnp.zeros((b_, H, E), jnp.float32)
            _, out = jax.lax.scan(step, (S0, z0), (qc, kc, vc))
            out = out.transpose(1, 0, 3, 2, 4).reshape(b_, l_, d_)
            return out @ Wo + bo
        key = jax.random.key(seed)
        ks = jax.random.split(key, 9)

        def w(k, shape, s=0.02):
            return jax.random.normal(k, shape, jnp.float32) * s
        return {'x': jax.random.normal(ks[0], (B, L, D), jnp.float32), 'g1': jnp.ones((D,), jnp.float32), 'b1': jnp.zeros((D,), jnp.float32), 'Wqkv_a': w(ks[1], (D, 3 * D)), 'bqkv_a': jnp.zeros((3 * D,), jnp.float32), 'Wp_a': w(ks[2], (D, D)), 'bp_a': jnp.zeros((D,), jnp.float32), 'Wqkv_s': w(ks[3], (D, 3 * D)), 'bqkv_s': jnp.zeros((3 * D,), jnp.float32), 'Wo_s': w(ks[4], (D, D)), 'bo_s': jnp.zeros((D,), jnp.float32), 'Wo': w(ks[5], (D, D)), 'bo': jnp.zeros((D,), jnp.float32), 'gm': jnp.ones((D,), jnp.float32), 'bm': jnp.zeros((D,), jnp.float32), 'W1': w(ks[6], (D, 4 * D)), 'b1m': jnp.zeros((4 * D,), jnp.float32), 'W2': w(ks[7], (4 * D, D)), 'b2m': jnp.zeros((D,), jnp.float32)}
    _L0_attn_in = _L0_attn_setup()

    def _L0_ffn_setup():
        import jax, jax.numpy as jnp
        import numpy as np
        HIDDEN = 128
        NUM_EXPERTS = 8
        TOP_K = 2
        BATCH, SEQ = (4, 512)
        key = jax.random.key(seed)
        ks = jax.random.split(key, 7)
        s = 0.02
        x = jax.random.normal(ks[0], (BATCH, SEQ, HIDDEN), dtype=jnp.float32)
        router_w = jax.random.normal(ks[1], (HIDDEN, NUM_EXPERTS), dtype=jnp.float32) * s
        router_b = jnp.zeros((NUM_EXPERTS,), dtype=jnp.float32)
        w1 = jax.random.normal(ks[2], (NUM_EXPERTS, HIDDEN, 2 * HIDDEN), dtype=jnp.float32) * s
        b1 = jnp.zeros((NUM_EXPERTS, 2 * HIDDEN), dtype=jnp.float32)
        w2 = jax.random.normal(ks[3], (NUM_EXPERTS, 2 * HIDDEN, HIDDEN), dtype=jnp.float32) * s
        b2 = jnp.zeros((NUM_EXPERTS, HIDDEN), dtype=jnp.float32)
        return {'x': x, 'router_w': router_w, 'router_b': router_b, 'w1': w1, 'b1': b1, 'w2': w2, 'b2': b2}
    _L0_ffn_in = _L0_ffn_setup()

    def _L1_attn_setup():
        import jax, jax.numpy as jnp
        import numpy as np
        B, N, D, H = (8, 512, 128, 16)
        HD = D // H
        EPS = 1e-05
        key = jax.random.key(seed)
        ks = jax.random.split(key, 18)
        s = 1.0 / np.sqrt(D)

        def lin(k):
            return (jax.random.normal(k, (D, D), jnp.float32) * s, jnp.zeros((D,), jnp.float32))
        Wg_w, Wg_b = lin(ks[0])
        Wr_w, Wr_b = lin(ks[1])
        Wk_w, Wk_b = lin(ks[2])
        Wv_w, Wv_b = lin(ks[3])
        Wo_w, Wo_b = lin(ks[4])
        mg = jax.random.uniform(ks[5], (D,), jnp.float32)
        mr = jax.random.uniform(ks[6], (D,), jnp.float32)
        mk = jax.random.uniform(ks[7], (D,), jnp.float32)
        mv = jax.random.uniform(ks[8], (D,), jnp.float32)
        w = jax.random.normal(ks[9], (H, HD), jnp.float32)
        u = jax.random.normal(ks[10], (H, HD), jnp.float32)
        x = jax.random.normal(ks[11], (B, N, D), jnp.float32)
        return {'x': x, 'Wg_w': Wg_w, 'Wg_b': Wg_b, 'Wr_w': Wr_w, 'Wr_b': Wr_b, 'Wk_w': Wk_w, 'Wk_b': Wk_b, 'Wv_w': Wv_w, 'Wv_b': Wv_b, 'Wo_w': Wo_w, 'Wo_b': Wo_b, 'mg': mg, 'mr': mr, 'mk': mk, 'mv': mv, 'w': w, 'u': u}
    _L1_attn_in = _L1_attn_setup()

    def _L1_ffn_setup():
        import jax, jax.numpy as jnp
        import numpy as np
        B, S, D, H, E = (2, 256, 128, 512, 8)
        key = jax.random.key(seed)
        k0, k1, k2, k3 = jax.random.split(key, 4)
        x = jax.random.normal(k0, (B, S, D), dtype=jnp.float32)
        router_w = jax.random.normal(k1, (E, D), dtype=jnp.float32) * 0.02
        w1 = jax.random.normal(k2, (E, D, H), dtype=jnp.float32) * 0.02
        w2 = jax.random.normal(k3, (E, H, D), dtype=jnp.float32) * 0.02
        return {'x': x, 'router_w': router_w, 'w1': w1, 'w2': w2}
    _L1_ffn_in = _L1_ffn_setup()
    _d = {'L0_attn_x': _L0_attn_in['x'], 'L0_attn_g1': _L0_attn_in['g1'], 'L0_attn_b1': _L0_attn_in['b1'], 'L0_attn_Wqkv_a': _L0_attn_in['Wqkv_a'], 'L0_attn_bqkv_a': _L0_attn_in['bqkv_a'], 'L0_attn_Wp_a': _L0_attn_in['Wp_a'], 'L0_attn_bp_a': _L0_attn_in['bp_a'], 'L0_attn_Wqkv_s': _L0_attn_in['Wqkv_s'], 'L0_attn_bqkv_s': _L0_attn_in['bqkv_s'], 'L0_attn_Wo_s': _L0_attn_in['Wo_s'], 'L0_attn_bo_s': _L0_attn_in['bo_s'], 'L0_attn_Wo': _L0_attn_in['Wo'], 'L0_attn_bo': _L0_attn_in['bo'], 'L0_attn_gm': _L0_attn_in['gm'], 'L0_attn_bm': _L0_attn_in['bm'], 'L0_attn_W1': _L0_attn_in['W1'], 'L0_attn_b1m': _L0_attn_in['b1m'], 'L0_attn_W2': _L0_attn_in['W2'], 'L0_attn_b2m': _L0_attn_in['b2m'], 'L0_ffn_router_w': _L0_ffn_in['router_w'], 'L0_ffn_router_b': _L0_ffn_in['router_b'], 'L0_ffn_w1': _L0_ffn_in['w1'], 'L0_ffn_b1': _L0_ffn_in['b1'], 'L0_ffn_w2': _L0_ffn_in['w2'], 'L0_ffn_b2': _L0_ffn_in['b2'], 'L1_attn_Wg_w': _L1_attn_in['Wg_w'], 'L1_attn_Wg_b': _L1_attn_in['Wg_b'], 'L1_attn_Wr_w': _L1_attn_in['Wr_w'], 'L1_attn_Wr_b': _L1_attn_in['Wr_b'], 'L1_attn_Wk_w': _L1_attn_in['Wk_w'], 'L1_attn_Wk_b': _L1_attn_in['Wk_b'], 'L1_attn_Wv_w': _L1_attn_in['Wv_w'], 'L1_attn_Wv_b': _L1_attn_in['Wv_b'], 'L1_attn_Wo_w': _L1_attn_in['Wo_w'], 'L1_attn_Wo_b': _L1_attn_in['Wo_b'], 'L1_attn_mg': _L1_attn_in['mg'], 'L1_attn_mr': _L1_attn_in['mr'], 'L1_attn_mk': _L1_attn_in['mk'], 'L1_attn_mv': _L1_attn_in['mv'], 'L1_attn_w': _L1_attn_in['w'], 'L1_attn_u': _L1_attn_in['u'], 'L1_ffn_router_w': _L1_ffn_in['router_w'], 'L1_ffn_w1': _L1_ffn_in['w1'], 'L1_ffn_w2': _L1_ffn_in['w2']}
    _x0 = _d['L0_attn_x']
    _d['L0_attn_x'] = jax.random.normal(jax.random.fold_in(jax.random.key(seed), 1), (8, 1024, 128), dtype=_x0.dtype)
    del _x0
    return _d

def reference(L0_attn_x, L0_attn_g1, L0_attn_b1, L0_attn_Wqkv_a, L0_attn_bqkv_a, L0_attn_Wp_a, L0_attn_bp_a, L0_attn_Wqkv_s, L0_attn_bqkv_s, L0_attn_Wo_s, L0_attn_bo_s, L0_attn_Wo, L0_attn_bo, L0_attn_gm, L0_attn_bm, L0_attn_W1, L0_attn_b1m, L0_attn_W2, L0_attn_b2m, L0_ffn_router_w, L0_ffn_router_b, L0_ffn_w1, L0_ffn_b1, L0_ffn_w2, L0_ffn_b2, L1_attn_Wg_w, L1_attn_Wg_b, L1_attn_Wr_w, L1_attn_Wr_b, L1_attn_Wk_w, L1_attn_Wk_b, L1_attn_Wv_w, L1_attn_Wv_b, L1_attn_Wo_w, L1_attn_Wo_b, L1_attn_mg, L1_attn_mr, L1_attn_mk, L1_attn_mv, L1_attn_w, L1_attn_u, L1_ffn_router_w, L1_ffn_w1, L1_ffn_w2):

    def _L0_attn_ref(x, g1, b1, Wqkv_a, bqkv_a, Wp_a, bp_a, Wqkv_s, bqkv_s, Wo_s, bo_s, Wo, bo, gm, bm, W1, b1m, W2, b2m):
        import jax, jax.numpy as jnp
        import numpy as np
        B, L, D, H, W = (2, 512, 128, 16, 128)
        E = D // H

        def _ln(x, g, b):
            m = jnp.mean(x, axis=-1, keepdims=True)
            v = jnp.mean((x - m) ** 2, axis=-1, keepdims=True)
            return (x - m) / jnp.sqrt(v + 1e-05) * g + b

        def _swa(xn, Wqkv, bqkv, Wp, bp):
            b_, l_, d_ = xn.shape
            nb = l_ // W
            qkv = xn @ Wqkv + bqkv
            q, k, v = jnp.split(qkv, 3, axis=-1)

            def heads(t):
                return t.reshape(b_, l_, H, E).transpose(0, 2, 1, 3)
            q, k, v = (heads(q), heads(k), heads(v))

            def blk(t):
                return t.reshape(b_, H, nb, W, E)
            qb, kb, vb = (blk(q), blk(k), blk(v))
            kprev = jnp.pad(kb, ((0, 0), (0, 0), (1, 0), (0, 0), (0, 0)))[:, :, :nb]
            vprev = jnp.pad(vb, ((0, 0), (0, 0), (1, 0), (0, 0), (0, 0)))[:, :, :nb]
            kc = jnp.concatenate([kprev, kb], axis=3)
            vc = jnp.concatenate([vprev, vb], axis=3)
            scores = jnp.einsum('bhnre,bhnse->bhnrs', qb, kc) / np.float32(np.sqrt(E))
            r = jnp.arange(W)[:, None]
            s = jnp.arange(2 * W)[None, :]
            band = (s >= r + 1) & (s <= r + W)
            first = band & (s >= W)
            mask = jnp.concatenate([first[None], jnp.broadcast_to(band, (nb - 1, W, 2 * W))], axis=0)
            scores = jnp.where(mask[None, None], scores, jnp.float32(-1e+30))
            attn = jax.nn.softmax(scores, axis=-1)
            out = jnp.einsum('bhnrs,bhnse->bhnre', attn, vc)
            out = out.reshape(b_, H, l_, E).transpose(0, 2, 1, 3).reshape(b_, l_, d_)
            return out @ Wp + bp

        def _linattn(xn, Wqkv, bqkv, Wo, bo):
            b_, l_, d_ = xn.shape
            C = 128
            nc = l_ // C
            qkv = xn @ Wqkv + bqkv
            q, k, v = jnp.split(qkv, 3, axis=-1)
            q = q.reshape(b_, l_, H, E)
            k = k.reshape(b_, l_, H, E)
            v = v.reshape(b_, l_, H, E)
            q = jax.nn.elu(q * np.float32(E ** (-0.5))) + np.float32(1.0001)
            k = jax.nn.elu(k) + np.float32(1.0001)

            def chunks(t):
                return t.reshape(b_, nc, C, H, E).transpose(1, 0, 3, 2, 4)
            qc, kc, vc = (chunks(q), chunks(k), chunks(v))
            tril = jnp.tril(jnp.ones((C, C), jnp.float32))

            def step(carry, inp):
                S, z = carry
                qi, ki, vi = inp
                A = jnp.einsum('bhce,bhde->bhcd', qi, ki) * tril
                num = jnp.einsum('bhce,bhef->bhcf', qi, S) + jnp.einsum('bhcd,bhdf->bhcf', A, vi)
                den = jnp.einsum('bhce,bhe->bhc', qi, z) + A.sum(-1)
                o = num / (den[..., None] + 1e-06)
                S = S + jnp.einsum('bhce,bhcf->bhef', ki, vi)
                z = z + ki.sum(2)
                return ((S, z), o)
            S0 = jnp.zeros((b_, H, E, E), jnp.float32)
            z0 = jnp.zeros((b_, H, E), jnp.float32)
            _, out = jax.lax.scan(step, (S0, z0), (qc, kc, vc))
            out = out.transpose(1, 0, 3, 2, 4).reshape(b_, l_, d_)
            return out @ Wo + bo
        xn = _ln(x, g1, b1)
        attn_out = _swa(xn, Wqkv_a, bqkv_a, Wp_a, bp_a)
        ssm_out = _linattn(xn, Wqkv_s, bqkv_s, Wo_s, bo_s)
        mixed = (attn_out + ssm_out) @ Wo + bo
        x1 = x + mixed
        h = _ln(x1, gm, bm)
        mlp = jax.nn.gelu(h @ W1 + b1m, approximate=False) @ W2 + b2m
        return x1 + mlp

    def _L0_ffn_ref(x, router_w, router_b, w1, b1, w2, b2):
        import jax, jax.numpy as jnp
        import numpy as np
        HIDDEN = 128
        NUM_EXPERTS = 8
        TOP_K = 2
        BATCH, SEQ = (4, 512)
        logits = jnp.einsum('bsh,he->bse', x, router_w) + router_b
        probs = jax.nn.softmax(logits, axis=-1)
        topk_p, topk_i = jax.lax.top_k(probs, TOP_K)
        topk_p = topk_p / jnp.sum(topk_p, axis=-1, keepdims=True)
        out = jnp.zeros_like(x)
        for e in range(NUM_EXPERTS):
            w = jnp.sum(jnp.where(topk_i == e, topk_p, 0.0), axis=-1)
            h = jax.nn.relu(jnp.einsum('bsh,hf->bsf', x, w1[e]) + b1[e])
            y = jnp.einsum('bsf,fh->bsh', h, w2[e]) + b2[e]
            out = out + w[..., None] * y
        return out

    def _L1_attn_ref(x, Wg_w, Wg_b, Wr_w, Wr_b, Wk_w, Wk_b, Wv_w, Wv_b, Wo_w, Wo_b, mg, mr, mk, mv, w, u):
        import jax, jax.numpy as jnp
        import numpy as np
        B, N, D, H = (8, 512, 128, 16)
        HD = D // H
        EPS = 1e-05
        b, n, d = x.shape
        x_shift = jnp.roll(x, shift=1, axis=1)

        def mix(m, W, bias):
            return (m * x + (1.0 - m) * x_shift) @ W.T + bias
        g = mix(mg, Wg_w, Wg_b).reshape(b, n, H, HD)
        r = mix(mr, Wr_w, Wr_b).reshape(b, n, H, HD)
        k = mix(mk, Wk_w, Wk_b).reshape(b, n, H, HD)
        v = mix(mv, Wv_w, Wv_b).reshape(b, n, H, HD)
        kv = k * v
        decay = jnp.exp(-jnp.exp(w))
        kv_t = jnp.swapaxes(kv, 0, 1)

        def step(acc, kvt):
            acc = decay * acc + kvt
            return (acc, acc)
        _, accs = jax.lax.scan(step, jnp.zeros((b, H, HD), x.dtype), kv_t)
        wkv = jnp.swapaxes(accs, 0, 1) + u * kv
        rw = r * wkv
        mean = jnp.mean(rw, axis=-1, keepdims=True)
        var = jnp.var(rw, axis=-1, keepdims=True)
        ln = (rw - mean) * jax.lax.rsqrt(var + EPS)
        out = (jax.nn.sigmoid(g) * ln).reshape(b, n, d)
        return out @ Wo_w.T + Wo_b

    def _L1_ffn_ref(x, router_w, w1, w2):
        import jax, jax.numpy as jnp
        import numpy as np
        B, S, D, H, E = (2, 256, 128, 512, 8)
        b, s, d = x.shape
        e = router_w.shape[0]
        xf = x.reshape(-1, d)
        probs = jax.nn.softmax(xf @ router_w.T, axis=-1)
        topv, topi = jax.lax.top_k(probs, 2)
        topv = topv / (topv.sum(axis=-1, keepdims=True) + 1e-09)
        cw = (jax.nn.one_hot(topi, e, dtype=xf.dtype) * topv[..., None]).sum(axis=1)
        h = jax.nn.gelu(jnp.einsum('td,edh->teh', xf, w1), approximate=False)
        y = jnp.einsum('teh,ehd->ted', h, w2)
        out = jnp.einsum('te,ted->td', cw, y)
        return out.reshape(b, s, d)
    x = L0_attn_x
    xn = _layernorm(x, axis=-1)
    x = x + _L0_attn_ref(xn, L0_attn_g1, L0_attn_b1, L0_attn_Wqkv_a, L0_attn_bqkv_a, L0_attn_Wp_a, L0_attn_bp_a, L0_attn_Wqkv_s, L0_attn_bqkv_s, L0_attn_Wo_s, L0_attn_bo_s, L0_attn_Wo, L0_attn_bo, L0_attn_gm, L0_attn_bm, L0_attn_W1, L0_attn_b1m, L0_attn_W2, L0_attn_b2m) + _L0_ffn_ref(xn, L0_ffn_router_w, L0_ffn_router_b, L0_ffn_w1, L0_ffn_b1, L0_ffn_w2, L0_ffn_b2)
    xn = _layernorm(x, axis=-1)
    x = x + _L1_attn_ref(xn, L1_attn_Wg_w, L1_attn_Wg_b, L1_attn_Wr_w, L1_attn_Wr_b, L1_attn_Wk_w, L1_attn_Wk_b, L1_attn_Wv_w, L1_attn_Wv_b, L1_attn_Wo_w, L1_attn_Wo_b, L1_attn_mg, L1_attn_mr, L1_attn_mk, L1_attn_mv, L1_attn_w, L1_attn_u) + _L1_ffn_ref(xn, L1_ffn_router_w, L1_ffn_w1, L1_ffn_w2)
    return x

_drawn_inputs = setup_inputs


def setup_inputs(seed=0):
    import zlib

    import numpy as np

    out = dict(_drawn_inputs(seed))
    spreads = {'L0_attn_g1': (1.0, 0.6),
     'L0_attn_b1': (0.0, 0.8),
     'L0_attn_bqkv_a': (0.0, 0.8),
     'L0_attn_bp_a': (0.0, 0.536),
     'L0_attn_bqkv_s': (0.0, 0.8),
     'L0_attn_bo_s': (0.0, 0.557),
     'L0_attn_bo': (0.0, 0.1),
     'L0_attn_gm': (1.0, 0.6),
     'L0_attn_bm': (0.0, 2.0),
     'L0_attn_b1m': (0.0, 0.552),
     'L0_attn_b2m': (0.0, 0.1),
     'L0_ffn_router_b': (0.0, 0.313),
     'L0_ffn_b1': (0.0, 0.8),
     'L0_ffn_b2': (0.0, 0.1),
     'L1_attn_Wg_b': (0.0, 0.761),
     'L1_attn_Wr_b': (0.0, 0.1),
     'L1_attn_Wk_b': (0.0, 0.1),
     'L1_attn_Wv_b': (0.0, 0.1),
     'L1_attn_Wo_b': (0.0, 0.1)}
    factors = {'L0_attn_Wqkv_a': 8.0,
     'L0_attn_Wp_a': 8.0,
     'L0_attn_Wqkv_s': 8.0,
     'L0_attn_Wo_s': 8.0,
     'L0_ffn_w1': 3.152,
     'L1_ffn_router_w': 3.538,
     'L1_ffn_w1': 3.142,
     'L1_ffn_w2': 3.11}
    for name, (base, spread) in spreads.items():
        noise = np.random.default_rng([zlib.crc32(name.encode()), seed]).standard_normal(out[name].shape)
        drawn = base * np.exp(spread * noise) if base else spread * noise
        out[name] = jnp.asarray(drawn.astype(out[name].dtype))
    for name, factor in factors.items():
        out[name] = (out[name] * factor).astype(out[name].dtype)
    return out
```

```python
from contextlib import ExitStack

import concourse.bass as bass
from concourse import mybir

ALU = mybir.AluOpType
ACT = mybir.ActivationFunctionType
F32 = mybir.dt.float32
BF16 = mybir.dt.bfloat16
U32 = mybir.dt.uint32
AX_X = mybir.AxisListType.X

P = 128
GT = 4
GC = GT * P
EPS = 1e-5
MASKED = -1e30
ARENA = 17800


def build(nc, I, out):
    B, L, D = I["L0_attn_x"].shape
    H = I["L1_attn_w"].shape[0]
    E = D // H
    TILES = B * L // P
    NG = TILES // GT
    EX = I["L0_ffn_w1"].shape[0]
    F0 = I["L0_ffn_w1"].shape[2]
    F1 = I["L1_ffn_w1"].shape[2]
    FM = I["L0_attn_W1"].shape[1]
    C0, C1, CM = F0 // P, F1 // P, FM // P
    assert D == P and L == 2 * GC and EX == 8 and H == 16 and E == 8
    QK = 6 * E
    QKM = QK + 3
    LR = 64
    RSQ = float(E) ** -0.5

    x_d = I["L0_attn_x"].rearrange("b (g j p) d -> (b g) p j d", j=GT, p=P)
    out_d = out.rearrange("b (g j p) d -> (b g) p j d", j=GT, p=P)
    xnT_d = nc.dram_tensor("xnT_d", [NG, P, GC], F32, kind="Internal").ap()
    hT_d = nc.dram_tensor("hT_d", [NG, P, GC], F32, kind="Internal").ap()
    yT_d = nc.dram_tensor("yT_d", [NG, P, GC], F32, kind="Internal").ap()
    part_d = [[nc.dram_tensor(f"part_d{i}{j}", [3, P, GC], BF16, kind="Internal").ap() for j in range(4)] for i in range(2)]

    with ExitStack() as ctx:
        def sb(name, shape, dt=F32):
            return ctx.enter_context(nc.sbuf_tensor(name, shape, dt))

        def sem(name):
            return ctx.enter_context(nc.semaphore(name))

        X = sb("X", [P, TILES, D])
        cw0 = sb("cw0", [P, TILES, EX + 1])
        cw1 = sb("cw1", [P, TILES, EX])
        ident = sb("ident", [P, P])
        identb = sb("identb", [P, P], BF16)
        ones_row = sb("ones_row", [1, P])
        half = sb("half", [P, GT])
        iot = sb("iot", [P, EX])
        iou = sb("iou", [P, EX], U32)

        wfm = sb("wfm", [P, 4, D])
        wtm = sb("wtm", [P, 3, D])
        btm = sb("btm", [P, 3, D])
        bfm = sb("bfm", [P, 4])
        gb = sb("gb", [P, 4])
        wsqT = sb("wsqT", [P, 8, D])
        wmix = sb("wmix", [P, 2, D])
        bcol = sb("bcol", [P, 3])
        bc_row = sb("bc_row", [1, D])
        wob_row = sb("wob_row", [1, D])
        rw0 = sb("rw0", [P, EX])
        rb = sb("rb", [P, 2, EX])
        rw1r = sb("rw1r", [EX, D])
        rw1 = sb("rw1", [P, EX])
        W1 = sb("W1", [P, CM, P])
        W2 = sb("W2", [P, CM, D])
        b1m = sb("b1m", [P, CM])
        b2x = sb("b2x", [EX + 1, D])
        fb1 = sb("fb1", [P, EX, C0])
        l1b = sb("l1b", [P, 4])
        l1m = sb("l1m", [P, 4])
        l1w = sb("l1w", [P, 4])

        mkey = sb("mkey", [P, 2, 2, P], BF16)
        mqry = sb("mqry", [P, 2, 2, P], BF16)
        tri = sb("tri", [P, P])
        bd = sb("bd", [P, H])
        cen = sb("cen", [P, P])
        avg = sb("avg", [P, P])

        big = [sb(f"big{i}", [P, H * GC // 2]) for i in range(4)]
        QS, KS = ([b_[:, :].bitcast(BF16).rearrange("p (h t) -> p h t", h=H) for b_ in big[2 * i:2 * i + 2]] for i in range(2))
        KT = sb("KT", [QKM, H, P], BF16)
        VA = [sb(f"VA{i}", [P, GT, H, E + 1]) for i in range(2)]
        VL = [sb(f"VL{i}", [P, GT, H, E + 1]) for i in range(2)]
        VT = sb("VT", [P, H, E + 1])
        SB = sb("SB", [P, H, 32])
        st6 = sb("st6", [P, GT, 6])
        mv = sb("mv", [P, GT, 2])
        rstd = sb("rstd", [P, GT])[:, :]
        lg = sb("lg", [P, GT, EX])[:, :, :]
        mx4 = sb("mx4", [P, GT])[:, :]
        t8 = sb("t8", [P, GT, EX])
        i8 = sb("i8", [P, GT, EX], U32)
        idf = sb("idf", [P, GT, 2])[:, :, :]
        oh = sb("oh", [P, 2, GT, EX])
        eps_col = sb("eps_col", [P, 1])
        arena = sb("arena", [P, ARENA])
        used = [0]

        def carve(*shape, dt=F32):
            n = 1
            for d in shape:
                n *= d
            w = n if dt == F32 else (n + 1) // 2
            a = arena[:, used[0]:used[0] + w]
            used[0] += w
            assert used[0] <= ARENA, used[0]
            if dt != F32:
                a = a.bitcast(dt)
            if len(shape) == 2:
                a = a.rearrange("p (a b) -> p a b", a=shape[0])
            if len(shape) == 3:
                a = a.rearrange("p (a b c) -> p a b c", a=shape[0], b=shape[1])
            return a

        wraw = [carve(3 * D) for _ in range(2)]
        braw = [carve(3 * D) for _ in range(2)]
        wsq = carve(8, D)
        idv = carve(P)
        btmp = carve(4, D)
        bo_row = carve(D)

        used[0] = 0
        XIN = [carve(GT, P) for _ in range(2)]
        XN = [carve(GT, P) for _ in range(2)]
        XH = carve(GT, P)
        X1 = carve(GT, P)
        HN = X1
        xnT = carve(GC)
        xhT = carve(GC)
        hT = carve(GC)
        parts = carve(2, 3, GC, dt=BF16)
        res = carve(2, GC)
        Y32 = carve(2, GC)
        QF = [carve(GC) for _ in range(2)]
        kraw = carve(GT, P)
        eb = carve(2, GC)
        kexp = eb[:, 0, :].rearrange("p (j f) -> p j f", j=GT)
        KST = [carve(GT, P) for _ in range(2)]
        PB = [carve(4, 2, P) for _ in range(2)]
        AB = [carve(8, P) for _ in range(2)]
        OAs = xhT.rearrange("p (j f) -> p j f", j=GT)
        OLs = carve(GT, P)
        ATM = carve(2, P)
        AST = carve(2, P)
        rec = carve(2, H)
        SU = carve(H, E + 1)
        mmax = carve(GT, H)
        mres = carve(GT, H)
        MS = carve(GT, 3 * H, dt=BF16)
        MT = carve(GC, dt=BF16)

        used[0] = 0
        YN = [carve(GT, P) for _ in range(2)]
        xT = carve(L + 4)
        DF = carve(2, GC)
        MX = carve(4, GC)
        SG = carve(GC)
        KK = carve(GC)
        KV = carve(GC)
        ACC = carve(2, GC)
        WK = carve(GC)
        RW = carve(GC)
        SQ = carve(GC)
        CS = carve(GC)
        RS = carve(GC)
        OT = carve(GC)
        fx = [[carve(GC) for _ in range(2)] for _ in range(2)]
        cwg = carve(GT, EX + 1)
        cwT = carve(GC)
        assert used[0] <= ARENA, used

        ring = [ctx.enter_context(nc.psum_tensor(f"ring{i}", [P, 2, GC], F32)) for i in range(2)]
        psA = ctx.enter_context(nc.psum_tensor("psA", [P, GT, P], F32))
        psL = ctx.enter_context(nc.psum_tensor("psL", [P, GT, P], F32))
        psT = ctx.enter_context(nc.psum_tensor("psT", [P, GT, P], F32))
        psY = ctx.enter_context(nc.psum_tensor("psY", [P, GC], F32))

        SETUP = 5
        N_CONSTS = 33

        START = 64
        counters = []

        def counter(name):
            counters.append(sem(name))
            return counters[-1]

        class S:
            amask = counter("amask")
            ast = counter("ast")
            at = counter("at")
            cen = counter("cen")
            cs = counter("cs")
            cwT = counter("cwT")
            cwT_turn = counter("cwT_turn")
            cwg = counter("cwg")
            diff = counter("diff")
            exps = counter("exps")
            grkv = counter("grkv")
            hT = counter("hT")
            hT_turn = counter("hT_turn")
            high = counter("high")
            kexp = counter("kexp")
            kk = counter("kk")
            kmax = counter("kmax")
            kmin = counter("kmin")
            kst = counter("kst")
            kv = counter("kv")
            lin_exp = counter("lin_exp")
            lin_min = counter("lin_min")
            lin_qk = counter("lin_qk")
            lin_res = counter("lin_res")
            lin_sum = counter("lin_sum")
            lin_y = counter("lin_y")
            lnc = counter("lnc")
            lnc_rstd = counter("lnc_rstd")
            lne = counter("lne")
            lne_rstd = counter("lne_rstd")
            lnp = counter("lnp")
            lnp_rstd = counter("lnp_rstd")
            lnv = counter("lnv")
            logit_turn = counter("logit_turn")
            logits = counter("logits")
            logits1 = counter("logits1")
            low = counter("low")
            lt = counter("lt")
            mT = counter("mT")
            mT_turn = counter("mT_turn")
            mid = counter("mid")
            mix = counter("mix")
            mixed = counter("mixed")
            mo = counter("mo")
            mparts = counter("mparts")
            mred = counter("mred")
            oas = counter("oas")
            ol = counter("ol")
            ols = counter("ols")
            ot = counter("ot")
            pv = counter("pv")
            rcp = counter("rcp")
            resid = counter("resid")
            rs = counter("rs")
            rt0 = counter("rt0")
            rt0_exp = counter("rt0_exp")
            rt1 = counter("rt1")
            rt1_exp = counter("rt1_exp")
            rw = counter("rw")
            sb = counter("sb")
            scan = counter("scan")
            sg = counter("sg")
            sq = counter("sq")
            state = counter("state")
            su = counter("su")
            t1 = counter("t1")
            t2 = counter("t2")
            tails = counter("tails")
            tailv = counter("tailv")
            tm = counter("tm")
            turn_attend = counter("turn_attend")
            turn_max = counter("turn_max")
            turn_prep = counter("turn_prep")
            var = counter("var")
            wkv = counter("wkv")
            x1 = counter("x1")
            xT = counter("xT")
            xT0 = counter("xT0")
            xT_turn = counter("xT_turn")
            xhT = counter("xhT")
            xnT = counter("xnT")
            xo = counter("xo")
            xsum = counter("xsum")
            y = counter("y")
            yT_out = counter("yT_out")
            facc = [counter("facc0"), counter("facc1")]
            fact = [counter("fact0"), counter("fact1")]
            fdown = [counter("fdown0"), counter("fdown1")]
            fup = [counter("fup0"), counter("fup1")]
            hT_out = [counter("hT_out0"), counter("hT_out1")]
            mrow = [counter("mrow0"), counter("mrow1")]
            sent = [counter("sent0"), counter("sent1")]
            xin = [counter("xin0"), counter("xin1")]
            xnT_out = [counter("xnT_out0"), counter("xnT_out1")]
            fx = [[counter("fx00"), counter("fx01")], [counter("fx10"), counter("fx11")]]
            stack = [[counter("stack00"), counter("stack01")], [counter("stack10"), counter("stack11")]]
            loaded = sem("loaded")
            consts = sem("consts")
            wT = sem("wT")
            wTc = sem("wTc")
            bperm = sem("bperm")
            bsum = sem("bsum")
            wmixed = sem("wmixed")
            actset = sem("actset")
            dveset = sem("dveset")
            setup = sem("setup")
            out = sem("out")
            waits_alone = sem("waits_alone")
            ffnw = [sem("ffnw0"), sem("ffnw1")]

        def h_e(ap):
            return ap.rearrange("p (h e) -> p h e", e=E)

        N2 = NG // 2

        def attention_order(eng, stages):
            norm, prep, mx, attend = stages
            norm(0, 0)
            prep(0, 0)
            with eng.Fori(0, N2 - 1) as b:
                for par in range(2):
                    norm(b + par, 1 - par)
                    mx(b, par)
                    prep(b + par, 1 - par)
                    attend(b, par, False)
            norm(N2 - 1, 1)
            mx(N2 - 1, 0)
            prep(N2 - 1, 1)
            attend(N2 - 1, 0, False)
            mx(N2 - 1, 1)
            attend(N2 - 1, 1, True)

        w_up = [big[0][:, 0:EX * F0].rearrange("p (e f) -> p e f", e=EX), big[2][:, :].rearrange("p (e f) -> p e f", e=EX)]
        w_dn = [big[0][:, EX * F0:2 * EX * F0].rearrange("p (e c d) -> p e c d", e=EX, c=C0),
                big[3][:, :].rearrange("p (e c d) -> p e c d", e=EX, c=C1)]
        HS = [big[1][:, i * 4 * GC:(i + 1) * 4 * GC].rearrange("p (c t) -> p c t", c=4) for i in range(2)]
        psO = [psA, psL]
        UNITS = [[("mlp", CM)] + [(e, C0) for e in range(EX)], [(e, C1) for e in range(EX)]]
        TURNS_F = [sum(c for _, c in u) // 2 for u in UNITS]

        def unit_turns(layer, n):
            first = sum(c for _, c in UNITS[layer][:n]) // 2
            return first, UNITS[layer][n][1] // 2

        def ffn_sp(sp, layer):
            dims = xnT_d if layer == 0 else yT_d
            if layer == 0:
                sp.wait_ge(S.amask, 8 * NG + START)
                sp.sem_inc(S.waits_alone, 1)
                sp.wait_ge(S.ol, GT * NG + START)
                sp.sem_inc(S.waits_alone, 1)
                for q in range(2):
                    sp.wait_ge(S.xnT_out[q], 16 * N2 + START)
                    sp.sem_inc(S.waits_alone, 1)
                    sp.wait_ge(S.hT_out[q], 16 * N2 + START)
                    sp.sem_inc(S.waits_alone, 1)
                sp.dma_start(w_up[0], I["L0_ffn_w1"].rearrange("e d f -> d e f")).then_inc(S.ffnw[0], 16)
                sp.dma_start(w_dn[0], I["L0_ffn_w2"].rearrange("e (c f) d -> f e c d", c=C0)).then_inc(S.ffnw[0], 16)
            else:
                sp.wait_ge(S.yT_out, 16 * NG + START)
                sp.sem_inc(S.waits_alone, 1)

            def load(g, par, used_units):
                sp.wait_ge(S.fdown[layer], used_units + START)
                sp.sem_inc(S.waits_alone, 1)
                sp.dma_start(fx[0][par], dims[g]).then_inc(S.fx[layer][par], 16)
                if layer == 0:
                    sp.dma_start(fx[1][par], hT_d[g]).then_inc(S.fx[layer][par], 16)

            def store(g):
                sp.wait_ge(S.facc[1], 32 * (g + 1) + START)
                sp.sem_inc(S.waits_alone, 1)
                sp.dma_start(out_d[g], X[:, bass.ds(g * GT, GT), :]).then_inc(S.out, 16)

            nu = len(UNITS[layer])
            load(0, 0, 0)
            with sp.Fori(0, N2 - 1) as b:
                load(2 * b + 1, 1, nu * 2 * b)
                load(2 * b + 2, 0, nu * (2 * b + 1))
                if layer == 1:
                    store(2 * b)
                    store(2 * b + 1)
            load(NG - 1, 1, nu * (NG - 2))
            if layer == 0:
                sp.dma_start(w_up[1], I["L1_ffn_w1"].rearrange("e d f -> d e f")).then_inc(S.ffnw[1], 16)
                sp.dma_start(w_dn[1], I["L1_ffn_w2"].rearrange("e (c f) d -> f e c d", c=C1)).then_inc(S.ffnw[1], 16)
            else:
                store(NG - 2)
                store(NG - 1)
                sp.wait_ge(S.out, 16 * NG)

        def ffn_pe(pe, layer):
            T = nc.tensor
            units, nt = UNITS[layer], TURNS_F[layer]
            nu = len(units)
            pe.wait_ge(S.ffnw[layer], 32)

            def up(g, b, par, n):
                e, chunks = units[n]
                first, turns = unit_turns(layer, n)
                for i in range(turns):
                    k = first + i
                    slot = (nt * par + k) % 2
                    pe.wait_ge(S.fact[layer], 2 * (nt * g + k - 1) + START)
                    for c in range(2):
                        w = W1[:, 2 * i + c, :] if e == "mlp" else w_up[layer][:, e, (2 * i + c) * P:(2 * i + c + 1) * P]
                        m = T.matmul(ring[slot][:, c, :], w, fx[1 if e == "mlp" else 0][par], start=True, stop=True)
                    m.then_inc(S.fup[layer], 1)

            def down(g, b, par, n):
                e, chunks = units[n]
                first, turns = unit_turns(layer, n)
                o = (nu * par + n)
                hs = HS[o % 2]
                pe.wait_ge(S.fact[layer], 2 * (nt * g + first + turns) + START)
                pe.wait_ge(S.facc[layer], facc_at(layer, g, n - 2) + START)
                for j in range(GT):
                    for c in range(chunks):
                        w = W2[:, c, :] if e == "mlp" else w_dn[layer][:, e, c, :]
                        last = c == chunks - 1 and e != "mlp"
                        m = T.matmul(psO[o % 2][:, j, :], hs[:, c, j * P:(j + 1) * P], w, start=(c == 0), stop=last)
                    if e == "mlp":
                        m = T.matmul(psO[o % 2][:, j, :], cwT[0:EX + 1, j * P:(j + 1) * P], b2x[:, :], start=False, stop=True)
                m.then_inc(S.fdown[layer], 1)

            with pe.Fori(0, N2) as b:
                for par in range(2):
                    g = 2 * b + par
                    pe.wait_ge(S.fx[layer][par], (32 if layer == 0 else 16) * (b + 1) + START)
                    if layer == 0:
                        pe.wait_ge(S.cwg, g + 1 + START)
                        for j in range(GT):
                            m = T.transpose(psT[0:EX + 1, j, :], cwg[:, j, :], ident[:, :])
                        m.then_inc(S.cwT_turn, 1)
                    for n in range(nu + 1):
                        if n < nu:
                            up(g, b, par, n)
                        if n == 1 and layer == 0:
                            pe.wait_ge(S.cwT, g + 1 + START)
                        if n > 0:
                            down(g, b, par, n - 1)

        def facc_at(layer, g, n):
            per = 33 if layer == 0 else 32
            if n < 0:
                return per * g
            n = max(n, 0)
            return per * g + (4 * n + 1 if layer == 0 else 4 * n + 4)

        def ffn_act(act, layer):
            V = nc.scalar
            units, nt = UNITS[layer], TURNS_F[layer]
            nu = len(units)
            func = ACT.Relu if layer == 0 else ACT.Gelu
            act.wait_ge(S.ffnw[layer], 32)
            with act.Fori(0, N2) as b:
                for par in range(2):
                    g = 2 * b + par
                    if layer == 0:
                        act.wait_ge(S.cwT_turn, g + 1 + START)
                        act.wait_ge(S.fdown[0], 9 * g + START)
                        V.activation(cwT[0:EX + 1, :], psT[0:EX + 1, :, :].rearrange("p a b -> p (a b)"), ACT.Copy).then_inc(S.cwT, 1)
                    for n, (e, chunks) in enumerate(units):
                        first, turns = unit_turns(layer, n)
                        hs = HS[(nu * par + n) % 2]
                        act.wait_ge(S.fdown[layer], nu * g + max(n - 1, 0) + START)
                        for i in range(turns):
                            k = first + i
                            slot = (nt * par + k) % 2
                            act.wait_ge(S.fup[layer], nt * g + k + 1 + START)
                            for c in range(2):
                                if layer == 0:
                                    bias = b1m[:, 2 * i + c:2 * i + c + 1] if e == "mlp" else fb1[:, e, 2 * i + c:2 * i + c + 1]
                                    f = ACT.Gelu if e == "mlp" else func
                                    V.activation(hs[:, 2 * i + c, :], ring[slot][:, c, :], f, bias=bias).then_inc(S.fact[0], 1)
                                else:
                                    V.activation(hs[:, 2 * i + c, :], ring[slot][:, c, :], func).then_inc(S.fact[1], 1)

        def ffn_dve(dve, layer):
            V = nc.vector
            units = UNITS[layer]
            nu = len(units)
            cw = (cw0, cw1)[layer]
            with dve.Fori(0, N2) as b:
                for par in range(2):
                    g = 2 * b + par
                    if layer == 0:
                        dve.wait_ge(S.cwT_turn, g + START)
                        V.tensor_copy(cwg, cw0[:, bass.ds(g * GT, GT), :]).then_inc(S.cwg, 1)
                    for n, (e, chunks) in enumerate(units):
                        o = psO[(nu * par + n) % 2]
                        dve.wait_ge(S.fdown[layer], nu * g + n + 1 + START)
                        dve.wait_ge(S.facc[layer], facc_at(layer, g, n - 1) + START)
                        if e == "mlp":
                            xg = X[:, bass.ds(g * GT, GT), :]
                            V.tensor_tensor(xg, o[:, :, :], xg, ALU.add).then_inc(S.facc[0], 1)
                            continue
                        for j in range(GT):
                            xt = X[:, bass.ds(g * GT + j, 1), :].rearrange("p a d -> p (a d)")
                            V.scalar_tensor_tensor(out=xt, in0=o[:, j, :], scalar=cw[:, bass.ds(g * GT + j, 1), e], in1=xt,
                                                   op0=ALU.mult, op1=ALU.add).then_inc(S.facc[layer], 1)

        psAf = psA[:, :, :].rearrange("p a b -> p (a b)")
        psLf = psL[:, :, :].rearrange("p a b -> p (a b)")
        psTf = psT[:, :, :].rearrange("p a b -> p (a b)")

        def mixer_sp(sp):
            with sp.Fori(0, B) as b:
                for q in range(2):
                    sp.wait_ge(S.xT, 2 * b + q + 1 + START)
                    sp.sem_inc(S.waits_alone, 1)
                    sp.wait_ge(S.yT_out, 16 * (2 * b + q) + START)
                    sp.sem_inc(S.waits_alone, 1)
                    sp.dma_start(yT_d[2 * b + q], xT[:, 1 + q * GC:1 + (q + 1) * GC]).then_inc(S.yT_out, 16)

        def mixer_pool(pool):
            V = nc.gpsimd
            with pool.Fori(0, B) as b:
                for q in range(2):
                    n = 2 * b + q
                    pool.wait_ge(S.lnc, 12 * n + 8 + START)
                    pool.sem_inc(S.waits_alone, 1)
                    V.tensor_scalar(rstd, mv[:, :, 1], EPS, 1.0, ALU.add, ALU.mult).then_inc(S.lnc_rstd, 1)
                    pool.wait_ge(S.lnc_rstd, 2 * n + 1 + START)
                    pool.sem_inc(S.waits_alone, 1)
                    V.tensor_tensor(rstd, rstd, half[:, :], ALU.pow).then_inc(S.lnc_rstd, 1)
                pool.wait_ge(S.xT, 2 * b + 2 + START)
                pool.sem_inc(S.waits_alone, 1)
                pool.wait_ge(S.xT0, b + 1 + START)
                pool.sem_inc(S.waits_alone, 1)
                pool.wait_ge(S.mixed, 8 * b + START)
                pool.sem_inc(S.waits_alone, 1)
                for q in range(2):
                    V.tensor_tensor(DF[:, q, :], xT[:, 1 + q * GC:1 + (q + 1) * GC], xT[:, q * GC:(q + 1) * GC], ALU.subtract)\
                        .then_inc(S.diff, 1)
                for q in range(2):
                    n = 2 * b + q
                    pool.wait_ge(S.cs, n + 1 + START)
                    pool.sem_inc(S.waits_alone, 1)
                    pool.wait_ge(S.rs, n + 1 + START)
                    pool.sem_inc(S.waits_alone, 1)
                    pool.wait_ge(S.mo, n + START)
                    pool.sem_inc(S.waits_alone, 1)
                    V.tensor_tensor(OT, CS, RS, ALU.mult).then_inc(S.ot, 1)

        def mixer_act(act):
            V = nc.scalar
            with act.Fori(0, B) as b:
                for q in range(2):
                    n = 2 * b + q
                    act.wait_ge(S.xT_turn, n + 1 + START)
                    act.wait_ge(S.yT_out, 16 * n + START)
                    act.wait_ge(S.mixed, 8 * b + START)
                    V.activation(xT[:, 1 + q * GC:1 + (q + 1) * GC], psTf, ACT.Copy).then_inc(S.xT, 1)
                act.wait_ge(S.xT, 2 * b + 2 + START)
                V.activation(xT[:, 0:1], xT[:, L:L + 1], ACT.Copy).then_inc(S.xT0, 1)
                for q in range(2):
                    n = 2 * b + q
                    act.wait_ge(S.rt1, 22 * n + 2 + START)
                    V.activation(lg, lg, ACT.Exp).then_inc(S.rt1_exp, 1)
                for q in range(2):
                    n = 2 * b + q
                    act.wait_ge(S.grkv, 2 * n + 2 + START)
                    act.wait_ge(S.cs, n + START)
                    V.activation(SG, ring[0][:, 0, :], ACT.Sigmoid, bias=l1b[:, 0:1]).then_inc(S.sg, 1)
                    act.wait_ge(S.kv, n + START)
                    V.activation(KK, ring[1][:, 0, :], ACT.Identity, bias=l1b[:, 2:3]).then_inc(S.kk, 1)
                    act.wait_ge(S.cen, n + 1 + START)
                    V.activation(SQ, psAf, ACT.Square).then_inc(S.sq, 1)
                    act.wait_ge(S.var, n + 1 + START)
                    act.wait_ge(S.ot, n + START)
                    V.activation(RS, psLf, ACT.Ln, bias=eps_col[:, 0:1]).then_inc(S.lnv, 1)
                    act.wait_ge(S.lnv, n + 1 + START)
                    V.activation(RS, RS, ACT.Exp, scale=-0.5).then_inc(S.rs, 1)

        def mixer_dve(dve):
            V = nc.vector
            with dve.Fori(0, B) as b:
                dve.wait_ge(S.facc[0], 33 * NG + START)
                for q in range(2):
                    n = 2 * b + q

                    def src(j, n=n):
                        return X[:, bass.ds(n * GT + j, 1), :].rearrange("p a d -> p (a d)")

                    layernorm(dve, S.lnc, S.lnc_rstd, n, src, lambda j: YN[q][:, j, :], S.xT_turn, 2 * b + START)
                for q in range(2):
                    n = 2 * b + q
                    dve.wait_ge(S.logit_turn, n + 1 + START)
                    route_start(dve, S.rt1, S.logits1, n, psY[:, 0:GT * EX].rearrange("p (a b) -> p a b", a=GT), 1)
                    route_end(dve, S.rt1, S.rt1_exp, n, 1, cw1)
                dve.wait_ge(S.diff, 2 * b + 2 + START)
                for q in range(2):
                    n = 2 * b + q
                    dve.wait_ge(S.grkv, 2 * n + START)
                    for i in range(4):
                        V.scalar_tensor_tensor(out=MX[:, i, :], in0=DF[:, q, :], scalar=l1m[:, i:i + 1], in1=xT[:, q * GC:(q + 1) * GC],
                                               op0=ALU.mult, op1=ALU.add).then_inc(S.mixed, 1)
                    dve.wait_ge(S.kk, n + 1 + START)
                    V.scalar_tensor_tensor(out=KV, in0=ring[1][:, 1, :], scalar=l1b[:, 3:4], in1=KK, op0=ALU.add, op1=ALU.mult)\
                        .then_inc(S.kv, 1)
                    dve.wait_ge(S.kv, n + 1 + START)
                    if q == 1:
                        dve.wait_ge(S.scan, n + START)
                    V.tensor_tensor_scan(ACC[:, q, :], l1w[:, 3:4].to_broadcast([P, GC]), KV, 0.0 if q == 0 else ACC[:, 0, GC - 1:GC],
                                         ALU.mult, ALU.add).then_inc(S.scan, 1)
                    dve.wait_ge(S.scan, n + 1 + START)
                    V.scalar_tensor_tensor(out=WK, in0=KV, scalar=l1w[:, 1:2], in1=ACC[:, q, :], op0=ALU.mult, op1=ALU.add)\
                        .then_inc(S.wkv, 1)
                    dve.wait_ge(S.wkv, n + 1 + START)
                    V.scalar_tensor_tensor(out=RW, in0=ring[0][:, 1, :], scalar=l1b[:, 1:2], in1=WK, op0=ALU.add, op1=ALU.mult)\
                        .then_inc(S.rw, 1)
                    dve.wait_ge(S.sq, n + 1 + START)
                    dve.wait_ge(S.sg, n + 1 + START)
                    dve.wait_ge(S.ot, n + START)
                    V.tensor_tensor(CS, psAf, SG, ALU.mult).then_inc(S.cs, 1)
                    dve.wait_ge(S.mo, n + 1 + START)
                    xg = X[:, bass.ds(n * GT, GT), :]
                    V.tensor_tensor(xg, psT[:, :, :], xg, ALU.add).then_inc(S.xo, 1)

        def mixer_pe(pe):
            T = nc.tensor
            with pe.Fori(0, B) as b:
                for q in range(2):
                    n = 2 * b + q
                    pe.wait_ge(S.lnc, 12 * n + 12 + START)
                    pe.wait_ge(S.xT, n + START)
                    pe.wait_ge(S.xo, 2 * b + START)
                    if q == 0:
                        pe.wait_ge(S.cwT, NG + START)
                    for j in range(GT):
                        m = T.transpose(psT[:, j, :], YN[q][:, j, :], ident[:, :])
                    m.then_inc(S.xT_turn, 1)
                for q in range(2):
                    n = 2 * b + q
                    pe.wait_ge(S.xT, 2 * b + q + 1 + START)
                    pe.wait_ge(S.logits1, n + START)
                    for j in range(GT):
                        c = 1 + q * GC + j * P
                        m = T.matmul(psY[:, j * EX:(j + 1) * EX], xT[:, c:c + P], rw1[:, :], start=True, stop=True)
                    m.then_inc(S.logit_turn, 1)
                for q in range(2):
                    n = 2 * b + q
                    pe.wait_ge(S.mixed, 4 * n + 4 + START)
                    pe.wait_ge(S.sg, n + START)
                    pe.wait_ge(S.kv, n + START)
                    pe.wait_ge(S.rw, n + START)
                    pe.wait_ge(S.facc[0], 33 * NG + START)
                    for i in range(2):
                        for k in range(2):
                            m = T.matmul(ring[i][:, k, :], wsqT[:, 3 + 2 * i + k, :], MX[:, 2 * i + k, :], start=True, stop=True)
                        m.then_inc(S.grkv, 1)
                    pe.wait_ge(S.rw, n + 1 + START)
                    pe.wait_ge(S.cs, n + START)
                    pe.wait_ge(S.sq, n + START)
                    T.matmul(psAf, cen[:, :], RW, start=True, stop=True).then_inc(S.cen, 1)
                    pe.wait_ge(S.sq, n + 1 + START)
                    pe.wait_ge(S.lnv, n + START)
                    T.matmul(psLf, avg[:, :], SQ, start=True, stop=True).then_inc(S.var, 1)
                    pe.wait_ge(S.ot, n + 1 + START)
                    pe.wait_ge(S.xo, n + START)
                    pe.wait_ge(S.xT, 2 * b + 2 + START)
                    for j in range(GT):
                        T.matmul(psT[:, j, :], OT[:, j * P:(j + 1) * P], wsqT[:, 7, :], start=True, stop=False)
                        m = T.matmul(psT[:, j, :], ones_row[:, :], wob_row[:, :], start=False, stop=True)
                    m.then_inc(S.mo, 1)

        def sp_rest(sp):
            ffn_sp(sp, 0)
            mixer_sp(sp)
            ffn_sp(sp, 1)

        def pool_rest(pool):
            mixer_pool(pool)

        def act_rest(act):
            ffn_act(act, 0)
            mixer_act(act)
            ffn_act(act, 1)

        def dve_rest(dve):
            ffn_dve(dve, 0)
            mixer_dve(dve)
            ffn_dve(dve, 1)

        def pe_rest(pe):
            ffn_pe(pe, 0)
            mixer_pe(pe)
            ffn_pe(pe, 1)

        def nothing(*a):
            pass

        block = ctx.enter_context(nc.Block())
        n_load = [0]

        @block.sync
        def _(sp):
            def load(dst, src, scattered=False):
                sp.dma_start(dst, src, allow_slow_non_contiguous=scattered).then_inc(S.loaded, 16)
                n_load[0] += 16

            bq = [I["L0_attn_bqkv_a"], I["L0_attn_bqkv_s"]]
            for a, w in enumerate(("L0_attn_Wqkv_a", "L0_attn_Wqkv_s")):
                load(wraw[a], I[w])
                load(braw[a], bq[a].partition_broadcast(P))
            for i, w in enumerate(("L0_attn_Wp_a", "L0_attn_Wo_s", "L0_attn_Wo", "L1_attn_Wg_w", "L1_attn_Wr_w", "L1_attn_Wk_w",
                                   "L1_attn_Wv_w", "L1_attn_Wo_w")):
                load(wsq[:, i, :], I[w])

            def col(dst, name):
                load(dst, I[name].rearrange("(p o) -> p o", o=1))

            for i, w in enumerate(("L0_attn_g1", "L0_attn_b1", "L0_attn_gm", "L0_attn_bm")):
                col(gb[:, i:i + 1], w)
            col(bcol[:, 0:1], "L0_attn_bp_a")
            col(bcol[:, 1:2], "L0_attn_bo_s")
            for i, w in enumerate("grkv"):
                col(l1b[:, i:i + 1], f"L1_attn_W{w}_b")
                col(l1m[:, i:i + 1], f"L1_attn_m{w}")
            load(l1w[:, 0:1], I["L1_attn_w"].rearrange("h (e o) -> (h e) o", o=1))
            load(l1w[:, 1:2], I["L1_attn_u"].rearrange("h (e o) -> (h e) o", o=1))
            load(bo_row[0:1, :], I["L0_attn_bo"].rearrange("(o n) -> o n", o=1))
            load(wob_row[:, :], I["L1_attn_Wo_b"].rearrange("(o n) -> o n", o=1))
            load(rw0[:, :], I["L0_ffn_router_w"])
            load(rb[:, 0, :], I["L0_ffn_router_b"].partition_broadcast(P))
            load(rw1r[:, :], I["L1_ffn_router_w"])
            load(W1[:, :, :], I["L0_attn_W1"].rearrange("d (c f) -> d c f", c=CM))
            load(W2[:, :, :], I["L0_attn_W2"].rearrange("(c f) d -> f c d", c=CM))
            load(b1m[:, :], I["L0_attn_b1m"].rearrange("(c f) -> f c", c=CM), scattered=True)
            load(b2x[0:EX, :], I["L0_ffn_b2"])
            load(b2x[EX:EX + 1, :], I["L0_attn_b2m"].rearrange("(o n) -> o n", o=1))
            load(fb1[:, :, :], I["L0_ffn_b1"].rearrange("e (c f) -> f e c", c=C0), scattered=True)
            for c in counters:
                sp.sem_inc(c, START)
            sp.sem_inc(S.setup, 1)
            sp.wait_ge(S.setup, SETUP)

            def norm(h, par):
                g = 2 * h + par
                sp.wait_ge(S.xsum, g - 1 + START)
                sp.sem_inc(S.waits_alone, 1)
                sp.dma_start(XIN[par], x_d[g]).then_inc(S.xin[par], 16)

            def send_parts(h, par, pair):
                g = 2 * h + par
                sp.wait_ge(S.low, 2 * g + pair + 1 + START)
                sp.sem_inc(S.waits_alone, 1)
                for i in range(2):
                    sp.wait_ge(S.stack[pair][par], 144 * h + START)
                    sp.sem_inc(S.waits_alone, 1)
                    sp.dma_start(part_d[par][2 * pair + i].rearrange("c p t -> p c t"), parts[:, i]).then_inc(S.sent[pair], 16)
                sp.wait_ge(S.sent[pair], 32 * (g + 1) + START)
                sp.sem_inc(S.waits_alone, 1)
                sp.wait_ge(S.amask, 8 * (g - 1) + START)
                sp.sem_inc(S.waits_alone, 1)
                sp.wait_ge(S.tails, 16 * h + START)
                sp.sem_inc(S.waits_alone, 1)
                r0 = LR if pair else 0
                q_d, k_d = part_d[par][2 * pair], part_d[par][2 * pair + 1]
                row = 0
                for n in (3, 2, 1):
                    sp.dma_start(QS[par][r0 + row:r0 + row + E * n, :, :],
                                 q_d[0:n].rearrange("c (e h) t -> (c e) h t", h=H)).then_inc(S.stack[pair][par], 16)
                    for i in range(n):
                        sp.dma_start(KS[par][r0 + row + E * i:r0 + row + E * i + E, :, :],
                                     k_d[3 - n].rearrange("(e h) t -> e h t", h=H)).then_inc(S.stack[pair][par], 16)
                    row += E * n

            def prep(h, par):
                g = 2 * h + par
                sp.wait_ge(S.xnT, g + 1 + START)
                sp.sem_inc(S.waits_alone, 1)
                sp.dma_start(xnT_d[g], xnT).then_inc(S.xnT_out[par], 16)
                send_parts(h, par, 0)
                send_parts(h, par, 1)

            def mx(h, par):
                g = 2 * h + par
                if par == 1:
                    sp.wait_ge(S.stack[0][0], 144 * (h + 1) + START)
                    sp.sem_inc(S.waits_alone, 1)
                    sp.wait_ge(S.exps, 32 * h + START)
                    sp.sem_inc(S.waits_alone, 1)
                    sp.dma_start(KT[:, :, :], KS[0][0:QKM, :, GC - P:GC]).then_inc(S.tails, 16)
                sp.wait_ge(S.mT, g + 1 + START)
                sp.sem_inc(S.waits_alone, 1)
                for c in range(3):
                    sp.dma_start(QS[par][QK + c:QK + c + 1, :, :], MT[c * H:(c + 1) * H, :]).then_inc(S.mrow[par], 16)

            def attend(h, par, last):
                if par == 1:
                    for q in range(2):
                        sp.wait_ge(S.hT, 2 * h + q + 1 + START)
                        sp.sem_inc(S.waits_alone, 1)
                        sp.dma_start(hT_d[2 * h + q], hT).then_inc(S.hT_out[q], 16)

            attention_order(sp, (norm, prep, mx, attend))
            sp_rest(sp)

        @block.gpsimd
        def _(pool):
            V = nc.gpsimd
            done = 0
            zero = [(ident[:, :], 0.0), (identb[:, :], 0.0), (mkey[:, :, :, :], 0.0), (mqry[:, :, :, :], 0.0), (tri[:, :], 1.0),
                    (avg[:, :], 1.0 / E), (half[:, :], -0.5), (ones_row[:, :], 1.0), (SB[:, :, :], 0.0), (rb[:, 1, :], 0.0),
                    (cw0[:, :, EX:EX + 1], 1.0)]
            zero += [(v[:, :, :, E:E + 1], 1.0) for v in VA + VL] + [(k[32:64, :, :], 1.0) for k in KS]
            for ap, value in zero:
                V.memset(ap, value).then_inc(S.consts, 1)
                done += 1
                pool.wait_ge(S.consts, done)
            V.iota(iou[:, :], pattern=[[1, EX]], base=0, channel_multiplier=0).then_inc(S.consts, 1)
            pool.wait_ge(S.consts, done + 1)
            V.tensor_copy(iot[:, :], iou[:, :]).then_inc(S.consts, 1)
            done += 2
            picks = [(ident[:, :], ALU.not_equal, 1.0, 0, [[-1, P]], 1), (identb[:, :], ALU.not_equal, 1.0, 0, [[-1, P]], 1),
                     (tri[:, :], ALU.is_ge, 0.0, 0, [[1, P]], -1)]
            for i in range(2):
                picks += [(mkey[:, i, 0, :], ALU.is_gt, MASKED, 0, [[-1, P]], 1),
                          (mkey[:, i, 1, :], ALU.is_ge, MASKED, 0, [[1, P]], -1),
                          (mqry[:, i, 0, :], ALU.is_gt, MASKED, 0, [[1, P]], -1),
                          (mqry[:, i, 1, :], ALU.is_ge, MASKED, 0, [[-1, P]], 1)]
            picks += [(h_e(avg[:, :]), ALU.is_ge, 0.0, 0, [[-E, H], [0, E]], 1),
                      (h_e(avg[:, :]), ALU.is_ge, 0.0, E - 1, [[E, H], [0, E]], -1)]
            for ap, compare, fill, base, pattern, mult in picks:
                pool.wait_ge(S.consts, done)
                V.affine_select(out=ap, in_=ap, compare_op=compare, fill=fill, base=base, pattern=pattern, channel_multiplier=mult)\
                    .then_inc(S.consts, 1)
                done += 1
            pool.wait_ge(S.consts, done)
            V.tensor_tensor(cen[:, :], ident[:, :], avg[:, :], ALU.subtract).then_inc(S.consts, 1)
            done += 1
            assert done == N_CONSTS, done
            pool.wait_ge(S.consts, done)
            V.memset(idv[0:1, 0:1], 0.0).then_inc(S.setup, 1)
            pool.wait_ge(S.setup, SETUP)

            def rstd_of(stats, rstds, n):
                pool.wait_ge(stats, 12 * n + 8 + START)
                pool.sem_inc(S.waits_alone, 1)
                V.tensor_scalar(rstd, mv[:, :, 1], EPS, 1.0, ALU.add, ALU.mult).then_inc(rstds, 1)
                pool.wait_ge(rstds, 2 * n + 1 + START)
                pool.sem_inc(S.waits_alone, 1)
                V.tensor_tensor(rstd, rstd, half[:, :], ALU.pow).then_inc(rstds, 1)

            def norm(h, par):
                g = 2 * h + par
                rstd_of(S.lnp, S.lnp_rstd, 2 * g)
                rstd_of(S.lnp, S.lnp_rstd, 2 * g + 1)

            def prep(h, par):
                g = 2 * h + par
                pool.wait_ge(S.resid, 2 * g + 2 + START)
                pool.sem_inc(S.waits_alone, 1)
                pool.wait_ge(S.sent[1], 32 * g + START)
                pool.sem_inc(S.waits_alone, 1)
                V.tensor_copy(parts[:, :, 1, :], res).then_inc(S.mid, 1)
                pool.wait_ge(S.mid, 2 * g + 1 + START)
                pool.sem_inc(S.waits_alone, 1)
                V.tensor_tensor(parts[:, :, 2, :], res, parts[:, :, 1, :], ALU.subtract).then_inc(S.low, 1)
                pool.wait_ge(S.lin_y, 2 * g + 2 + START)
                pool.sem_inc(S.waits_alone, 1)
                pool.wait_ge(S.lin_sum, g + START)
                pool.sem_inc(S.waits_alone, 1)
                V.tensor_scalar(eb, Y32, 0.0, MASKED, ALU.min, ALU.max).then_inc(S.lin_min, 1)
                pool.wait_ge(S.lin_sum, g + 1 + START)
                pool.sem_inc(S.waits_alone, 1)
                pool.wait_ge(S.ol, 4 * (g - 1) + START)
                pool.sem_inc(S.waits_alone, 1)
                V.tensor_scalar(QF[par], Y32[:, 0, :], 1e-4, 1.0, ALU.add, ALU.mult).then_inc(S.lin_qk, 1)
                V.tensor_scalar(Y32[:, 1, :], Y32[:, 1, :], 1e-4, 1.0, ALU.add, ALU.mult).then_inc(S.lin_qk, 1)
                pool.wait_ge(S.high, 4 * g + 4 + START)
                pool.sem_inc(S.waits_alone, 1)
                pool.wait_ge(S.low, 2 * g + 1 + START)
                pool.sem_inc(S.waits_alone, 1)
                V.tensor_tensor(res[:, 0, :], QF[par], parts[:, 0, 0, :], ALU.subtract).then_inc(S.lin_res, 1)
                V.tensor_tensor(res[:, 1, :], Y32[:, 1, :], parts[:, 1, 0, :], ALU.subtract).then_inc(S.lin_res, 1)
                pool.wait_ge(S.lin_res, 2 * g + 2 + START)
                pool.sem_inc(S.waits_alone, 1)
                V.tensor_copy(parts[:, :, 1, :], res).then_inc(S.mid, 1)
                pool.wait_ge(S.mid, 2 * g + 2 + START)
                pool.sem_inc(S.waits_alone, 1)
                V.tensor_tensor(parts[:, :, 2, :], res, parts[:, :, 1, :], ALU.subtract).then_inc(S.low, 1)
                pool.wait_ge(S.tm, 12 * g + 12 + START)
                pool.sem_inc(S.waits_alone, 1)
                V.tensor_scalar(kexp, kraw, 0.0, MASKED, ALU.min, ALU.max).then_inc(S.kmin, 1)
                pool.wait_ge(S.kmin, g + 1 + START)
                pool.sem_inc(S.waits_alone, 1)
                V.tensor_scalar(kraw, kraw, 0.0, 1e-4, ALU.max, ALU.add).then_inc(S.kmax, 1)
                pool.wait_ge(S.kmax, g + 1 + START)
                pool.sem_inc(S.waits_alone, 1)
                pool.wait_ge(S.kexp, g + 1 + START)
                pool.sem_inc(S.waits_alone, 1)
                V.tensor_tensor(KST[par], kraw, kexp, ALU.add).then_inc(S.kst, 1)
                if par == 1:
                    pool.wait_ge(S.tm, 12 * g + START)
                    pool.sem_inc(S.waits_alone, 1)
                    pool.wait_ge(S.pv, 32 * h + START)
                    pool.sem_inc(S.waits_alone, 1)
                    V.tensor_copy(VT[:, :, :], VA[0][:, GT - 1, :, :]).then_inc(S.tailv, 1)

            def attend(h, par, last):
                g = 2 * h + par
                pool.wait_ge(S.x1, 4 * g + 4 + START)
                pool.sem_inc(S.waits_alone, 1)
                V.tensor_tensor(X[:, bass.ds(g * GT, GT), :], X1, XIN[par], ALU.add).then_inc(S.xsum, 1)
                rstd_of(S.lne, S.lne_rstd, g)

            attention_order(pool, (norm, prep, nothing, attend))
            pool_rest(pool)

        @block.scalar
        def _(act):
            V = nc.scalar
            act.wait_ge(S.loaded, n_load[0])
            act.wait_ge(S.wT, 1)
            for i in range(2):
                V.activation(wsqT[:, 4 * i:4 * i + 4, :].rearrange("p a b -> p (a b)"), ring[i][:, 0, :], ACT.Copy).then_inc(S.wTc, 1)
            act.wait_ge(S.wmixed, 1)
            V.activation(wmix[:, :, :], psT[:, 0:2, :], ACT.Copy).then_inc(S.actset, 1)
            V.activation(rw1[:, :], psY[:, 0:EX], ACT.Copy).then_inc(S.actset, 1)
            V.activation(bfm[:, :], psY[:, 16:20], ACT.Copy).then_inc(S.actset, 1)
            V.activation(l1w[:, 2:3], l1w[:, 0:1], ACT.Exp).then_inc(S.actset, 1)
            act.wait_ge(S.actset, 4)
            V.activation(l1w[:, 3:4], l1w[:, 2:3], ACT.Exp, scale=-1.0).then_inc(S.actset, 1)
            act.wait_ge(S.actset, 5)
            V.activation(bcol[:, 2:3], l1w[:, 2:3], ACT.Copy).then_inc(S.setup, 1)
            act.wait_ge(S.setup, SETUP)

            def prep(h, par):
                g = 2 * h + par
                r = lambda k: ring[k % 2]
                act.wait_ge(S.turn_prep, 6 * g + 1 + START)
                act.wait_ge(S.xnT_out[1 - par], 16 * (h if par == 0 else h + 1) + START)
                V.activation(xnT, r(0)[:, 0, :], ACT.Copy).then_inc(S.xnT, 1)
                act.wait_ge(S.turn_prep, 6 * g + 2 + START)
                V.activation(xhT, r(1)[:, 0, :], ACT.Identity, scale=gb[:, 0:1], bias=gb[:, 1:2]).then_inc(S.xhT, 1)
                act.wait_ge(S.turn_prep, 6 * g + 3 + START)
                act.wait_ge(S.sent[1], 32 * g + START)
                for i in range(2):
                    V.activation(parts[:, i, 0, :], r(2)[:, i, :], ACT.Identity, bias=bfm[:, i:i + 1]).then_inc(S.high, 1)
                act.wait_ge(S.rt0, 22 * g + 2 + START)
                V.activation(lg, lg, ACT.Exp).then_inc(S.rt0_exp, 1)
                act.wait_ge(S.lin_min, g + 1 + START)
                V.activation(eb, eb, ACT.Exp).then_inc(S.lin_exp, 1)
                act.wait_ge(S.lin_qk, 2 * g + 2 + START)
                act.wait_ge(S.sent[0], 32 * (g + 1) + START)
                V.activation(parts[:, 0, 0, :], QF[par], ACT.Copy).then_inc(S.high, 1)
                V.activation(parts[:, 1, 0, :], Y32[:, 1, :], ACT.Copy).then_inc(S.high, 1)
                act.wait_ge(S.kmin, g + 1 + START)
                V.activation(kexp, kexp, ACT.Exp).then_inc(S.kexp, 1)

            def send_hT(g, par, h):
                act.wait_ge(S.hT_turn, g + 1 + START)
                act.wait_ge(S.hT_out[1 - par], 16 * (h + par) + START)
                V.activation(hT, psT[:, :, :].rearrange("p a b -> p (a b)"), ACT.Identity, scale=gb[:, 2:3],
                             bias=gb[:, 3:4]).then_inc(S.hT, 1)

            def mx(h, par):
                g = 2 * h + par
                act.wait_ge(S.mT_turn, g + 1 + START)
                act.wait_ge(S.mrow[1 - par], 48 * (h + par) + START)
                V.activation(MT[0:3 * H, :], psY[:, 256:512].bitcast(BF16)[0:3 * H, :], ACT.Copy).then_inc(S.mT, 1)
                if par == 1:
                    send_hT(g - 1, 0, h)

            def attend(h, par, last):
                g = 2 * h + par
                for j in range(GT + 1):
                    t = GT * g + j
                    if j < GT:
                        for q in range(4):
                            act.wait_ge(S.turn_attend, 24 * g + 6 * j + q + 1 + START)
                            act.wait_ge(S.pv, 4 * t + max(q - 1, 0) + START)
                            n = 256 if par == 0 and j == 0 else 512
                            V.activation(PB[q % 2].rearrange("p a b c -> p (a b c)")[:, 0:2 * n].rearrange("p (a n) -> p a n", a=2),
                                         ring[q % 2][:, :, 0:n], ACT.Exp, scale=RSQ).then_inc(S.exps, 1)
                    if j > 0:
                        act.wait_ge(S.y, t + START)
                        V.activation(AST, psT[:, 0:2, :], ACT.Copy).then_inc(S.ast, 1)
                    if j < GT:
                        act.wait_ge(S.pv, 4 * t + 4 + START)
                        act.wait_ge(S.t1, t + START)
                        V.activation(OAs, psA[:, :, :], ACT.Copy).then_inc(S.oas, 1)
                        act.wait_ge(S.ol, t + 1 + START)
                        act.wait_ge(S.t2, t + START)
                        V.activation(OLs, psL[:, :, :], ACT.Copy).then_inc(S.ols, 1)
                if par == 1:
                    send_hT(g, 1, h)

            attention_order(act, (nothing, prep, mx, attend))
            act_rest(act)

        def layernorm(eng, steps, rstds, n, src, dst, free=None, value=None):
            V = nc.vector
            for j in range(GT):
                V.bn_stats(st6[:, j, :], src(j)).then_inc(steps, 1)
            eng.wait_ge(steps, 12 * n + 4 + START)
            eng.sem_inc(S.waits_alone, 1)
            for j in range(GT):
                V.bn_aggr(mv[:, j, :], st6[:, j, :]).then_inc(steps, 1)
            eng.wait_ge(rstds, 2 * n + 2 + START)
            if free is not None:
                eng.wait_ge(free, value)
            for j in range(GT):
                V.tensor_scalar(dst(j), src(j), mv[:, j, 0:1], rstd[:, j:j + 1], ALU.subtract, ALU.mult).then_inc(steps, 1)

        def route_start(eng, steps, read, g, logits, layer):
            V = nc.vector
            V.tensor_tensor(lg, logits, rb[:, layer, :].unsqueeze(1).to_broadcast([P, GT, EX]), ALU.add).then_inc(read, 1)
            eng.wait_ge(read, g + 1 + START)
            V.tensor_reduce(mx4, lg, AX_X, ALU.max).then_inc(steps, 1)
            eng.wait_ge(steps, 22 * g + 1 + START)
            V.tensor_tensor(lg, lg, mx4.unsqueeze(2).to_broadcast([P, GT, EX]), ALU.subtract).then_inc(steps, 1)

        def route_end(eng, steps, exps, g, layer, cw):
            V = nc.vector
            base = 22 * g + START
            eng.wait_ge(exps, g + 1 + START)
            V.tensor_reduce(mx4, lg, AX_X, ALU.add).then_inc(steps, 1)
            eng.wait_ge(steps, base + 3)
            V.reciprocal(mx4, mx4).then_inc(steps, 1)
            eng.wait_ge(steps, base + 4)
            V.tensor_tensor(lg, lg, mx4.unsqueeze(2).to_broadcast([P, GT, EX]), ALU.mult).then_inc(steps, 1)
            eng.wait_ge(steps, base + 5)
            eng.sem_inc(S.waits_alone, 1)
            for j in range(GT):
                V.max(t8[:, j, :], lg[:, j, :]).then_inc(steps, 1)
            eng.wait_ge(steps, base + 9)
            eng.sem_inc(S.waits_alone, 1)
            for j in range(GT):
                V.max_index(i8[:, j, :], t8[:, j, :], lg[:, j, :]).then_inc(steps, 1)
            eng.wait_ge(steps, base + 13)
            V.tensor_copy(idf, i8[:, :, 0:2]).then_inc(steps, 1)
            eng.wait_ge(steps, base + 14)
            for k in range(2):
                V.tensor_tensor(oh[:, k], iot[:, :].unsqueeze(1).to_broadcast([P, GT, EX]),
                                idf[:, :, k].unsqueeze(2).to_broadcast([P, GT, EX]), ALU.is_equal).then_inc(steps, 1)
            V.tensor_tensor(mx4, t8[:, :, 0], t8[:, :, 1], ALU.add).then_inc(steps, 1)
            eng.wait_ge(steps, base + 17)
            V.tensor_tensor(oh[:, 0], oh[:, 0], oh[:, 1], ALU.add).then_inc(steps, 1)
            V.tensor_scalar(mx4, mx4, 1e-9 * layer, None, ALU.add).then_inc(steps, 1)
            eng.wait_ge(steps, base + 19)
            V.reciprocal(mx4, mx4).then_inc(steps, 1)
            V.tensor_tensor(oh[:, 0], oh[:, 0], lg, ALU.mult).then_inc(steps, 1)
            eng.wait_ge(steps, base + 21)
            V.tensor_tensor(cw[:, bass.ds(g * GT, GT), 0:EX], oh[:, 0], mx4.unsqueeze(2).to_broadcast([P, GT, EX]), ALU.mult)\
                .then_inc(steps, 1)

        @block.vector
        def _(dve):
            V = nc.vector
            V.memset(psA[:, :, :], 0.0).then_inc(S.dveset, 1)
            V.memset(psL[:, :, :], 0.0).then_inc(S.dveset, 1)
            V.memset(eps_col[:, :], EPS).then_inc(S.dveset, 1)
            dve.wait_ge(S.loaded, n_load[0])
            for i, (a, o) in enumerate(((0, 0), (0, 1), (1, 0), (1, 1))):
                V.tensor_copy(wfm[:, i, :].rearrange("p (e h) -> p h e", e=E), h_e(wraw[a][:, o * D:o * D + D])).then_inc(S.dveset, 1)
                V.tensor_copy(btmp[0:1, i, :].rearrange("p (e h) -> p h e", e=E), h_e(braw[a][0:1, o * D:o * D + D])).then_inc(S.bperm, 1)
            for dst, src in ((wtm, wraw), (btm, braw)):
                V.tensor_copy(dst[:, 0, :], src[0][:, 2 * D:3 * D]).then_inc(S.dveset, 1)
                V.tensor_copy(dst[:, 1, :], src[1][:, 2 * D:3 * D]).then_inc(S.dveset, 1)
                V.tensor_copy(dst[:, 2, :].rearrange("p (e h) -> p h e", e=E), h_e(src[1][:, D:2 * D])).then_inc(S.dveset, 1)
            V.tensor_tensor(bcol[:, 2:3], bcol[:, 0:1], bcol[:, 1:2], ALU.add).then_inc(S.bsum, 1)
            dve.wait_ge(S.actset, 3)
            V.tensor_tensor(bc_row[:, :], psY[0:1, 32:32 + D], bo_row[0:1, :], ALU.add).then_inc(S.dveset, 1)
            dve.wait_ge(S.consts, N_CONSTS)
            V.tensor_reduce(bd[:, :], ident[:, :].rearrange("p (e h) -> p h e", e=E), AX_X, ALU.add).then_inc(S.dveset, 1)
            dve.wait_ge(S.dveset, 15)
            V.memset(st6[:, :, :], 0.0).then_inc(S.setup, 1)
            dve.wait_ge(S.setup, SETUP)

            def norm(h, par):
                g = 2 * h + par
                dve.wait_ge(S.xin[par], 16 * (h + 1) + START)
                layernorm(dve, S.lnp, S.lnp_rstd, 2 * g, lambda j: XIN[par][:, j, :], lambda j: XN[par][:, j, :])
                dve.wait_ge(S.lnp, 24 * g + 12 + START)
                layernorm(dve, S.lnp, S.lnp_rstd, 2 * g + 1, lambda j: XN[par][:, j, :], lambda j: XH[:, j, :],
                          S.turn_prep, 6 * (g - 1) + 2 + START)

            def mx(h, par):
                g = 2 * h + par
                for j in range(GT):
                    n = P if par == 0 and j == 0 else 2 * P
                    for q in range(4):
                        dve.wait_ge(S.turn_max, 16 * g + 4 * j + q + 1 + START)
                        V.tensor_reduce(mmax[:, j, 4 * q:4 * q + 4].rearrange("p (a b) -> p a b", a=2),
                                        ring[q % 2][:, :, 0:2 * n].rearrange("p a (b n) -> p a b n", b=2), AX_X, ALU.max)\
                            .then_inc(S.mred, 1)
                dve.wait_ge(S.mred, 16 * g + 16 + START)
                dve.wait_ge(S.mT_turn, g + START)
                V.tensor_scalar(MS[:, :, 0:H], mmax, -1.0, None, ALU.mult).then_inc(S.mparts, 1)
                dve.wait_ge(S.mparts, 4 * g + 1 + START)
                V.scalar_tensor_tensor(out=mres, in0=mmax, scalar=-1.0, in1=MS[:, :, 0:H], op0=ALU.mult, op1=ALU.subtract)\
                    .then_inc(S.mparts, 1)
                dve.wait_ge(S.mparts, 4 * g + 2 + START)
                V.tensor_copy(MS[:, :, H:2 * H], mres).then_inc(S.mparts, 1)
                dve.wait_ge(S.mparts, 4 * g + 3 + START)
                V.tensor_tensor(MS[:, :, 2 * H:3 * H], mres, MS[:, :, H:2 * H], ALU.subtract).then_inc(S.mparts, 1)

            def prep(h, par):
                g = 2 * h + par
                r = lambda k: ring[k % 2]
                dve.wait_ge(S.turn_prep, 6 * g + 2 + START)
                route_start(dve, S.rt0, S.logits, g, r(1)[:, 1, 0:GT * EX].rearrange("p (a b) -> p a b", a=GT), 0)
                dve.wait_ge(S.turn_prep, 6 * g + 3 + START)
                dve.wait_ge(S.low, 2 * g + START)
                for i in range(2):
                    dve.wait_ge(S.high, 4 * g + i + 1 + START)
                    V.scalar_tensor_tensor(out=res[:, i, :], in0=r(2)[:, i, :], scalar=bfm[:, i:i + 1], in1=parts[:, i, 0, :],
                                           op0=ALU.add, op1=ALU.subtract).then_inc(S.resid, 1)
                dve.wait_ge(S.turn_prep, 6 * g + 4 + START)
                for i in range(2):
                    V.tensor_scalar(Y32[:, i, :], r(3)[:, i, :], bfm[:, 2 + i:3 + i], (RSQ, 1.0)[i], ALU.add, ALU.mult)\
                        .then_inc(S.lin_y, 1)
                dve.wait_ge(S.pv, 16 * (g - 1) + START)
                dve.wait_ge(S.ol, 4 * (g - 1) + START)
                dve.wait_ge(S.kst, g + START)
                if par == 0:
                    dve.wait_ge(S.tailv, h + START)
                for j in range(GT):
                    dve.wait_ge(S.turn_prep, 6 * g + 5 + j // 2 + START)
                    src = r(4 + j // 2)[:, j % 2, 0:3 * D].rearrange("p (a n) -> p a n", a=3)
                    for i, dst in enumerate((VA[par][:, j, :, 0:E], VL[par][:, j, :, 0:E], h_e(kraw[:, j, :]))):
                        V.tensor_tensor(dst, h_e(src[:, i, :]), h_e(btm[:, i, :]), ALU.add).then_inc(S.tm, 1)
                dve.wait_ge(S.lin_exp, g + 1 + START)
                V.scalar_tensor_tensor(out=Y32.rearrange("p a b -> p (a b)"), in0=Y32.rearrange("p a b -> p (a b)"), scalar=0.0,
                                       in1=eb.rearrange("p a b -> p (a b)"), op0=ALU.max, op1=ALU.add).then_inc(S.lin_sum, 1)
                route_end(dve, S.rt0, S.rt0_exp, g, 0, cw0)

            def attend(h, par, last):
                g = 2 * h + par
                heads = psT[:, :, :].rearrange("p a (b e) -> p (a b) e", e=32)
                for j in range(GT + 1):
                    t = GT * g + j
                    if j > 0:
                        u = t - 1
                        dve.wait_ge(S.t1, u + 1 + START)
                        V.reciprocal(rec[:, 0, :], heads[:, :, E]).then_inc(S.rcp, 1)
                        dve.wait_ge(S.rcp, 3 * u + 1 + START)
                        dve.wait_ge(S.y, u + START)
                        V.tensor_tensor(h_e(ATM[:, 0, :]), heads[:, :, 0:E], rec[:, 0, :].unsqueeze(2).to_broadcast([P, H, E]),
                                        ALU.mult).then_inc(S.at, 1)
                        dve.wait_ge(S.t2, u + 1 + START)
                        V.tensor_scalar(rec[:, 1, :], heads[:, :, E], 1e-6, None, ALU.add).then_inc(S.rcp, 1)
                        dve.wait_ge(S.rcp, 3 * u + 2 + START)
                        V.reciprocal(rec[:, 1, :], rec[:, 1, :]).then_inc(S.rcp, 1)
                        dve.wait_ge(S.rcp, 3 * u + 3 + START)
                        V.tensor_tensor(h_e(ATM[:, 1, :]), heads[:, :, 0:E], rec[:, 1, :].unsqueeze(2).to_broadcast([P, H, E]),
                                        ALU.mult).then_inc(S.lt, 1)
                    if j < GT:
                        for i in range(2):
                            dve.wait_ge(S.turn_attend, 24 * g + 6 * j + 5 + i + START)
                            dve.wait_ge(S.ol, t + START)
                            V.tensor_tensor(AB[i], ring[i][:, :, :].rearrange("p a (b c) -> p (a b) c", c=P),
                                            tri[:, :].unsqueeze(1).to_broadcast([P, 8, P]), ALU.mult).then_inc(S.amask, 1)
                    if j > 0:
                        dve.wait_ge(S.mix, t + START)
                        dve.wait_ge(S.hT_turn, g + START)
                        V.tensor_tensor(X1[:, j - 1, :], psT[:, 2, :], XN[par][:, j - 1, :], ALU.add).then_inc(S.x1, 1)
                    if j < GT and not (par == 1 and j == GT - 1):
                        n = 7 * h + GT * par + j
                        dve.wait_ge(S.state, n + 1 + START)
                        V.tensor_tensor(SU, psY[:, 0:H * (E + 1)].rearrange("p (h e) -> p h e", h=H),
                                        bd[:, :].unsqueeze(2).to_broadcast([P, H, E + 1]), ALU.mult).then_inc(S.su, 1)
                        dve.wait_ge(S.su, n + 1 + START)
                        dve.wait_ge(S.ol, t + 1 + START)
                        if par == 0 and j == 0:
                            V.tensor_copy(SB[:, :, 0:E + 1], SU).then_inc(S.sb, 1)
                        else:
                            dve.wait_ge(S.sb, n + START)
                            V.tensor_tensor(SB[:, :, 0:E + 1], SB[:, :, 0:E + 1], SU, ALU.add).then_inc(S.sb, 1)
                dve.wait_ge(S.x1, 4 * g + 4 + START)
                layernorm(dve, S.lne, S.lne_rstd, g, lambda j: X1[:, j, :], lambda j: HN[:, j, :], S.xsum, g + 1 + START)

            attention_order(dve, (norm, prep, mx, attend))
            dve_rest(dve)

        @block.tensor
        def _(pe):
            T = nc.tensor
            pe.wait_ge(S.loaded, n_load[0])
            pe.wait_ge(S.consts, N_CONSTS)
            for i in range(8):
                m = T.transpose(ring[i // 4][:, 0, :].rearrange("p (a b) -> p a b", a=GT)[:, i % 4, :], wsq[:, i, :], ident[:, :])
            m.then_inc(S.wT, 1)
            T.transpose(psY[:, 0:EX], rw1r[:, :], ident[0:EX, 0:EX])
            pe.wait_ge(S.bperm, 4)
            for i in range(4):
                T.matmul(psY[:, 16 + i:17 + i], btmp[0:1, i, :], ones_row[0:1, 0:1], start=True, stop=True)
            pe.wait_ge(S.wTc, 2)
            pe.wait_ge(S.bsum, 1)
            T.matmul(psY[0:1, 32:32 + D], bcol[:, 2:3], wsq[:, 2, :], start=True, stop=True)
            T.matmul(psT[:, 0, :], wsqT[:, 0, :], wsq[:, 2, :], start=True, stop=True)
            T.matmul(psT[:, 1, :], wsqT[:, 1, :], wsq[:, 2, :], start=True, stop=True).then_inc(S.wmixed, 1)
            pe.wait_ge(S.actset, 5)
            pe.wait_ge(S.dveset, 15)
            T.transpose(psY[:, 0:EX], rw1r[:, :], ident[0:EX, 0:EX]).then_inc(S.setup, 1)
            pe.wait_ge(S.setup, SETUP)

            def tile(j):
                return slice(j * P, (j + 1) * P)

            def prep(h, par):
                g = 2 * h + par
                r = lambda k: ring[k % 2]

                pe.wait_ge(S.mred, 16 * (g - 1) + 15 + START)
                pe.wait_ge(S.lnp, 24 * g + 12 + START)
                for j in range(GT):
                    m = T.transpose(r(0)[:, 0, tile(j)], XN[par][:, j, :], ident[:, :])
                m.then_inc(S.turn_prep, 1)
                pe.wait_ge(S.mred, 16 * (g - 1) + 16 + START)
                pe.wait_ge(S.lnp, 24 * g + 24 + START)
                for j in range(GT):
                    T.transpose(r(1)[:, 0, tile(j)], XH[:, j, :], ident[:, :])
                pe.wait_ge(S.xnT, g + 1 + START)
                for j in range(GT):
                    m = T.matmul(r(1)[:, 1, j * EX:(j + 1) * EX], xnT[:, tile(j)], rw0[:, :], start=True, stop=True)
                m.then_inc(S.turn_prep, 1)
                pe.wait_ge(S.xhT, g + 1 + START)
                for k in range(2):
                    if k == 1:
                        pe.wait_ge(S.logits, g + 1 + START)
                    for i in range(2):
                        m = T.matmul(r(k)[:, i, :], wfm[:, 2 * k + i, :], xhT, start=True, stop=True)
                    m.then_inc(S.turn_prep, 1)
                for k in range(2):
                    if k == 0:
                        pe.wait_ge(S.resid, 2 * g + 2 + START)
                    else:
                        pe.wait_ge(S.lin_y, 2 * g + 2 + START)
                    for i in range(2):
                        m = T.matmul(r(k)[:, i, 0:3 * D], xhT[:, tile(2 * k + i)], wtm[:, :, :].rearrange("p a b -> p (a b)"),
                                     start=True, stop=True)
                    m.then_inc(S.turn_prep, 1)

            def scores(j, par, q, mask, rows, by_key):
                for a in range(2):
                    first = par == 0 and j == 0
                    bank = ring[q % 2][:, a, :]
                    if first:
                        T.matmul(bank[:, 0:2 * P].rearrange("p (b n) -> p b n", b=2), identb[:, :], mask[:, :, 1, :], start=True, stop=True)
                    else:
                        T.matmul(bank, identb[:, :], mask[:, :, :, :].rearrange("p a b c -> p (a b c)"), start=True, stop=True)
                for a in range(2):
                    for b in range(2):
                        hd = 4 * q + 2 * a + b
                        own = KS[par][0:rows, hd, tile(j)]
                        before = KS[par][0:rows, hd, tile(j - 1)] if j > 0 else KT[0:rows, hd, :]
                        blocks = [own] if first else [before, own]
                        for n, keys in enumerate(blocks):
                            c = (len(blocks) * b + n) * P
                            query = QS[par][0:rows, hd, tile(j)]
                            lhsT, rhs = (keys, query) if by_key else (query, keys)
                            m = T.matmul(ring[q % 2][:, a, c:c + P], lhsT, rhs, start=False, stop=True,
                                         skip_group_check=True)
                return m

            def hidden_turn(g):
                pe.wait_ge(S.lne, 12 * g + 12 + START)
                for j in range(GT):
                    m = T.transpose(psT[:, j, :], HN[:, j, :], ident[:, :])
                m.then_inc(S.hT_turn, 1)

            def mx(h, par):
                g = 2 * h + par
                pe.wait_ge(S.stack[0][par], 144 * (h + 1) + START)
                if par == 1:
                    pe.wait_ge(S.tails, 16 * (h + 1) + START)
                for j in range(GT):
                    for q in range(4):
                        if j == 0 and q < 2:
                            pe.wait_ge(S.tm, 12 * g + 6 * (q + 1) + START)
                            pe.wait_ge(S.amask, 8 * g + START)
                        else:
                            pe.wait_ge(S.mred, 16 * g + 4 * j + q - 1 + START)
                        scores(j, par, q, mqry, QK, False).then_inc(S.turn_max, 1)
                pe.wait_ge(S.mparts, 4 * g + 4 + START)
                pe.wait_ge(S.su, 7 * h + GT * par + START)
                pe.wait_ge(S.mT, g + START)
                pe.sem_inc(S.waits_alone, 1)
                for j in range(GT):
                    m = T.transpose(psY[:, 256:512].bitcast(BF16)[0:3 * H, tile(j)], MS[:, j, :], identb[:, :])
                m.then_inc(S.mT_turn, 1)
                if par == 1:
                    hidden_turn(g - 1)

            def attend(h, par, last):
                g = 2 * h + par

                def values(j, q):
                    t = GT * g + j
                    pe.wait_ge(S.exps, 4 * t + q + 1 + START)
                    if q == 0:
                        pe.wait_ge(S.oas, t + START)
                        if j == 0 and par == 1:
                            pe.wait_ge(S.tailv, h + 1 + START)
                    first = par == 0 and j == 0
                    for a in range(4):
                        hd = 4 * q + a
                        before = VA[par][:, j - 1, hd, :] if j > 0 else VT[:, hd, :]
                        blocks = [VA[par][:, j, hd, :]] if first else [before, VA[par][:, j, hd, :]]
                        flat = PB[q % 2].rearrange("p a b c -> p (a b c)")
                        for n, v in enumerate(blocks):
                            c = (len(blocks) * a + n) * P
                            m = T.matmul(psA[32 * a:32 * a + E + 1, q, :], v, flat[:, c:c + P], start=(n == 0), stop=(n == len(blocks) - 1),
                                         skip_group_check=True)
                    m.then_inc(S.pv, 1)

                def finish(j, part):
                    u = GT * g + j
                    if part == 0:
                        pe.wait_ge(S.oas, u + 1 + START)
                        pe.wait_ge(S.x1, u + START)
                        pe.wait_ge(S.hT, g + START)
                        for a in range(4):
                            m = T.transpose(psT[:, a, :], OAs[:, a, :], ident[:, :])
                        m.then_inc(S.t1, 1)
                    elif part == 1:
                        pe.wait_ge(S.ols, u + 1 + START)
                        pe.wait_ge(S.at, u + 1 + START)
                        for a in range(4):
                            m = T.transpose(psT[:, a, :], OLs[:, a, :], ident[:, :])
                        m.then_inc(S.t2, 1)
                    elif part == 2:
                        pe.wait_ge(S.lt, u + 1 + START)
                        for a in range(2):
                            m = T.transpose(psT[:, a, :], ATM[:, a, :], ident[:, :])
                        m.then_inc(S.y, 1)
                    else:
                        pe.wait_ge(S.ast, u + 1 + START)
                        T.matmul(psT[:, 2, :], AST[:, 0, :], wmix[:, 0, :], start=True, stop=False)
                        T.matmul(psT[:, 2, :], AST[:, 1, :], wmix[:, 1, :], start=False, stop=False)
                        T.matmul(psT[:, 2, :], ones_row[:, :], bc_row[:, :], start=False, stop=True).then_inc(S.mix, 1)

                pe.wait_ge(S.stack[1][par], 144 * (h + 1) + START)
                pe.wait_ge(S.mrow[par], 48 * (h + 1) + START)
                for j in range(GT):
                    t = GT * g + j
                    for q in range(4):
                        if j == 0 and q < 2:
                            if last:
                                pe.wait_ge(S.mred, 16 * g + 15 + q + START)
                            else:
                                pe.wait_ge(S.tm, 12 * (g + 1) + 6 * (q + 1) + START)
                        elif q < 2:
                            pe.wait_ge(S.amask, 8 * g + 2 * j + q - 1 + START)
                        else:
                            pe.wait_ge(S.exps, 16 * g + 4 * j + q - 1 + START)
                        scores(j, par, q, mkey, QKM, True).then_inc(S.turn_attend, 1)
                        if q > 0:
                            values(j, q - 1)
                            if j > 0:
                                finish(j - 1, q - 1)
                    for i in range(2):
                        pe.wait_ge(S.exps, 16 * g + 4 * j + i + 3 + START)
                        for m_ in range(8):
                            hd = 8 * i + m_
                            m = T.matmul(ring[i][:, m_ // 4, (m_ % 4) * P:(m_ % 4 + 1) * P], KS[par][LR:LR + QK, hd, tile(j)],
                                         QS[par][LR:LR + QK, hd, tile(j)], start=True, stop=True)
                        m.then_inc(S.turn_attend, 1)
                        if i == 0:
                            values(j, 3)
                            if j > 0:
                                finish(j - 1, 3)
                    n = 7 * h + GT * par + j
                    if not (par == 1 and j == GT - 1):
                        pe.wait_ge(S.kst, g + 1 + START)
                        pe.wait_ge(S.su, n + START)
                        pe.wait_ge(S.mT, g + 1 + START)
                        T.matmul(psY[:, 0:H * (E + 1)], KST[par][:, j, :], VL[par][:, j, :, :].rearrange("p h e -> p (h e)"),
                                 start=True, stop=True).then_inc(S.state, 1)
                    pe.wait_ge(S.lin_qk, 2 * g + 1 + START)
                    pe.wait_ge(S.ols, t + START)
                    pe.wait_ge(S.amask, 8 * g + 2 * j + 2 + START)
                    pe.wait_ge(S.sb, n + START)
                    first = par == 0 and j == 0
                    for q in range(4):
                        if not first:
                            T.matmul(psL[:, q, :], SB[:, 4 * q:4 * q + 4, :].rearrange("p h e -> p (h e)"), QF[par][:, tile(j)],
                                     start=True, stop=True)
                        for a in range(4):
                            hd = 4 * q + a
                            m = T.matmul(psL[32 * a:32 * a + E + 1, q, :], VL[par][:, j, hd, :], AB[hd // 8][:, hd % 8, :],
                                         start=first, stop=True, skip_group_check=True)
                    m.then_inc(S.ol, 1)
                for part in range(4):
                    finish(GT - 1, part)
                if par == 1:
                    hidden_turn(g)

            attention_order(pe, (nothing, prep, mx, attend))
            pe_rest(pe)


_OUTS = [((8, 1024, 128), 'float32')]


def kernel(**inputs):
    import numpy as _np
    import concourse.bacc as _bacc
    from concourse import mybir as _mybir
    from concourse.bass_utils import run_bass_kernel_spmd as _run

    nc = _bacc.Bacc("TRN2", target_bir_lowering=False, num_devices=1)
    arrays, I = {}, {}
    for name in inputs:
        a = _np.ascontiguousarray(inputs[name])
        arrays[f"in_{name}_dram"] = a
        I[name] = nc.dram_tensor(f"in_{name}_dram", a.shape, _mybir.dt.from_np(a.dtype), kind="ExternalInput").ap()
    shape, dtype = _OUTS[0]
    out = nc.dram_tensor("out_0_dram", shape, _mybir.dt.from_np(_np.dtype(dtype)), kind="ExternalOutput").ap()
    build(nc, I, out)
    r = _run(nc, [arrays], core_ids=[0])
    return r.results[0]["out_0_dram"]
```

```python
from contextlib import ExitStack

import concourse.bass as bass
from concourse import mybir

ALU = mybir.AluOpType
ACT = mybir.ActivationFunctionType
F32 = mybir.dt.float32
BF16 = mybir.dt.bfloat16
U32 = mybir.dt.uint32
AX_X = mybir.AxisListType.X

P = 128
GT = 4
GC = GT * P
EPS = 1e-5
MASKED = -1e30
ARENA = 17800


def build(nc, I, out):
    B, L, D = I["L0_attn_x"].shape
    H = I["L1_attn_w"].shape[0]
    E = D // H
    TILES = B * L // P
    NG = TILES // GT
    EX = I["L0_ffn_w1"].shape[0]
    F0 = I["L0_ffn_w1"].shape[2]
    F1 = I["L1_ffn_w1"].shape[2]
    FM = I["L0_attn_W1"].shape[1]
    C0, C1, CM = F0 // P, F1 // P, FM // P
    assert D == P and L == 2 * GC and EX == 8 and H == 16 and E == 8
    QK = 6 * E
    QKM = QK + 3
    LR = 64
    RSQ = float(E) ** -0.5

    x_d = I["L0_attn_x"].rearrange("b (g j p) d -> (b g) p j d", j=GT, p=P)
    out_d = out.rearrange("b (g j p) d -> (b g) p j d", j=GT, p=P)
    xnT_d = nc.dram_tensor("xnT_d", [NG, P, GC], F32, kind="Internal").ap()
    hT_d = nc.dram_tensor("hT_d", [NG, P, GC], F32, kind="Internal").ap()
    yT_d = nc.dram_tensor("yT_d", [NG, P, GC], F32, kind="Internal").ap()
    part_d = [[nc.dram_tensor(f"part_d{i}{j}", [3, P, GC], BF16, kind="Internal").ap() for j in range(4)] for i in range(2)]

    with ExitStack() as ctx:
        def sb(name, shape, dt=F32):
            return ctx.enter_context(nc.sbuf_tensor(name, shape, dt))

        def sem(name):
            return ctx.enter_context(nc.semaphore(name))

        X = sb("X", [P, TILES, D])
        cw0 = sb("cw0", [P, TILES, EX + 1])
        cw1 = sb("cw1", [P, TILES, EX])
        ident = sb("ident", [P, P])
        identb = sb("identb", [P, P], BF16)
        ones_row = sb("ones_row", [1, P])
        half = sb("half", [P, GT])
        iot = sb("iot", [P, EX])
        iou = sb("iou", [P, EX], U32)

        wfm = sb("wfm", [P, 4, D])
        wtm = sb("wtm", [P, 3, D])
        btm = sb("btm", [P, 3, D])
        bfm = sb("bfm", [P, 4])
        gb = sb("gb", [P, 4])
        wsqT = sb("wsqT", [P, 8, D])
        wmix = sb("wmix", [P, 2, D])
        bcol = sb("bcol", [P, 3])
        bc_row = sb("bc_row", [1, D])
        wob_row = sb("wob_row", [1, D])
        rw0 = sb("rw0", [P, EX])
        rb = sb("rb", [P, 2, EX])
        rw1r = sb("rw1r", [EX, D])
        rw1 = sb("rw1", [P, EX])
        W1 = sb("W1", [P, CM, P])
        W2 = sb("W2", [P, CM, D])
        b1m = sb("b1m", [P, CM])
        b2x = sb("b2x", [EX + 1, D])
        fb1 = sb("fb1", [P, EX, C0])
        l1b = sb("l1b", [P, 4])
        l1m = sb("l1m", [P, 4])
        l1w = sb("l1w", [P, 4])

        mkey = sb("mkey", [P, 2, 2, P], BF16)
        mqry = sb("mqry", [P, 2, 2, P], BF16)
        tri = sb("tri", [P, P])
        bd = sb("bd", [P, H])
        cen = sb("cen", [P, P])
        avg = sb("avg", [P, P])

        big = [sb(f"big{i}", [P, H * GC // 2]) for i in range(4)]
        QS, KS = ([b_[:, :].bitcast(BF16).rearrange("p (h t) -> p h t", h=H) for b_ in big[2 * i:2 * i + 2]] for i in range(2))
        KT = sb("KT", [QKM, H, P], BF16)
        VA = [sb(f"VA{i}", [P, GT, H, E + 1]) for i in range(2)]
        VL = [sb(f"VL{i}", [P, GT, H, E + 1]) for i in range(2)]
        VT = sb("VT", [P, H, E + 1])
        SB = sb("SB", [P, H, 32])
        st6 = sb("st6", [P, GT, 6])
        mv = sb("mv", [P, GT, 2])
        rstd = sb("rstd", [P, GT])[:, :]
        rstd2 = sb("rstd2", [P, GT])[:, :]
        lg = sb("lg", [P, GT, EX])[:, :, :]
        mx4 = sb("mx4", [P, GT])[:, :]
        t8 = sb("t8", [P, GT, EX])
        i8 = sb("i8", [P, GT, EX], U32)
        idf = sb("idf", [P, GT, 2])[:, :, :]
        oh = sb("oh", [P, 2, GT, EX])
        eps_col = sb("eps_col", [P, 1])
        arena = sb("arena", [P, ARENA])
        used = [0]

        def carve(*shape, dt=F32):
            n = 1
            for d in shape:
                n *= d
            w = n if dt == F32 else (n + 1) // 2
            a = arena[:, used[0]:used[0] + w]
            used[0] += w
            assert used[0] <= ARENA, used[0]
            if dt != F32:
                a = a.bitcast(dt)
            if len(shape) == 2:
                a = a.rearrange("p (a b) -> p a b", a=shape[0])
            if len(shape) == 3:
                a = a.rearrange("p (a b c) -> p a b c", a=shape[0], b=shape[1])
            return a

        wraw = [carve(3 * D) for _ in range(2)]
        braw = [carve(3 * D) for _ in range(2)]
        wsq = carve(8, D)
        idv = carve(P)
        btmp = carve(4, D)
        bo_row = carve(D)

        used[0] = 0
        XIN = [carve(GT, P) for _ in range(2)]
        XN = [carve(GT, P) for _ in range(2)]
        XH = carve(GT, P)
        X1 = carve(GT, P)
        HN = X1
        xnT = carve(GC)
        xhT = carve(GC)
        hT = carve(GC)
        parts = carve(2, 3, GC, dt=BF16)
        res = carve(2, GC)
        Y32 = carve(2, GC)
        QF = [carve(GC) for _ in range(2)]
        kraw = carve(GT, P)
        eb = carve(2, GC)
        kexp = eb[:, 0, :].rearrange("p (j f) -> p j f", j=GT)
        KST = [carve(GT, P) for _ in range(2)]
        PB = [carve(4, 2, P) for _ in range(2)]
        AB = [carve(8, P) for _ in range(2)]
        OAs = xhT.rearrange("p (j f) -> p j f", j=GT)
        OLs = carve(GT, P)
        ATM = carve(2, P)
        AST = carve(2, P)
        rec = carve(2, H)
        SU = carve(H, E + 1)
        mmax = carve(GT, H)
        mres = carve(GT, H)
        MS = carve(GT, 3 * H, dt=BF16)
        MT = carve(GC, dt=BF16)

        used[0] = 0
        YN = [carve(GT, P) for _ in range(2)]
        xT = carve(L + 4)
        DF = carve(2, GC)
        MX = [big[1][:, i * 4 * GC:(i + 1) * 4 * GC].rearrange("p (c t) -> p c t", c=4) for i in range(2)]
        SG = carve(2, GC)
        KK = carve(2, GC)
        KV = carve(GC)
        ACC = carve(2, GC)
        WK = carve(GC)
        RW = carve(GC)
        SQ = carve(GC)
        CS = carve(2, GC)
        RS = carve(2, GC)
        OT = carve(2, GC)
        fx = [[carve(GC) for _ in range(2)] for _ in range(2)]
        cwg = carve(GT, EX + 1)
        cwT = carve(GC)
        assert used[0] <= ARENA, used

        ring = [ctx.enter_context(nc.psum_tensor(f"ring{i}", [P, 2, GC], F32)) for i in range(2)]
        psA = ctx.enter_context(nc.psum_tensor("psA", [P, GT, P], F32))
        psL = ctx.enter_context(nc.psum_tensor("psL", [P, GT, P], F32))
        psT = ctx.enter_context(nc.psum_tensor("psT", [P, GT, P], F32))
        psY = ctx.enter_context(nc.psum_tensor("psY", [P, GC], F32))

        SETUP = 5
        N_CONSTS = 33

        START = 64
        counters = []

        def counter(name):
            counters.append(sem(name))
            return counters[-1]

        class S:
            amask = counter("amask")
            ast = counter("ast")
            at = counter("at")
            cen = counter("cen")
            cs = counter("cs")
            cwT = counter("cwT")
            cwT_turn = counter("cwT_turn")
            cwg = counter("cwg")
            diff = counter("diff")
            exps = counter("exps")
            grkv = counter("grkv")
            hT = counter("hT")
            hT_turn = counter("hT_turn")
            high = counter("high")
            kexp = counter("kexp")
            kk = counter("kk")
            kmax = counter("kmax")
            kmin = counter("kmin")
            kst = counter("kst")
            kv = counter("kv")
            lin_exp = counter("lin_exp")
            lin_min = counter("lin_min")
            lin_qk = counter("lin_qk")
            lin_res = counter("lin_res")
            lin_sum = counter("lin_sum")
            lin_y = counter("lin_y")
            lnc = counter("lnc")
            lnc_rstd = counter("lnc_rstd")
            lne = counter("lne")
            lne_rstd = counter("lne_rstd")
            lnp = counter("lnp")
            lnp_rstd = counter("lnp_rstd")
            lnv = counter("lnv")
            logit_turn = counter("logit_turn")
            logits = counter("logits")
            logits1 = counter("logits1")
            low = counter("low")
            lt = counter("lt")
            mT = counter("mT")
            mT_turn = counter("mT_turn")
            mid = counter("mid")
            mix = counter("mix")
            mixed = counter("mixed")
            mo = counter("mo")
            mparts = counter("mparts")
            mred = counter("mred")
            oas = counter("oas")
            ol = counter("ol")
            ols = counter("ols")
            ot = counter("ot")
            pv = counter("pv")
            rcp = counter("rcp")
            resid = counter("resid")
            rs = counter("rs")
            rt0 = counter("rt0")
            rt0_exp = counter("rt0_exp")
            rt1 = counter("rt1")
            rt1_exp = counter("rt1_exp")
            rw = counter("rw")
            sb = counter("sb")
            scan = counter("scan")
            sg = counter("sg")
            sq = counter("sq")
            state = counter("state")
            su = counter("su")
            t1 = counter("t1")
            t2 = counter("t2")
            tails = counter("tails")
            tailv = counter("tailv")
            tm = counter("tm")
            turn_attend = counter("turn_attend")
            turn_max = counter("turn_max")
            turn_prep = counter("turn_prep")
            var = counter("var")
            wkv = counter("wkv")
            x1 = counter("x1")
            xT = counter("xT")
            xT0 = counter("xT0")
            xT_turn = counter("xT_turn")
            xhT = counter("xhT")
            xnT = counter("xnT")
            xo = counter("xo")
            xsum = counter("xsum")
            y = counter("y")
            yT_out = counter("yT_out")
            facc = [counter("facc0"), counter("facc1")]
            fact = [counter("fact0"), counter("fact1")]
            fdown = [counter("fdown0"), counter("fdown1")]
            fup = [counter("fup0"), counter("fup1")]
            hT_out = [counter("hT_out0"), counter("hT_out1")]
            mrow = [counter("mrow0"), counter("mrow1")]
            sent = [counter("sent0"), counter("sent1")]
            xin = [counter("xin0"), counter("xin1")]
            xnT_out = [counter("xnT_out0"), counter("xnT_out1")]
            fx = [[counter("fx00"), counter("fx01")], [counter("fx10"), counter("fx11")]]
            stack = [[counter("stack00"), counter("stack01")], [counter("stack10"), counter("stack11")]]
            loaded = sem("loaded")
            consts = sem("consts")
            wT = sem("wT")
            wTc = sem("wTc")
            bperm = sem("bperm")
            bsum = sem("bsum")
            wmixed = sem("wmixed")
            actset = sem("actset")
            dveset = sem("dveset")
            setup = sem("setup")
            out = sem("out")
            waits_alone = sem("waits_alone")
            ffnw = [sem("ffnw0"), sem("ffnw1")]

        def h_e(ap):
            return ap.rearrange("p (h e) -> p h e", e=E)

        N2 = NG // 2

        def attention_order(prep, late, attend, mx, norm, finish, eng):
            norm(0, 0)
            prep(0, 0, False)
            late(0, 0)
            mx(0, 0, False, True)
            with eng.Fori(0, N2 - 1) as b:
                for par in range(2):
                    prep(b + par, 1 - par, True)
                    attend(b, par, False)
                    mx(b + par, 1 - par, True, True)
            prep(N2 - 1, 1, True)
            attend(N2 - 1, 0, False)
            mx(N2 - 1, 1, True, False)
            attend(N2 - 1, 1, True)
            finish(N2 - 1, 1)

        w_up = [big[0][:, 0:EX * F0].rearrange("p (e f) -> p e f", e=EX), big[2][:, :].rearrange("p (e f) -> p e f", e=EX)]
        w_dn = [big[0][:, EX * F0:2 * EX * F0].rearrange("p (e c d) -> p e c d", e=EX, c=C0),
                big[3][:, :].rearrange("p (e c d) -> p e c d", e=EX, c=C1)]
        HS = [big[1][:, i * 4 * GC:(i + 1) * 4 * GC].rearrange("p (c t) -> p c t", c=4) for i in range(2)]
        psO = [psA, psL]
        UNITS = [[("mlp", CM)] + [(e, C0) for e in range(EX)], [(e, C1) for e in range(EX)]]
        TURNS_F = [sum(c for _, c in u) // 2 for u in UNITS]

        def unit_turns(layer, n):
            first = sum(c for _, c in UNITS[layer][:n]) // 2
            return first, UNITS[layer][n][1] // 2

        def ffn_sp(sp, layer):
            dims = xnT_d if layer == 0 else yT_d
            if layer == 0:
                sp.wait_ge(S.amask, 8 * NG + START)
                sp.sem_inc(S.waits_alone, 1)
                sp.wait_ge(S.ol, GT * NG + START)
                sp.sem_inc(S.waits_alone, 1)
                for q in range(2):
                    sp.wait_ge(S.xnT_out[q], 16 * N2 + START)
                    sp.sem_inc(S.waits_alone, 1)
                    sp.wait_ge(S.hT_out[q], 16 * N2 + START)
                    sp.sem_inc(S.waits_alone, 1)
                sp.dma_start(w_up[0], I["L0_ffn_w1"].rearrange("e d f -> d e f")).then_inc(S.ffnw[0], 16)
                sp.dma_start(w_dn[0], I["L0_ffn_w2"].rearrange("e (c f) d -> f e c d", c=C0)).then_inc(S.ffnw[0], 16)
            else:
                sp.wait_ge(S.yT_out, 16 * NG + START)
                sp.sem_inc(S.waits_alone, 1)

            def load(g, par, used_units):
                sp.wait_ge(S.fdown[layer], used_units + START)
                sp.sem_inc(S.waits_alone, 1)
                sp.dma_start(fx[0][par], dims[g]).then_inc(S.fx[layer][par], 16)
                if layer == 0:
                    sp.dma_start(fx[1][par], hT_d[g]).then_inc(S.fx[layer][par], 16)

            def store(g):
                sp.wait_ge(S.facc[1], 32 * (g + 1) + START)
                sp.sem_inc(S.waits_alone, 1)
                sp.dma_start(out_d[g], X[:, bass.ds(g * GT, GT), :]).then_inc(S.out, 16)

            nu = len(UNITS[layer])
            load(0, 0, 0)
            with sp.Fori(0, N2 - 1) as b:
                load(2 * b + 1, 1, nu * 2 * b)
                load(2 * b + 2, 0, nu * (2 * b + 1))
                if layer == 1:
                    store(2 * b)
                    store(2 * b + 1)
            load(NG - 1, 1, nu * (NG - 2))
            if layer == 0:
                sp.dma_start(w_up[1], I["L1_ffn_w1"].rearrange("e d f -> d e f")).then_inc(S.ffnw[1], 16)
                sp.dma_start(w_dn[1], I["L1_ffn_w2"].rearrange("e (c f) d -> f e c d", c=C1)).then_inc(S.ffnw[1], 16)
            else:
                store(NG - 2)
                store(NG - 1)
                sp.wait_ge(S.out, 16 * NG)

        def ffn_pe(pe, layer):
            T = nc.tensor
            units, nt = UNITS[layer], TURNS_F[layer]
            nu = len(units)
            pe.wait_ge(S.ffnw[layer], 32)

            def up(g, b, par, n):
                e, chunks = units[n]
                first, turns = unit_turns(layer, n)
                for i in range(turns):
                    k = first + i
                    slot = (nt * par + k) % 2
                    pe.wait_ge(S.fact[layer], 2 * (nt * g + k - 1) + START)
                    for c in range(2):
                        w = W1[:, 2 * i + c, :] if e == "mlp" else w_up[layer][:, e, (2 * i + c) * P:(2 * i + c + 1) * P]
                        m = T.matmul(ring[slot][:, c, :], w, fx[1 if e == "mlp" else 0][par], start=True, stop=True)
                    m.then_inc(S.fup[layer], 1)

            def down(g, b, par, n):
                e, chunks = units[n]
                first, turns = unit_turns(layer, n)
                o = (nu * par + n)
                hs = HS[o % 2]
                pe.wait_ge(S.fact[layer], 2 * (nt * g + first + turns) + START)
                pe.wait_ge(S.facc[layer], facc_at(layer, g, n - 2) + START)
                for j in range(GT):
                    for c in range(chunks):
                        w = W2[:, c, :] if e == "mlp" else w_dn[layer][:, e, c, :]
                        last = c == chunks - 1 and e != "mlp"
                        m = T.matmul(psO[o % 2][:, j, :], hs[:, c, j * P:(j + 1) * P], w, start=(c == 0), stop=last)
                    if e == "mlp":
                        m = T.matmul(psO[o % 2][:, j, :], cwT[0:EX + 1, j * P:(j + 1) * P], b2x[:, :], start=False, stop=True)
                m.then_inc(S.fdown[layer], 1)

            with pe.Fori(0, N2) as b:
                for par in range(2):
                    g = 2 * b + par
                    pe.wait_ge(S.fx[layer][par], (32 if layer == 0 else 16) * (b + 1) + START)
                    if layer == 0:
                        pe.wait_ge(S.cwg, g + 1 + START)
                        for j in range(GT):
                            m = T.transpose(psT[0:EX + 1, j, :], cwg[:, j, :], ident[:, :])
                        m.then_inc(S.cwT_turn, 1)
                    for n in range(nu + 1):
                        if n < nu:
                            up(g, b, par, n)
                        if n == 1 and layer == 0:
                            pe.wait_ge(S.cwT, g + 1 + START)
                        if n > 0:
                            down(g, b, par, n - 1)

        def facc_at(layer, g, n):
            per = 33 if layer == 0 else 32
            if n < 0:
                return per * g
            n = max(n, 0)
            return per * g + (4 * n + 1 if layer == 0 else 4 * n + 4)

        def ffn_act(act, layer):
            V = nc.scalar
            units, nt = UNITS[layer], TURNS_F[layer]
            nu = len(units)
            func = ACT.Relu if layer == 0 else ACT.Gelu
            act.wait_ge(S.ffnw[layer], 32)
            with act.Fori(0, N2) as b:
                for par in range(2):
                    g = 2 * b + par
                    if layer == 0:
                        act.wait_ge(S.cwT_turn, g + 1 + START)
                        act.wait_ge(S.fdown[0], 9 * g + START)
                        V.activation(cwT[0:EX + 1, :], psT[0:EX + 1, :, :].rearrange("p a b -> p (a b)"), ACT.Copy).then_inc(S.cwT, 1)
                    for n, (e, chunks) in enumerate(units):
                        first, turns = unit_turns(layer, n)
                        hs = HS[(nu * par + n) % 2]
                        act.wait_ge(S.fdown[layer], nu * g + max(n - 1, 0) + START)
                        for i in range(turns):
                            k = first + i
                            slot = (nt * par + k) % 2
                            act.wait_ge(S.fup[layer], nt * g + k + 1 + START)
                            for c in range(2):
                                if layer == 0:
                                    bias = b1m[:, 2 * i + c:2 * i + c + 1] if e == "mlp" else fb1[:, e, 2 * i + c:2 * i + c + 1]
                                    f = ACT.Gelu if e == "mlp" else func
                                    V.activation(hs[:, 2 * i + c, :], ring[slot][:, c, :], f, bias=bias).then_inc(S.fact[0], 1)
                                else:
                                    V.activation(hs[:, 2 * i + c, :], ring[slot][:, c, :], func).then_inc(S.fact[1], 1)

        def ffn_dve(dve, layer):
            V = nc.vector
            units = UNITS[layer]
            nu = len(units)
            cw = (cw0, cw1)[layer]
            with dve.Fori(0, N2) as b:
                for par in range(2):
                    g = 2 * b + par
                    if layer == 0:
                        dve.wait_ge(S.cwT_turn, g + START)
                        V.tensor_copy(cwg, cw0[:, bass.ds(g * GT, GT), :]).then_inc(S.cwg, 1)
                    for n, (e, chunks) in enumerate(units):
                        o = psO[(nu * par + n) % 2]
                        dve.wait_ge(S.fdown[layer], nu * g + n + 1 + START)
                        dve.wait_ge(S.facc[layer], facc_at(layer, g, n - 1) + START)
                        if e == "mlp":
                            xg = X[:, bass.ds(g * GT, GT), :]
                            V.tensor_tensor(xg, o[:, :, :], xg, ALU.add).then_inc(S.facc[0], 1)
                            continue
                        for j in range(GT):
                            xt = X[:, bass.ds(g * GT + j, 1), :].rearrange("p a d -> p (a d)")
                            V.scalar_tensor_tensor(out=xt, in0=o[:, j, :], scalar=cw[:, bass.ds(g * GT + j, 1), e], in1=xt,
                                                   op0=ALU.mult, op1=ALU.add).then_inc(S.facc[layer], 1)

        psAf = psA[:, :, :].rearrange("p a b -> p (a b)")
        psLf = psL[:, :, :].rearrange("p a b -> p (a b)")
        psTf = psT[:, :, :].rearrange("p a b -> p (a b)")

        def mixer_sp(sp):
            with sp.Fori(0, B) as b:
                for q in range(2):
                    sp.wait_ge(S.xT, 2 * b + q + 1 + START)
                    sp.sem_inc(S.waits_alone, 1)
                    sp.wait_ge(S.yT_out, 16 * (2 * b + q) + START)
                    sp.sem_inc(S.waits_alone, 1)
                    sp.dma_start(yT_d[2 * b + q], xT[:, 1 + q * GC:1 + (q + 1) * GC]).then_inc(S.yT_out, 16)

        def mixer_order(eng, prologue, batch):
            prologue()
            batch(0, False, True)
            with eng.Fori(1, B - 1) as b:
                batch(b, True, True)
            batch(B - 1, True, False)

        def mixer_pool(pool):
            V = nc.gpsimd

            def rstd_of(n):
                pool.wait_ge(S.lnc, 12 * n + 8 + START)
                pool.sem_inc(S.waits_alone, 1)
                V.tensor_scalar(rstd, mv[:, :, 1], EPS, 1.0, ALU.add, ALU.mult).then_inc(S.lnc_rstd, 1)
                pool.wait_ge(S.lnc_rstd, 2 * n + 1 + START)
                pool.sem_inc(S.waits_alone, 1)
                V.tensor_tensor(rstd, rstd, half[:, :], ALU.pow).then_inc(S.lnc_rstd, 1)

            def differences(b):
                pool.wait_ge(S.xT, 2 * b + 2 + START)
                pool.sem_inc(S.waits_alone, 1)
                pool.wait_ge(S.xT0, b + 1 + START)
                pool.sem_inc(S.waits_alone, 1)
                for q in range(2):
                    V.tensor_tensor(DF[:, q, :], xT[:, 1 + q * GC:1 + (q + 1) * GC], xT[:, q * GC:(q + 1) * GC], ALU.subtract)\
                        .then_inc(S.diff, 1)

            def gate(n, q):
                pool.wait_ge(S.cs, n + 1 + START)
                pool.sem_inc(S.waits_alone, 1)
                pool.wait_ge(S.rs, n + 2 - q + START)
                pool.sem_inc(S.waits_alone, 1)
                pool.wait_ge(S.mo, n - 1 + START)
                pool.sem_inc(S.waits_alone, 1)
                V.tensor_tensor(OT[:, q, :], CS[:, q, :], RS[:, q, :], ALU.mult).then_inc(S.ot, 1)

            def prologue():
                rstd_of(0)
                rstd_of(1)
                differences(0)

            def batch(b, follows, more):
                if more:
                    rstd_of(2 * b + 2)
                    rstd_of(2 * b + 3)
                    differences(b + 1)
                gate(2 * b, 0)
                gate(2 * b + 1, 1)

            mixer_order(pool, prologue, batch)

        def mixer_act(act):
            V = nc.scalar

            def features(n, q):
                act.wait_ge(S.xT_turn, n + 1 + START)
                act.wait_ge(S.yT_out, 16 * (n - q) + START)
                act.wait_ge(S.mixed, 4 * (n - q) + START)
                V.activation(xT[:, 1 + q * GC:1 + (q + 1) * GC], psTf, ACT.Copy).then_inc(S.xT, 1)
                if q == 1:
                    act.wait_ge(S.xT, n + 1 + START)
                    V.activation(xT[:, 0:1], xT[:, L:L + 1], ACT.Copy).then_inc(S.xT0, 1)

            def router_exp(n):
                act.wait_ge(S.rt1, 22 * n + 2 + START)
                V.activation(lg, lg, ACT.Exp).then_inc(S.rt1_exp, 1)

            def project(n, q):
                act.wait_ge(S.grkv, 2 * n + 1 + START)
                act.wait_ge(S.cs, n - 1 + START)
                V.activation(SG[:, q, :], ring[0][:, 0, :], ACT.Sigmoid, bias=l1b[:, 0:1]).then_inc(S.sg, 1)
                act.wait_ge(S.grkv, 2 * n + 2 + START)
                V.activation(KK[:, q, :], ring[1][:, 0, :], ACT.Identity, bias=l1b[:, 2:3]).then_inc(S.kk, 1)

            def square(n):
                act.wait_ge(S.cen, n + 1 + START)
                V.activation(SQ, psAf, ACT.Square).then_inc(S.sq, 1)

            def variance(n, q):
                act.wait_ge(S.var, n + 1 + START)
                act.wait_ge(S.ot, n - 1 + START)
                V.activation(RS[:, q, :], psLf, ACT.Ln, bias=eps_col[:, 0:1]).then_inc(S.lnv, 1)

            def prologue():
                for q in range(2):
                    features(q, q)
                for q in range(2):
                    router_exp(q)

            def batch(b, follows, more):
                n = 2 * b
                project(n, 0)
                if more:
                    features(n + 2, 0)
                square(n)
                project(n + 1, 1)
                variance(n, 0)
                if more:
                    features(n + 3, 1)
                square(n + 1)
                variance(n + 1, 1)
                act.wait_ge(S.lnv, n + 2 + START)
                V.activation(RS, RS, ACT.Exp, scale=-0.5).then_inc(S.rs, 2)
                if more:
                    router_exp(n + 2)
                    router_exp(n + 3)

            mixer_order(act, prologue, batch)

        def mixer_dve(dve):
            V = nc.vector

            def norm_stats(n):
                for j in range(GT):
                    V.bn_stats(st6[:, j, :], X[:, bass.ds(n * GT + j, 1), :].rearrange("p a d -> p (a d)")).then_inc(S.lnc, 1)
                dve.wait_ge(S.lnc, 12 * n + 4 + START)
                dve.sem_inc(S.waits_alone, 1)
                for j in range(GT):
                    V.bn_aggr(mv[:, j, :], st6[:, j, :]).then_inc(S.lnc, 1)

            def norm_apply(n, q):
                dve.wait_ge(S.lnc_rstd, 2 * n + 2 + START)
                dve.wait_ge(S.xT_turn, n - 1 + START)
                for j in range(GT):
                    V.tensor_scalar(YN[q][:, j, :], X[:, bass.ds(n * GT + j, 1), :].rearrange("p a d -> p (a d)"), mv[:, j, 0:1],
                                    rstd[:, j:j + 1], ALU.subtract, ALU.mult).then_inc(S.lnc, 1)

            def router_start(n, q):
                dve.wait_ge(S.logit_turn, n - q + 2 + START)
                route_start(dve, S.rt1, S.logits1, n, psY[:, q * GT * EX:(q + 1) * GT * EX].rearrange("p (a b) -> p a b", a=GT), 1)

            def router_end(n):
                route_end(dve, S.rt1, S.rt1_exp, n, 1, cw1)

            def mix(n, q):
                dve.wait_ge(S.diff, n - q + 2 + START)
                dve.wait_ge(S.grkv, 2 * n - 2 + START)
                for i in range(4):
                    V.scalar_tensor_tensor(out=MX[q][:, i, :], in0=DF[:, q, :], scalar=l1m[:, i:i + 1],
                                           in1=xT[:, q * GC:(q + 1) * GC], op0=ALU.mult, op1=ALU.add).then_inc(S.mixed, 1)

            def project(n, q):
                dve.wait_ge(S.kk, n + 1 + START)
                V.scalar_tensor_tensor(out=KV, in0=ring[1][:, 1, :], scalar=l1b[:, 3:4], in1=KK[:, q, :], op0=ALU.add, op1=ALU.mult)\
                    .then_inc(S.kv, 1)
                dve.wait_ge(S.kv, n + 1 + START)
                dve.wait_ge(S.scan, n + START)
                V.tensor_tensor_scan(ACC[:, q, :], l1w[:, 3:4].to_broadcast([P, GC]), KV, 0.0 if q == 0 else ACC[:, 0, GC - 1:GC],
                                     ALU.mult, ALU.add).then_inc(S.scan, 1)
                dve.wait_ge(S.scan, n + 1 + START)
                V.scalar_tensor_tensor(out=WK, in0=KV, scalar=l1w[:, 1:2], in1=ACC[:, q, :], op0=ALU.mult, op1=ALU.add)\
                    .then_inc(S.wkv, 1)
                dve.wait_ge(S.wkv, n + 1 + START)
                V.scalar_tensor_tensor(out=RW, in0=ring[0][:, 1, :], scalar=l1b[:, 1:2], in1=WK, op0=ALU.add, op1=ALU.mult)\
                    .then_inc(S.rw, 1)

            def centred(n, q):
                dve.wait_ge(S.sq, n + 1 + START)
                dve.wait_ge(S.ot, n - 1 + START)
                V.tensor_tensor(CS[:, q, :], psAf, SG[:, q, :], ALU.mult).then_inc(S.cs, 1)

            def add(n):
                dve.wait_ge(S.mo, n + 1 + START)
                xg = X[:, bass.ds(n * GT, GT), :]
                V.tensor_tensor(xg, psT[:, :, :], xg, ALU.add).then_inc(S.xo, 1)

            def prologue():
                dve.wait_ge(S.facc[0], 33 * NG + START)
                for q in range(2):
                    norm_stats(q)
                    norm_apply(q, q)
                for q in range(2):
                    router_start(q, q)
                    router_end(q)

            def batch(b, follows, more):
                n = 2 * b
                mix(n, 0)
                mix(n + 1, 1)
                if more:
                    norm_stats(n + 2)
                if follows:
                    add(n - 2)
                project(n, 0)
                if follows:
                    add(n - 1)
                if more:
                    norm_apply(n + 2, 0)
                    norm_stats(n + 3)
                centred(n, 0)
                if more:
                    norm_apply(n + 3, 1)
                project(n + 1, 1)
                if more:
                    router_start(n + 2, 0)
                centred(n + 1, 1)
                if more:
                    router_end(n + 2)
                    router_start(n + 3, 1)
                    router_end(n + 3)

            mixer_order(dve, prologue, batch)
            add(2 * B - 2)
            add(2 * B - 1)

        def mixer_pe(pe):
            T = nc.tensor

            def features(n, q):
                pe.wait_ge(S.lnc, 12 * n + 12 + START)
                pe.wait_ge(S.xT, n + START)
                pe.wait_ge(S.xo, n - 2 - q + START)
                for j in range(GT):
                    m = T.transpose(psT[:, j, :], YN[q][:, j, :], ident[:, :])
                m.then_inc(S.xT_turn, 1)

            def router(n, q):
                pe.wait_ge(S.xT, n + 1 + START)
                pe.wait_ge(S.logits1, n - q + START)
                for j in range(GT):
                    c = 1 + q * GC + j * P
                    m = T.matmul(psY[:, (q * GT + j) * EX:(q * GT + j + 1) * EX], xT[:, c:c + P], rw1[:, :], start=True, stop=True)
                m.then_inc(S.logit_turn, 1)

            def project(n, q):
                pe.wait_ge(S.mixed, 4 * n + 4 + START)
                pe.wait_ge(S.sg, n + START)
                pe.wait_ge(S.rw, n + START)
                for i in range(2):
                    for k in range(2):
                        m = T.matmul(ring[i][:, k, :], wsqT[:, 3 + 2 * i + k, :], MX[q][:, 2 * i + k, :], start=True, stop=True)
                    m.then_inc(S.grkv, 1)

            def centre(n):
                pe.wait_ge(S.rw, n + 1 + START)
                pe.wait_ge(S.cs, n + START)
                T.matmul(psAf, cen[:, :], RW, start=True, stop=True).then_inc(S.cen, 1)

            def variance(n):
                pe.wait_ge(S.sq, n + 1 + START)
                pe.wait_ge(S.lnv, n + START)
                T.matmul(psLf, avg[:, :], SQ, start=True, stop=True).then_inc(S.var, 1)

            def output(n, q, more=True):
                pe.wait_ge(S.ot, n + 1 + START)
                pe.wait_ge(S.xo, n + START)
                pe.wait_ge(S.xT, n - q + 4 + START if more else n - q + 2 + START)
                for j in range(GT):
                    T.matmul(psT[:, j, :], OT[:, q, j * P:(j + 1) * P], wsqT[:, 7, :], start=True, stop=False)
                    m = T.matmul(psT[:, j, :], ones_row[:, :], wob_row[:, :], start=False, stop=True)
                m.then_inc(S.mo, 1)

            def prologue():
                pe.wait_ge(S.cwT, NG + START)
                pe.wait_ge(S.facc[0], 33 * NG + START)
                for q in range(2):
                    features(q, q)
                for q in range(2):
                    router(q, q)

            def batch(b, follows, more):
                n = 2 * b
                project(n, 0)
                if follows:
                    output(n - 2, 0)
                    output(n - 1, 1)
                if more:
                    features(n + 2, 0)
                centre(n)
                project(n + 1, 1)
                variance(n)
                if more:
                    features(n + 3, 1)
                centre(n + 1)
                if more:
                    router(n + 2, 0)
                    router(n + 3, 1)
                variance(n + 1)

            mixer_order(pe, prologue, batch)
            output(2 * B - 2, 0, False)
            output(2 * B - 1, 1, False)

        def sp_rest(sp):
            ffn_sp(sp, 0)
            mixer_sp(sp)
            ffn_sp(sp, 1)

        def pool_rest(pool):
            mixer_pool(pool)

        def act_rest(act):
            ffn_act(act, 0)
            mixer_act(act)
            ffn_act(act, 1)

        def dve_rest(dve):
            ffn_dve(dve, 0)
            mixer_dve(dve)
            ffn_dve(dve, 1)

        def pe_rest(pe):
            ffn_pe(pe, 0)
            mixer_pe(pe)
            ffn_pe(pe, 1)

        def nothing(*a):
            pass

        block = ctx.enter_context(nc.Block())
        n_load = [0]

        @block.sync
        def _(sp):
            def load(dst, src, scattered=False):
                sp.dma_start(dst, src, allow_slow_non_contiguous=scattered).then_inc(S.loaded, 16)
                n_load[0] += 16

            bq = [I["L0_attn_bqkv_a"], I["L0_attn_bqkv_s"]]
            for a, w in enumerate(("L0_attn_Wqkv_a", "L0_attn_Wqkv_s")):
                load(wraw[a], I[w])
                load(braw[a], bq[a].partition_broadcast(P))
            for i, w in enumerate(("L0_attn_Wp_a", "L0_attn_Wo_s", "L0_attn_Wo", "L1_attn_Wg_w", "L1_attn_Wr_w", "L1_attn_Wk_w",
                                   "L1_attn_Wv_w", "L1_attn_Wo_w")):
                load(wsq[:, i, :], I[w])

            def col(dst, name):
                load(dst, I[name].rearrange("(p o) -> p o", o=1))

            for i, w in enumerate(("L0_attn_g1", "L0_attn_b1", "L0_attn_gm", "L0_attn_bm")):
                col(gb[:, i:i + 1], w)
            col(bcol[:, 0:1], "L0_attn_bp_a")
            col(bcol[:, 1:2], "L0_attn_bo_s")
            for i, w in enumerate("grkv"):
                col(l1b[:, i:i + 1], f"L1_attn_W{w}_b")
                col(l1m[:, i:i + 1], f"L1_attn_m{w}")
            load(l1w[:, 0:1], I["L1_attn_w"].rearrange("h (e o) -> (h e) o", o=1))
            load(l1w[:, 1:2], I["L1_attn_u"].rearrange("h (e o) -> (h e) o", o=1))
            load(bo_row[0:1, :], I["L0_attn_bo"].rearrange("(o n) -> o n", o=1))
            load(wob_row[:, :], I["L1_attn_Wo_b"].rearrange("(o n) -> o n", o=1))
            load(rw0[:, :], I["L0_ffn_router_w"])
            load(rb[:, 0, :], I["L0_ffn_router_b"].partition_broadcast(P))
            load(rw1r[:, :], I["L1_ffn_router_w"])
            load(W1[:, :, :], I["L0_attn_W1"].rearrange("d (c f) -> d c f", c=CM))
            load(W2[:, :, :], I["L0_attn_W2"].rearrange("(c f) d -> f c d", c=CM))
            load(b1m[:, :], I["L0_attn_b1m"].rearrange("(c f) -> f c", c=CM), scattered=True)
            load(b2x[0:EX, :], I["L0_ffn_b2"])
            load(b2x[EX:EX + 1, :], I["L0_attn_b2m"].rearrange("(o n) -> o n", o=1))
            load(fb1[:, :, :], I["L0_ffn_b1"].rearrange("e (c f) -> f e c", c=C0), scattered=True)
            for c in counters:
                sp.sem_inc(c, START)
            sp.sem_inc(S.setup, 1)
            sp.wait_ge(S.setup, SETUP)

            def norm(h, par):
                g = 2 * h + par
                sp.wait_ge(S.xsum, g - 1 + START)
                sp.sem_inc(S.waits_alone, 1)
                sp.dma_start(XIN[par], x_d[g]).then_inc(S.xin[par], 16)

            def send_parts(h, par, pair):
                g = 2 * h + par
                sp.wait_ge(S.low, 2 * g + pair + 1 + START)
                sp.sem_inc(S.waits_alone, 1)
                for i in range(2):
                    sp.wait_ge(S.stack[pair][par], 144 * h + START)
                    sp.sem_inc(S.waits_alone, 1)
                    sp.dma_start(part_d[par][2 * pair + i].rearrange("c p t -> p c t"), parts[:, i]).then_inc(S.sent[pair], 16)
                sp.wait_ge(S.sent[pair], 32 * (g + 1) + START)
                sp.sem_inc(S.waits_alone, 1)
                sp.wait_ge(S.amask, 8 * (g - 1) + START)
                sp.sem_inc(S.waits_alone, 1)
                sp.wait_ge(S.tails, 16 * h + START)
                sp.sem_inc(S.waits_alone, 1)
                r0 = LR if pair else 0
                q_d, k_d = part_d[par][2 * pair], part_d[par][2 * pair + 1]
                row = 0
                for n in (3, 2, 1):
                    sp.dma_start(QS[par][r0 + row:r0 + row + E * n, :, :],
                                 q_d[0:n].rearrange("c (e h) t -> (c e) h t", h=H)).then_inc(S.stack[pair][par], 16)
                    for i in range(n):
                        sp.dma_start(KS[par][r0 + row + E * i:r0 + row + E * i + E, :, :],
                                     k_d[3 - n].rearrange("(e h) t -> e h t", h=H)).then_inc(S.stack[pair][par], 16)
                    row += E * n

            def prep(h, par, follows):
                g = 2 * h + par
                if par == 1:
                    sp.wait_ge(S.stack[0][0], 144 * (h + 1) + START)
                    sp.sem_inc(S.waits_alone, 1)
                    sp.wait_ge(S.exps, 32 * h + START)
                    sp.sem_inc(S.waits_alone, 1)
                    sp.dma_start(KT[:, :, :], KS[0][0:QKM, :, GC - P:GC]).then_inc(S.tails, 16)
                sp.wait_ge(S.xnT, g + 1 + START)
                sp.sem_inc(S.waits_alone, 1)
                sp.dma_start(xnT_d[g], xnT).then_inc(S.xnT_out[par], 16)
                if follows:
                    minus_rows(h - 1 + par, 1 - par)
                send_parts(h, par, 0)
                send_parts(h, par, 1)

            def minus_rows(h, par):
                g = 2 * h + par
                sp.wait_ge(S.mT, g + 1 + START)
                sp.sem_inc(S.waits_alone, 1)
                for c in range(3):
                    sp.dma_start(QS[par][QK + c:QK + c + 1, :, :], MT[c * H:(c + 1) * H, :]).then_inc(S.mrow[par], 16)

            def store_hidden(h, par):
                g = 2 * h + par
                sp.wait_ge(S.hT, g + 1 + START)
                sp.sem_inc(S.waits_alone, 1)
                sp.dma_start(hT_d[g], hT).then_inc(S.hT_out[par], 16)

            def mx(h, par, follows, more):
                if more:
                    norm(h + par, 1 - par)
                if follows:
                    store_hidden(h - 1 + par, 1 - par)
                if not more:
                    minus_rows(h, par)

            attention_order(prep, nothing, nothing, mx, norm, store_hidden, sp)
            sp_rest(sp)

        @block.gpsimd
        def _(pool):
            V = nc.gpsimd
            done = 0
            zero = [(ident[:, :], 0.0), (identb[:, :], 0.0), (mkey[:, :, :, :], 0.0), (mqry[:, :, :, :], 0.0), (tri[:, :], 1.0),
                    (avg[:, :], 1.0 / E), (half[:, :], -0.5), (ones_row[:, :], 1.0), (SB[:, :, :], 0.0), (rb[:, 1, :], 0.0),
                    (cw0[:, :, EX:EX + 1], 1.0)]
            zero += [(v[:, :, :, E:E + 1], 1.0) for v in VA + VL] + [(k[32:64, :, :], 1.0) for k in KS]
            for ap, value in zero:
                V.memset(ap, value).then_inc(S.consts, 1)
                done += 1
                pool.wait_ge(S.consts, done)
            V.iota(iou[:, :], pattern=[[1, EX]], base=0, channel_multiplier=0).then_inc(S.consts, 1)
            pool.wait_ge(S.consts, done + 1)
            V.tensor_copy(iot[:, :], iou[:, :]).then_inc(S.consts, 1)
            done += 2
            picks = [(ident[:, :], ALU.not_equal, 1.0, 0, [[-1, P]], 1), (identb[:, :], ALU.not_equal, 1.0, 0, [[-1, P]], 1),
                     (tri[:, :], ALU.is_ge, 0.0, 0, [[1, P]], -1)]
            for i in range(2):
                picks += [(mkey[:, i, 0, :], ALU.is_gt, MASKED, 0, [[-1, P]], 1),
                          (mkey[:, i, 1, :], ALU.is_ge, MASKED, 0, [[1, P]], -1),
                          (mqry[:, i, 0, :], ALU.is_gt, MASKED, 0, [[1, P]], -1),
                          (mqry[:, i, 1, :], ALU.is_ge, MASKED, 0, [[-1, P]], 1)]
            picks += [(h_e(avg[:, :]), ALU.is_ge, 0.0, 0, [[-E, H], [0, E]], 1),
                      (h_e(avg[:, :]), ALU.is_ge, 0.0, E - 1, [[E, H], [0, E]], -1)]
            for ap, compare, fill, base, pattern, mult in picks:
                pool.wait_ge(S.consts, done)
                V.affine_select(out=ap, in_=ap, compare_op=compare, fill=fill, base=base, pattern=pattern, channel_multiplier=mult)\
                    .then_inc(S.consts, 1)
                done += 1
            pool.wait_ge(S.consts, done)
            V.tensor_tensor(cen[:, :], ident[:, :], avg[:, :], ALU.subtract).then_inc(S.consts, 1)
            done += 1
            assert done == N_CONSTS, done
            pool.wait_ge(S.consts, done)
            V.memset(idv[0:1, 0:1], 0.0).then_inc(S.setup, 1)
            pool.wait_ge(S.setup, SETUP)

            def rstd_of(stats, rstds, n):
                pool.wait_ge(stats, 12 * n + 8 + START)
                pool.sem_inc(S.waits_alone, 1)
                V.tensor_scalar(rstd, mv[:, :, 1], EPS, 1.0, ALU.add, ALU.mult).then_inc(rstds, 1)
                pool.wait_ge(rstds, 2 * n + 1 + START)
                pool.sem_inc(S.waits_alone, 1)
                V.tensor_tensor(rstd, rstd, half[:, :], ALU.pow).then_inc(rstds, 1)

            def norm(h, par):
                g = 2 * h + par
                pool.wait_ge(S.lnp, 16 * g + 8 + START)
                pool.sem_inc(S.waits_alone, 1)
                V.tensor_scalar(rstd, mv[:, :, 1], EPS, 1.0, ALU.add, ALU.mult).then_inc(S.lnp_rstd, 1)
                pool.wait_ge(S.lnp_rstd, 6 * g + 1 + START)
                pool.sem_inc(S.waits_alone, 1)
                V.tensor_tensor(rstd, rstd, half[:, :], ALU.pow).then_inc(S.lnp_rstd, 1)
                pool.wait_ge(S.lnp_rstd, 6 * g + 2 + START)
                pool.sem_inc(S.waits_alone, 1)
                V.tensor_tensor(rstd2, rstd, rstd, ALU.mult).then_inc(S.lnp_rstd, 1)
                pool.wait_ge(S.lnp_rstd, 6 * g + 3 + START)
                pool.sem_inc(S.waits_alone, 1)
                V.tensor_tensor(rstd2, rstd2, mv[:, :, 1], ALU.mult).then_inc(S.lnp_rstd, 1)
                pool.wait_ge(S.lnp_rstd, 6 * g + 4 + START)
                pool.sem_inc(S.waits_alone, 1)
                V.tensor_scalar(rstd2, rstd2, EPS, 1.0, ALU.add, ALU.mult).then_inc(S.lnp_rstd, 1)
                pool.wait_ge(S.lnp_rstd, 6 * g + 5 + START)
                pool.sem_inc(S.waits_alone, 1)
                V.tensor_tensor(rstd2, rstd2, half[:, :], ALU.pow).then_inc(S.lnp_rstd, 1)

            def prep(h, par, follows):
                g = 2 * h + par
                pool.wait_ge(S.resid, 2 * g + 2 + START)
                pool.sem_inc(S.waits_alone, 1)
                pool.wait_ge(S.sent[1], 32 * g + START)
                pool.sem_inc(S.waits_alone, 1)
                V.tensor_copy(parts[:, :, 1, :], res).then_inc(S.mid, 1)
                pool.wait_ge(S.mid, 2 * g + 1 + START)
                pool.sem_inc(S.waits_alone, 1)
                V.tensor_tensor(parts[:, :, 2, :], res, parts[:, :, 1, :], ALU.subtract).then_inc(S.low, 1)
                pool.wait_ge(S.lin_y, 2 * g + 2 + START)
                pool.sem_inc(S.waits_alone, 1)
                pool.wait_ge(S.lin_sum, g + START)
                pool.sem_inc(S.waits_alone, 1)
                V.tensor_scalar(eb, Y32, 0.0, MASKED, ALU.min, ALU.max).then_inc(S.lin_min, 1)
                pool.wait_ge(S.lin_sum, g + 1 + START)
                pool.sem_inc(S.waits_alone, 1)
                pool.wait_ge(S.tm, 12 * g + 12 + START)
                pool.sem_inc(S.waits_alone, 1)
                V.tensor_scalar(kexp, kraw, 0.0, MASKED, ALU.min, ALU.max).then_inc(S.kmin, 1)
                pool.wait_ge(S.ol, 4 * (g - 1) + START)
                pool.sem_inc(S.waits_alone, 1)
                V.tensor_scalar(QF[par], Y32[:, 0, :], 1e-4, 1.0, ALU.add, ALU.mult).then_inc(S.lin_qk, 1)
                V.tensor_scalar(Y32[:, 1, :], Y32[:, 1, :], 1e-4, 1.0, ALU.add, ALU.mult).then_inc(S.lin_qk, 1)
                pool.wait_ge(S.high, 4 * g + 4 + START)
                pool.sem_inc(S.waits_alone, 1)
                pool.wait_ge(S.low, 2 * g + 1 + START)
                pool.sem_inc(S.waits_alone, 1)
                V.tensor_tensor(res[:, 0, :], QF[par], parts[:, 0, 0, :], ALU.subtract).then_inc(S.lin_res, 1)
                V.tensor_tensor(res[:, 1, :], Y32[:, 1, :], parts[:, 1, 0, :], ALU.subtract).then_inc(S.lin_res, 1)
                pool.wait_ge(S.lin_res, 2 * g + 2 + START)
                pool.sem_inc(S.waits_alone, 1)
                V.tensor_copy(parts[:, :, 1, :], res).then_inc(S.mid, 1)
                pool.wait_ge(S.mid, 2 * g + 2 + START)
                pool.sem_inc(S.waits_alone, 1)
                V.tensor_tensor(parts[:, :, 2, :], res, parts[:, :, 1, :], ALU.subtract).then_inc(S.low, 1)
                pool.wait_ge(S.kmin, g + 1 + START)
                pool.sem_inc(S.waits_alone, 1)
                V.tensor_scalar(kraw, kraw, 0.0, 1e-4, ALU.max, ALU.add).then_inc(S.kmax, 1)
                pool.wait_ge(S.kmax, g + 1 + START)
                pool.sem_inc(S.waits_alone, 1)
                pool.wait_ge(S.kexp, g + 1 + START)
                pool.sem_inc(S.waits_alone, 1)
                V.tensor_tensor(KST[par], kraw, kexp, ALU.add).then_inc(S.kst, 1)
                if par == 1:
                    pool.wait_ge(S.tm, 12 * g + START)
                    pool.sem_inc(S.waits_alone, 1)
                    pool.wait_ge(S.pv, 32 * h + START)
                    pool.sem_inc(S.waits_alone, 1)
                    V.tensor_copy(VT[:, :, :], VA[0][:, GT - 1, :, :]).then_inc(S.tailv, 1)

            def finish(h, par):
                g = 2 * h + par
                pool.wait_ge(S.x1, 4 * g + 4 + START)
                pool.sem_inc(S.waits_alone, 1)
                V.tensor_tensor(X[:, bass.ds(g * GT, GT), :], X1, XIN[par], ALU.add).then_inc(S.xsum, 1)
                rstd_of(S.lne, S.lne_rstd, g)

            def mx(h, par, follows, more):
                if follows:
                    finish(h - 1 + par, 1 - par)
                if more:
                    norm(h + par, 1 - par)

            attention_order(prep, nothing, nothing, mx, norm, finish, pool)
            pool_rest(pool)

        @block.scalar
        def _(act):
            V = nc.scalar
            act.wait_ge(S.loaded, n_load[0])
            act.wait_ge(S.wT, 1)
            for i in range(2):
                V.activation(wsqT[:, 4 * i:4 * i + 4, :].rearrange("p a b -> p (a b)"), ring[i][:, 0, :], ACT.Copy).then_inc(S.wTc, 1)
            act.wait_ge(S.wmixed, 1)
            V.activation(wmix[:, :, :], psT[:, 0:2, :], ACT.Copy).then_inc(S.actset, 1)
            V.activation(rw1[:, :], psY[:, 0:EX], ACT.Copy).then_inc(S.actset, 1)
            V.activation(bfm[:, :], psY[:, 16:20], ACT.Copy).then_inc(S.actset, 1)
            V.activation(l1w[:, 2:3], l1w[:, 0:1], ACT.Exp).then_inc(S.actset, 1)
            act.wait_ge(S.actset, 4)
            V.activation(l1w[:, 3:4], l1w[:, 2:3], ACT.Exp, scale=-1.0).then_inc(S.actset, 1)
            act.wait_ge(S.actset, 5)
            V.activation(bcol[:, 2:3], l1w[:, 2:3], ACT.Copy).then_inc(S.setup, 1)
            act.wait_ge(S.setup, SETUP)

            def prep(h, par, follows):
                g = 2 * h + par
                r = lambda k: ring[k % 2]
                act.wait_ge(S.turn_prep, 6 * g + 1 + START)
                act.wait_ge(S.xnT_out[1 - par], 16 * (h if par == 0 else h + 1) + START)
                V.activation(xnT, r(0)[:, 0, :], ACT.Copy).then_inc(S.xnT, 1)
                act.wait_ge(S.turn_prep, 6 * g + 2 + START)
                V.activation(xhT, r(1)[:, 0, :], ACT.Identity, scale=gb[:, 0:1], bias=gb[:, 1:2]).then_inc(S.xhT, 1)
                if follows:
                    minus_rows(h - 1 + par, 1 - par)
                act.wait_ge(S.turn_prep, 6 * g + 3 + START)
                act.wait_ge(S.sent[1], 32 * g + START)
                for i in range(2):
                    V.activation(parts[:, i, 0, :], r(2)[:, i, :], ACT.Identity, bias=bfm[:, i:i + 1]).then_inc(S.high, 1)
                act.wait_ge(S.rt0, 22 * g + 2 + START)
                V.activation(lg, lg, ACT.Exp).then_inc(S.rt0_exp, 1)

            def late_exp(h, par):
                g = 2 * h + par
                act.wait_ge(S.lin_min, g + 1 + START)
                V.activation(eb, eb, ACT.Exp).then_inc(S.lin_exp, 1)

            def late_high(h, par):
                g = 2 * h + par
                act.wait_ge(S.lin_qk, 2 * g + 2 + START)
                act.wait_ge(S.sent[0], 32 * (g + 1) + START)
                V.activation(parts[:, 0, 0, :], QF[par], ACT.Copy).then_inc(S.high, 1)
                V.activation(parts[:, 1, 0, :], Y32[:, 1, :], ACT.Copy).then_inc(S.high, 1)
                act.wait_ge(S.kmin, g + 1 + START)
                V.activation(kexp, kexp, ACT.Exp).then_inc(S.kexp, 1)

            def late(h, par):
                late_exp(h, par)
                late_high(h, par)

            def minus_rows(h, par):
                g = 2 * h + par
                act.wait_ge(S.mT_turn, g + 1 + START)
                act.wait_ge(S.mrow[1 - par], 48 * (h + par) + START)
                V.activation(MT[0:3 * H, :], psY[:, 256:512].bitcast(BF16)[0:3 * H, :], ACT.Copy).then_inc(S.mT, 1)

            def copy_attended(u):
                act.wait_ge(S.y, u + 1 + START)
                V.activation(AST, psT[:, 0:2, :], ACT.Copy).then_inc(S.ast, 1)

            def copy_hidden(h, par):
                g = 2 * h + par
                act.wait_ge(S.hT_turn, g + 1 + START)
                act.wait_ge(S.hT_out[1 - par], 16 * (h + par) + START)
                V.activation(hT, psT[:, :, :].rearrange("p a b -> p (a b)"), ACT.Identity, scale=gb[:, 2:3],
                             bias=gb[:, 3:4]).then_inc(S.hT, 1)

            def finish(h, par):
                copy_attended(GT * (2 * h + par) + GT - 1)
                copy_hidden(h, par)

            def mx(h, par, follows, more):
                if follows:
                    finish(h - 1 + par, 1 - par)
                if not more:
                    minus_rows(h, par)

            def attend(h, par, last):
                g = 2 * h + par
                for j in range(GT):
                    t = GT * g + j
                    for q in range(4):
                        if q == 3 and j > 0:
                            copy_attended(t - 1)
                        act.wait_ge(S.turn_attend, 24 * g + 6 * j + q + 3 + START)
                        act.wait_ge(S.pv, 4 * t + max(q - 1, 0) + START)
                        n = 256 if par == 0 and j == 0 else 512
                        V.activation(PB[q % 2].rearrange("p a b c -> p (a b c)")[:, 0:2 * n].rearrange("p (a n) -> p a n", a=2),
                                     ring[q % 2][:, :, 0:n], ACT.Exp, scale=RSQ).then_inc(S.exps, 1)
                    act.wait_ge(S.pv, 4 * t + 4 + START)
                    act.wait_ge(S.t1, t + START)
                    V.activation(OAs, psA[:, :, :], ACT.Copy).then_inc(S.oas, 1)
                    act.wait_ge(S.ol, t + 1 + START)
                    act.wait_ge(S.t2, t + START)
                    V.activation(OLs, psL[:, :, :], ACT.Copy).then_inc(S.ols, 1)
                    if j == 0 and not last:
                        late_exp(h + par, 1 - par)
                    if j == 2 and not last:
                        late_high(h + par, 1 - par)

            attention_order(prep, late, attend, mx, nothing, finish, act)
            act_rest(act)

        def layernorm(eng, steps, rstds, n, src, dst, free=None, value=None):
            V = nc.vector
            for j in range(GT):
                V.bn_stats(st6[:, j, :], src(j)).then_inc(steps, 1)
            eng.wait_ge(steps, 12 * n + 4 + START)
            eng.sem_inc(S.waits_alone, 1)
            for j in range(GT):
                V.bn_aggr(mv[:, j, :], st6[:, j, :]).then_inc(steps, 1)
            eng.wait_ge(rstds, 2 * n + 2 + START)
            if free is not None:
                eng.wait_ge(free, value)
            for j in range(GT):
                V.tensor_scalar(dst(j), src(j), mv[:, j, 0:1], rstd[:, j:j + 1], ALU.subtract, ALU.mult).then_inc(steps, 1)

        def route_start(eng, steps, read, g, logits, layer):
            V = nc.vector
            V.tensor_tensor(lg, logits, rb[:, layer, :].unsqueeze(1).to_broadcast([P, GT, EX]), ALU.add).then_inc(read, 1)
            eng.wait_ge(read, g + 1 + START)
            V.tensor_reduce(mx4, lg, AX_X, ALU.max).then_inc(steps, 1)
            eng.wait_ge(steps, 22 * g + 1 + START)
            V.tensor_tensor(lg, lg, mx4.unsqueeze(2).to_broadcast([P, GT, EX]), ALU.subtract).then_inc(steps, 1)

        def route_end(eng, steps, exps, g, layer, cw):
            V = nc.vector
            base = 22 * g + START
            eng.wait_ge(exps, g + 1 + START)
            V.tensor_reduce(mx4, lg, AX_X, ALU.add).then_inc(steps, 1)
            eng.wait_ge(steps, base + 3)
            V.reciprocal(mx4, mx4).then_inc(steps, 1)
            eng.wait_ge(steps, base + 4)
            V.tensor_tensor(lg, lg, mx4.unsqueeze(2).to_broadcast([P, GT, EX]), ALU.mult).then_inc(steps, 1)
            eng.wait_ge(steps, base + 5)
            eng.sem_inc(S.waits_alone, 1)
            for j in range(GT):
                V.max(t8[:, j, :], lg[:, j, :]).then_inc(steps, 1)
            eng.wait_ge(steps, base + 9)
            eng.sem_inc(S.waits_alone, 1)
            for j in range(GT):
                V.max_index(i8[:, j, :], t8[:, j, :], lg[:, j, :]).then_inc(steps, 1)
            eng.wait_ge(steps, base + 13)
            V.tensor_copy(idf, i8[:, :, 0:2]).then_inc(steps, 1)
            eng.wait_ge(steps, base + 14)
            for k in range(2):
                V.tensor_tensor(oh[:, k], iot[:, :].unsqueeze(1).to_broadcast([P, GT, EX]),
                                idf[:, :, k].unsqueeze(2).to_broadcast([P, GT, EX]), ALU.is_equal).then_inc(steps, 1)
            V.tensor_tensor(mx4, t8[:, :, 0], t8[:, :, 1], ALU.add).then_inc(steps, 1)
            eng.wait_ge(steps, base + 17)
            V.tensor_tensor(oh[:, 0], oh[:, 0], oh[:, 1], ALU.add).then_inc(steps, 1)
            V.tensor_scalar(mx4, mx4, 1e-9 * layer, None, ALU.add).then_inc(steps, 1)
            eng.wait_ge(steps, base + 19)
            V.reciprocal(mx4, mx4).then_inc(steps, 1)
            V.tensor_tensor(oh[:, 0], oh[:, 0], lg, ALU.mult).then_inc(steps, 1)
            eng.wait_ge(steps, base + 21)
            V.tensor_tensor(cw[:, bass.ds(g * GT, GT), 0:EX], oh[:, 0], mx4.unsqueeze(2).to_broadcast([P, GT, EX]), ALU.mult)\
                .then_inc(steps, 1)

        @block.vector
        def _(dve):
            V = nc.vector
            V.memset(psA[:, :, :], 0.0).then_inc(S.dveset, 1)
            V.memset(psL[:, :, :], 0.0).then_inc(S.dveset, 1)
            V.memset(eps_col[:, :], EPS).then_inc(S.dveset, 1)
            dve.wait_ge(S.loaded, n_load[0])
            for i, (a, o) in enumerate(((0, 0), (0, 1), (1, 0), (1, 1))):
                V.tensor_copy(wfm[:, i, :].rearrange("p (e h) -> p h e", e=E), h_e(wraw[a][:, o * D:o * D + D])).then_inc(S.dveset, 1)
                V.tensor_copy(btmp[0:1, i, :].rearrange("p (e h) -> p h e", e=E), h_e(braw[a][0:1, o * D:o * D + D])).then_inc(S.bperm, 1)
            for dst, src in ((wtm, wraw), (btm, braw)):
                V.tensor_copy(dst[:, 0, :], src[0][:, 2 * D:3 * D]).then_inc(S.dveset, 1)
                V.tensor_copy(dst[:, 1, :], src[1][:, 2 * D:3 * D]).then_inc(S.dveset, 1)
                V.tensor_copy(dst[:, 2, :].rearrange("p (e h) -> p h e", e=E), h_e(src[1][:, D:2 * D])).then_inc(S.dveset, 1)
            V.tensor_tensor(bcol[:, 2:3], bcol[:, 0:1], bcol[:, 1:2], ALU.add).then_inc(S.bsum, 1)
            dve.wait_ge(S.actset, 3)
            V.tensor_tensor(bc_row[:, :], psY[0:1, 32:32 + D], bo_row[0:1, :], ALU.add).then_inc(S.dveset, 1)
            dve.wait_ge(S.consts, N_CONSTS)
            V.tensor_reduce(bd[:, :], ident[:, :].rearrange("p (e h) -> p h e", e=E), AX_X, ALU.add).then_inc(S.dveset, 1)
            dve.wait_ge(S.dveset, 15)
            V.memset(st6[:, :, :], 0.0).then_inc(S.setup, 1)
            dve.wait_ge(S.setup, SETUP)

            heads = psT[:, :, :].rearrange("p a (b e) -> p (a b) e", e=32)

            def norm_stats(h, par):
                g = 2 * h + par
                dve.wait_ge(S.xin[par], 16 * (h + 1) + START)
                for j in range(GT):
                    V.bn_stats(st6[:, j, :], XIN[par][:, j, :]).then_inc(S.lnp, 1)
                dve.wait_ge(S.lnp, 16 * g + 4 + START)
                dve.sem_inc(S.waits_alone, 1)
                for j in range(GT):
                    V.bn_aggr(mv[:, j, :], st6[:, j, :]).then_inc(S.lnp, 1)

            def norm_apply(h, par):
                g = 2 * h + par
                dve.wait_ge(S.lnp_rstd, 6 * g + 6 + START)
                for j in range(GT):
                    V.tensor_scalar(XN[par][:, j, :], XIN[par][:, j, :], mv[:, j, 0:1], rstd[:, j:j + 1], ALU.subtract, ALU.mult)\
                        .then_inc(S.lnp, 1)
                dve.wait_ge(S.lnp, 16 * g + 12 + START)
                dve.wait_ge(S.turn_prep, 6 * (g - 1) + 2 + START)
                for j in range(GT):
                    V.tensor_scalar(XH[:, j, :], XN[par][:, j, :], rstd2[:, j:j + 1], None, ALU.mult).then_inc(S.lnp, 1)

            def norm(h, par):
                norm_stats(h, par)
                norm_apply(h, par)

            def attended_softmax(u):
                dve.wait_ge(S.t1, u + 1 + START)
                V.reciprocal(rec[:, 0, :], heads[:, :, E]).then_inc(S.rcp, 1)
                dve.wait_ge(S.rcp, 3 * u + 1 + START)
                dve.wait_ge(S.y, u + START)
                V.tensor_tensor(h_e(ATM[:, 0, :]), heads[:, :, 0:E], rec[:, 0, :].unsqueeze(2).to_broadcast([P, H, E]),
                                ALU.mult).then_inc(S.at, 1)

            def attended_linear(u):
                dve.wait_ge(S.t2, u + 1 + START)
                V.tensor_scalar(rec[:, 1, :], heads[:, :, E], 1e-6, None, ALU.add).then_inc(S.rcp, 1)
                dve.wait_ge(S.rcp, 3 * u + 2 + START)
                V.reciprocal(rec[:, 1, :], rec[:, 1, :]).then_inc(S.rcp, 1)
                dve.wait_ge(S.rcp, 3 * u + 3 + START)
                V.tensor_tensor(h_e(ATM[:, 1, :]), heads[:, :, 0:E], rec[:, 1, :].unsqueeze(2).to_broadcast([P, H, E]),
                                ALU.mult).then_inc(S.lt, 1)

            def add_mixed(g, par, j):
                dve.wait_ge(S.mix, GT * g + j + 1 + START)
                dve.wait_ge(S.hT_turn, g + START)
                V.tensor_tensor(X1[:, j, :], psT[:, 2, :], XN[par][:, j, :], ALU.add).then_inc(S.x1, 1)

            def hidden_stats(g):
                dve.wait_ge(S.x1, 4 * g + 4 + START)
                for j in range(GT):
                    V.bn_stats(st6[:, j, :], X1[:, j, :]).then_inc(S.lne, 1)
                dve.wait_ge(S.lne, 12 * g + 4 + START)
                dve.sem_inc(S.waits_alone, 1)
                for j in range(GT):
                    V.bn_aggr(mv[:, j, :], st6[:, j, :]).then_inc(S.lne, 1)

            def hidden_apply(g):
                dve.wait_ge(S.lne_rstd, 2 * g + 2 + START)
                dve.wait_ge(S.xsum, g + 1 + START)
                for j in range(GT):
                    V.tensor_scalar(HN[:, j, :], X1[:, j, :], mv[:, j, 0:1], rstd[:, j:j + 1], ALU.subtract, ALU.mult)\
                        .then_inc(S.lne, 1)

            def finish(h, par):
                g = 2 * h + par
                attended_softmax(GT * g + GT - 1)
                attended_linear(GT * g + GT - 1)
                add_mixed(g, par, GT - 1)
                hidden_stats(g)
                hidden_apply(g)

            def mx(h, par, follows, more):
                g = 2 * h + par
                for j in range(GT):
                    n = P if par == 0 and j == 0 else 2 * P
                    for q in range(4):
                        if follows and j == 0 and q == 0:
                            attended_softmax(GT * g - 1)
                        if follows and j == 0 and q == 1:
                            attended_linear(GT * g - 1)
                        if follows and j == 0 and q == 3:
                            add_mixed(g - 1, 1 - par, GT - 1)
                            hidden_stats(g - 1)
                        if follows and j == 1 and q == 0:
                            hidden_apply(g - 1)
                        if more and j == 2 and q == 0:
                            norm_stats(h + par, 1 - par)
                        if more and j == 3 and q == 0:
                            norm_apply(h + par, 1 - par)
                        dve.wait_ge(S.turn_max, 16 * g + 4 * j + q + 1 + START)
                        V.tensor_reduce(mmax[:, j, 4 * q:4 * q + 4].rearrange("p (a b) -> p a b", a=2),
                                        ring[q % 2][:, :, 0:2 * n].rearrange("p a (b n) -> p a b n", b=2), AX_X, ALU.max)\
                            .then_inc(S.mred, 1)
                dve.wait_ge(S.mred, 16 * g + 16 + START)
                dve.wait_ge(S.mT_turn, g + START)
                V.tensor_scalar(MS[:, :, 0:H], mmax, -1.0, None, ALU.mult).then_inc(S.mparts, 1)
                dve.wait_ge(S.mparts, 4 * g + 1 + START)
                V.scalar_tensor_tensor(out=mres, in0=mmax, scalar=-1.0, in1=MS[:, :, 0:H], op0=ALU.mult, op1=ALU.subtract)\
                    .then_inc(S.mparts, 1)
                dve.wait_ge(S.mparts, 4 * g + 2 + START)
                V.tensor_copy(MS[:, :, H:2 * H], mres).then_inc(S.mparts, 1)
                dve.wait_ge(S.mparts, 4 * g + 3 + START)
                V.tensor_tensor(MS[:, :, 2 * H:3 * H], mres, MS[:, :, H:2 * H], ALU.subtract).then_inc(S.mparts, 1)

            def prep(h, par, follows):
                g = 2 * h + par
                r = lambda k: ring[k % 2]
                dve.wait_ge(S.turn_prep, 6 * g + 2 + START)
                route_start(dve, S.rt0, S.logits, g, r(1)[:, 1, 0:GT * EX].rearrange("p (a b) -> p a b", a=GT), 0)
                dve.wait_ge(S.turn_prep, 6 * g + 3 + START)
                dve.wait_ge(S.low, 2 * g + START)
                for i in range(2):
                    dve.wait_ge(S.high, 4 * g + i + 1 + START)
                    V.scalar_tensor_tensor(out=res[:, i, :], in0=r(2)[:, i, :], scalar=bfm[:, i:i + 1], in1=parts[:, i, 0, :],
                                           op0=ALU.add, op1=ALU.subtract).then_inc(S.resid, 1)
                dve.wait_ge(S.turn_prep, 6 * g + 4 + START)
                for i in range(2):
                    V.tensor_scalar(Y32[:, i, :], r(3)[:, i, :], bfm[:, 2 + i:3 + i], (RSQ, 1.0)[i], ALU.add, ALU.mult)\
                        .then_inc(S.lin_y, 1)
                dve.wait_ge(S.pv, 16 * (g - 1) + START)
                dve.wait_ge(S.ol, 4 * (g - 1) + START)
                dve.wait_ge(S.kst, g + START)
                if par == 0:
                    dve.wait_ge(S.tailv, h + START)
                for j in range(GT):
                    dve.wait_ge(S.turn_prep, 6 * g + 5 + j // 2 + START)
                    src = r(4 + j // 2)[:, j % 2, 0:3 * D].rearrange("p (a n) -> p a n", a=3)
                    for i, dst in enumerate((VA[par][:, j, :, 0:E], VL[par][:, j, :, 0:E], h_e(kraw[:, j, :]))):
                        V.tensor_tensor(dst, h_e(src[:, i, :]), h_e(btm[:, i, :]), ALU.add).then_inc(S.tm, 1)

            def late_router(h, par):
                route_end(dve, S.rt0, S.rt0_exp, 2 * h + par, 0, cw0)

            def late_sum(h, par):
                g = 2 * h + par
                dve.wait_ge(S.lin_exp, g + 1 + START)
                V.scalar_tensor_tensor(out=Y32.rearrange("p a b -> p (a b)"), in0=Y32.rearrange("p a b -> p (a b)"), scalar=0.0,
                                       in1=eb.rearrange("p a b -> p (a b)"), op0=ALU.max, op1=ALU.add).then_inc(S.lin_sum, 1)

            def late(h, par):
                late_router(h, par)
                late_sum(h, par)

            def attend(h, par, last):
                g = 2 * h + par
                for j in range(GT):
                    t = GT * g + j
                    for i in range(2):
                        dve.wait_ge(S.turn_attend, 24 * g + 6 * j + i + 1 + START)
                        dve.wait_ge(S.ol, t + START)
                        V.tensor_tensor(AB[i], ring[i][:, :, :].rearrange("p a (b c) -> p (a b) c", c=P),
                                        tri[:, :].unsqueeze(1).to_broadcast([P, 8, P]), ALU.mult).then_inc(S.amask, 1)
                    n = 7 * h + GT * par + j
                    if not (par == 0 and j == 0):
                        if par == 0 and j == 1:
                            dve.wait_ge(S.su, n + START)
                            V.tensor_copy(SB[:, :, 0:E + 1], SU).then_inc(S.sb, 1)
                        else:
                            dve.wait_ge(S.sb, n - 1 + START)
                            dve.wait_ge(S.su, n + START)
                            V.tensor_tensor(SB[:, :, 0:E + 1], SB[:, :, 0:E + 1], SU, ALU.add).then_inc(S.sb, 1)
                    if j > 0:
                        attended_softmax(t - 1)
                        attended_linear(t - 1)
                    if j == 0 and not last:
                        late_router(h + par, 1 - par)
                    if j == 1 and not last:
                        late_sum(h + par, 1 - par)
                    if j > 0:
                        add_mixed(g, par, j - 1)
                    if not (par == 1 and j == GT - 1):
                        dve.wait_ge(S.state, n + 1 + START)
                        dve.wait_ge(S.sb, n + START)
                        V.tensor_tensor(SU, psY[:, 0:H * (E + 1)].rearrange("p (h e) -> p h e", h=H),
                                        bd[:, :].unsqueeze(2).to_broadcast([P, H, E + 1]), ALU.mult).then_inc(S.su, 1)

            attention_order(prep, late, attend, mx, norm, finish, dve)
            dve_rest(dve)

        @block.tensor
        def _(pe):
            T = nc.tensor
            pe.wait_ge(S.loaded, n_load[0])
            pe.wait_ge(S.consts, N_CONSTS)
            for i in range(8):
                m = T.transpose(ring[i // 4][:, 0, :].rearrange("p (a b) -> p a b", a=GT)[:, i % 4, :], wsq[:, i, :], ident[:, :])
            m.then_inc(S.wT, 1)
            T.transpose(psY[:, 0:EX], rw1r[:, :], ident[0:EX, 0:EX])
            pe.wait_ge(S.bperm, 4)
            for i in range(4):
                T.matmul(psY[:, 16 + i:17 + i], btmp[0:1, i, :], ones_row[0:1, 0:1], start=True, stop=True)
            pe.wait_ge(S.wTc, 2)
            pe.wait_ge(S.bsum, 1)
            T.matmul(psY[0:1, 32:32 + D], bcol[:, 2:3], wsq[:, 2, :], start=True, stop=True)
            T.matmul(psT[:, 0, :], wsqT[:, 0, :], wsq[:, 2, :], start=True, stop=True)
            T.matmul(psT[:, 1, :], wsqT[:, 1, :], wsq[:, 2, :], start=True, stop=True).then_inc(S.wmixed, 1)
            pe.wait_ge(S.actset, 5)
            pe.wait_ge(S.dveset, 15)
            T.transpose(psY[:, 0:EX], rw1r[:, :], ident[0:EX, 0:EX]).then_inc(S.setup, 1)
            pe.wait_ge(S.setup, SETUP)

            def tile(j):
                return slice(j * P, (j + 1) * P)

            def prep(h, par, follows):
                g = 2 * h + par
                r = lambda k: ring[k % 2]

                pe.wait_ge(S.mred, 16 * (g - 1) + 15 + START)
                pe.wait_ge(S.lnp, 16 * g + 12 + START)
                for j in range(GT):
                    m = T.transpose(r(0)[:, 0, tile(j)], XN[par][:, j, :], ident[:, :])
                m.then_inc(S.turn_prep, 1)
                pe.wait_ge(S.mred, 16 * (g - 1) + 16 + START)
                pe.wait_ge(S.lnp, 16 * g + 16 + START)
                for j in range(GT):
                    T.transpose(r(1)[:, 0, tile(j)], XH[:, j, :], ident[:, :])
                pe.wait_ge(S.xnT, g + 1 + START)
                for j in range(GT):
                    m = T.matmul(r(1)[:, 1, j * EX:(j + 1) * EX], xnT[:, tile(j)], rw0[:, :], start=True, stop=True)
                m.then_inc(S.turn_prep, 1)
                if follows:
                    minus_rows(h - 1 + par, 1 - par)
                pe.wait_ge(S.xhT, g + 1 + START)
                for k in range(2):
                    if k == 1:
                        pe.wait_ge(S.logits, g + 1 + START)
                    for i in range(2):
                        m = T.matmul(r(k)[:, i, :], wfm[:, 2 * k + i, :], xhT, start=True, stop=True)
                    m.then_inc(S.turn_prep, 1)
                for k in range(2):
                    if k == 0:
                        pe.wait_ge(S.resid, 2 * g + 2 + START)
                    else:
                        pe.wait_ge(S.lin_y, 2 * g + 2 + START)
                    for i in range(2):
                        m = T.matmul(r(k)[:, i, 0:3 * D], xhT[:, tile(2 * k + i)], wtm[:, :, :].rearrange("p a b -> p (a b)"),
                                     start=True, stop=True)
                    m.then_inc(S.turn_prep, 1)

            def scores(j, par, q, mask, rows, by_key):
                for a in range(2):
                    first = par == 0 and j == 0
                    bank = ring[q % 2][:, a, :]
                    if first:
                        T.matmul(bank[:, 0:2 * P].rearrange("p (b n) -> p b n", b=2), identb[:, :], mask[:, :, 1, :], start=True, stop=True)
                    else:
                        T.matmul(bank, identb[:, :], mask[:, :, :, :].rearrange("p a b c -> p (a b c)"), start=True, stop=True)
                for a in range(2):
                    for b in range(2):
                        hd = 4 * q + 2 * a + b
                        own = KS[par][0:rows, hd, tile(j)]
                        before = KS[par][0:rows, hd, tile(j - 1)] if j > 0 else KT[0:rows, hd, :]
                        blocks = [own] if first else [before, own]
                        for n, keys in enumerate(blocks):
                            c = (len(blocks) * b + n) * P
                            query = QS[par][0:rows, hd, tile(j)]
                            lhsT, rhs = (keys, query) if by_key else (query, keys)
                            m = T.matmul(ring[q % 2][:, a, c:c + P], lhsT, rhs, start=False, stop=True,
                                         skip_group_check=True)
                return m

            def hidden_turn(g):
                pe.wait_ge(S.lne, 12 * g + 12 + START)
                for j in range(GT):
                    m = T.transpose(psT[:, j, :], HN[:, j, :], ident[:, :])
                m.then_inc(S.hT_turn, 1)

            def minus_rows(h, par):
                g = 2 * h + par
                pe.wait_ge(S.mparts, 4 * g + 4 + START)
                pe.wait_ge(S.su, 7 * h + GT * par + START)
                pe.wait_ge(S.mT, g + START)
                pe.sem_inc(S.waits_alone, 1)
                for j in range(GT):
                    m = T.transpose(psY[:, 256:512].bitcast(BF16)[0:3 * H, tile(j)], MS[:, j, :], identb[:, :])
                m.then_inc(S.mT_turn, 1)

            def finish_part(u, g, part):
                if part == 0:
                    pe.wait_ge(S.oas, u + 1 + START)
                    pe.wait_ge(S.x1, u + START)
                    pe.wait_ge(S.hT, g + START)
                    for a in range(4):
                        m = T.transpose(psT[:, a, :], OAs[:, a, :], ident[:, :])
                    m.then_inc(S.t1, 1)
                elif part == 1:
                    pe.wait_ge(S.ols, u + 1 + START)
                    pe.wait_ge(S.at, u + 1 + START)
                    for a in range(4):
                        m = T.transpose(psT[:, a, :], OLs[:, a, :], ident[:, :])
                    m.then_inc(S.t2, 1)
                elif part == 2:
                    pe.wait_ge(S.lt, u + 1 + START)
                    for a in range(2):
                        m = T.transpose(psT[:, a, :], ATM[:, a, :], ident[:, :])
                    m.then_inc(S.y, 1)
                else:
                    pe.wait_ge(S.ast, u + 1 + START)
                    T.matmul(psT[:, 2, :], AST[:, 0, :], wmix[:, 0, :], start=True, stop=False)
                    T.matmul(psT[:, 2, :], AST[:, 1, :], wmix[:, 1, :], start=False, stop=False)
                    T.matmul(psT[:, 2, :], ones_row[:, :], bc_row[:, :], start=False, stop=True).then_inc(S.mix, 1)

            def finish(h, par):
                g = 2 * h + par
                for part in range(4):
                    finish_part(GT * g + GT - 1, g, part)
                hidden_turn(g)

            def mx(h, par, follows, more):
                g = 2 * h + par
                pe.wait_ge(S.stack[0][par], 144 * (h + 1) + START)
                if par == 1:
                    pe.wait_ge(S.tails, 16 * (h + 1) + START)
                for j in range(GT):
                    for q in range(4):
                        if j == 0 and q < 2:
                            pe.wait_ge(S.tm, 12 * g + 6 * (q + 1) + START)
                            pe.wait_ge(S.exps, 16 * g + START)
                        else:
                            pe.wait_ge(S.mred, 16 * g + 4 * j + q - 1 + START)
                        scores(j, par, q, mqry, QK, False).then_inc(S.turn_max, 1)
                        if follows and j == 0:
                            finish_part(GT * g - 1, g - 1, q)
                    if follows and j == 1:
                        hidden_turn(g - 1)
                if not more:
                    minus_rows(h, par)

            def attend(h, par, last):
                g = 2 * h + par

                def values(j, q):
                    t = GT * g + j
                    pe.wait_ge(S.exps, 4 * t + q + 1 + START)
                    if q == 0:
                        pe.wait_ge(S.oas, t + START)
                        if j == 0 and par == 1:
                            pe.wait_ge(S.tailv, h + 1 + START)
                    first = par == 0 and j == 0
                    for a in range(4):
                        hd = 4 * q + a
                        before = VA[par][:, j - 1, hd, :] if j > 0 else VT[:, hd, :]
                        blocks = [VA[par][:, j, hd, :]] if first else [before, VA[par][:, j, hd, :]]
                        flat = PB[q % 2].rearrange("p a b c -> p (a b c)")
                        for n, v in enumerate(blocks):
                            c = (len(blocks) * a + n) * P
                            m = T.matmul(psA[32 * a:32 * a + E + 1, q, :], v, flat[:, c:c + P], start=(n == 0), stop=(n == len(blocks) - 1),
                                         skip_group_check=True)
                    m.then_inc(S.pv, 1)

                pe.wait_ge(S.stack[1][par], 144 * (h + 1) + START)
                pe.wait_ge(S.mrow[par], 48 * (h + 1) + START)
                for j in range(GT):
                    t = GT * g + j
                    for i in range(2):
                        if j > 0:
                            pe.wait_ge(S.exps, 16 * g + 4 * j + i - 1 + START)
                        elif last:
                            pe.wait_ge(S.mred, 16 * g + 15 + i + START)
                        else:
                            pe.wait_ge(S.tm, 12 * (g + 1) + 6 * (i + 1) + START)
                        for k in range(8):
                            hd = 8 * i + k
                            m = T.matmul(ring[i][:, k // 4, (k % 4) * P:(k % 4 + 1) * P], KS[par][LR:LR + QK, hd, tile(j)],
                                         QS[par][LR:LR + QK, hd, tile(j)], start=True, stop=True)
                        m.then_inc(S.turn_attend, 1)
                    if j > 0:
                        finish_part(t - 1, g, 0)
                    for q in range(4):
                        if q < 2:
                            pe.wait_ge(S.amask, 8 * g + 2 * j + q + 1 + START)
                        else:
                            pe.wait_ge(S.exps, 16 * g + 4 * j + q - 1 + START)
                        scores(j, par, q, mkey, QKM, True).then_inc(S.turn_attend, 1)
                        if q > 0:
                            values(j, q - 1)
                            if j > 0:
                                finish_part(t - 1, g, q)
                    values(j, 3)
                    n = 7 * h + GT * par + j
                    if not (par == 1 and j == GT - 1):
                        pe.wait_ge(S.kst, g + 1 + START)
                        pe.wait_ge(S.su, n + START)
                        pe.wait_ge(S.mT, g + 1 + START)
                        T.matmul(psY[:, 0:H * (E + 1)], KST[par][:, j, :], VL[par][:, j, :, :].rearrange("p h e -> p (h e)"),
                                 start=True, stop=True).then_inc(S.state, 1)
                    pe.wait_ge(S.lin_qk, 2 * g + 1 + START)
                    pe.wait_ge(S.ols, t + START)
                    pe.wait_ge(S.sb, n + START)
                    first = par == 0 and j == 0
                    for q in range(4):
                        if not first:
                            T.matmul(psL[:, q, :], SB[:, 4 * q:4 * q + 4, :].rearrange("p h e -> p (h e)"), QF[par][:, tile(j)],
                                     start=True, stop=True)
                        for a in range(4):
                            hd = 4 * q + a
                            m = T.matmul(psL[32 * a:32 * a + E + 1, q, :], VL[par][:, j, hd, :], AB[hd // 8][:, hd % 8, :],
                                         start=first, stop=True, skip_group_check=True)
                    m.then_inc(S.ol, 1)

            attention_order(prep, nothing, attend, mx, nothing, finish, pe)
            pe_rest(pe)


_OUTS = [((8, 1024, 128), 'float32')]


def kernel(**inputs):
    import numpy as _np
    import concourse.bacc as _bacc
    from concourse import mybir as _mybir
    from concourse.bass_utils import run_bass_kernel_spmd as _run

    nc = _bacc.Bacc("TRN2", target_bir_lowering=False, num_devices=1)
    arrays, I = {}, {}
    for name in inputs:
        a = _np.ascontiguousarray(inputs[name])
        arrays[f"in_{name}_dram"] = a
        I[name] = nc.dram_tensor(f"in_{name}_dram", a.shape, _mybir.dt.from_np(a.dtype), kind="ExternalInput").ap()
    shape, dtype = _OUTS[0]
    out = nc.dram_tensor("out_0_dram", shape, _mybir.dt.from_np(_np.dtype(dtype)), kind="ExternalOutput").ap()
    build(nc, I, out)
    r = _run(nc, [arrays], core_ids=[0])
    return r.results[0]["out_0_dram"]
```

```python
from contextlib import ExitStack

import concourse.bass as bass
from concourse import mybir

ALU = mybir.AluOpType
ACT = mybir.ActivationFunctionType
F32 = mybir.dt.float32
BF16 = mybir.dt.bfloat16
U32 = mybir.dt.uint32
AX_X = mybir.AxisListType.X

P = 128
GT = 4
GC = GT * P
EPS = 1e-5
MASKED = -1e30
ARENA = 17628


def build(nc, I, out):
    B, L, D = I["L0_attn_x"].shape
    H = I["L1_attn_w"].shape[0]
    E = D // H
    TILES = B * L // P
    NG = TILES // GT
    EX = I["L0_ffn_w1"].shape[0]
    F0 = I["L0_ffn_w1"].shape[2]
    F1 = I["L1_ffn_w1"].shape[2]
    FM = I["L0_attn_W1"].shape[1]
    C0, C1, CM = F0 // P, F1 // P, FM // P
    assert D == P and L == 2 * GC and EX == 8 and H == 16 and E == 8
    QK = 6 * E
    QKM = QK + 3
    LR = 64
    RSQ = float(E) ** -0.5

    x_d = I["L0_attn_x"].rearrange("b (g j p) d -> (b g) p j d", j=GT, p=P)
    out_d = out.rearrange("b (g j p) d -> (b g) p j d", j=GT, p=P)
    xnT_d = nc.dram_tensor("xnT_d", [NG, P, GC], F32, kind="Internal").ap()
    hT_d = nc.dram_tensor("hT_d", [NG, P, GC], F32, kind="Internal").ap()
    yT_d = nc.dram_tensor("yT_d", [NG, P, GC], F32, kind="Internal").ap()
    part_d = [[nc.dram_tensor(f"part_d{i}{j}", [3, P, GC], BF16, kind="Internal").ap() for j in range(4)] for i in range(2)]

    with ExitStack() as ctx:
        def sb(name, shape, dt=F32):
            return ctx.enter_context(nc.sbuf_tensor(name, shape, dt))

        def sem(name):
            return ctx.enter_context(nc.semaphore(name))

        X = sb("X", [P, TILES, D])
        cw0 = sb("cw0", [P, TILES + GT, EX + 1])
        cw1 = sb("cw1", [P, TILES, EX])
        ident = sb("ident", [P, P])
        identb = sb("identb", [P, P], BF16)
        ones_row = sb("ones_row", [1, P])
        half = sb("half", [P, GT])
        iot = sb("iot", [P, EX])
        iou = sb("iou", [P, EX], U32)

        wfm = sb("wfm", [P, 4, D])
        wtm = sb("wtm", [P, 3, D])
        btm = sb("btm", [P, 3, D])
        bfm = sb("bfm", [P, 4])
        gb = sb("gb", [P, 4])
        wsqT = sb("wsqT", [P, 8, D])
        wmix = sb("wmix", [P, 2, D])
        bcol = sb("bcol", [P, 3])
        bc_row = sb("bc_row", [1, D])
        wob_row = sb("wob_row", [1, D])
        rw0 = sb("rw0", [P, EX])
        rb = sb("rb", [P, 2, EX])
        rw1r = sb("rw1r", [EX, D])
        rw1 = sb("rw1", [P, EX])
        W1 = sb("W1", [P, CM, P])
        W2 = sb("W2", [P, CM, D])
        b1m = sb("b1m", [P, CM])
        b2x = sb("b2x", [EX + 1, D])
        fb1 = sb("fb1", [P, EX, C0])
        l1b = sb("l1b", [P, 4])
        l1m = sb("l1m", [P, 4])
        l1w = sb("l1w", [P, 4])

        mkey = sb("mkey", [P, 2, 2, P], BF16)
        mqry = sb("mqry", [P, 2, 2, P], BF16)
        tri = sb("tri", [P, P])
        bd = sb("bd", [P, H])
        cen = sb("cen", [P, P])
        avg = sb("avg", [P, P])

        big = [sb(f"big{i}", [P, H * GC // 2]) for i in range(4)]
        QS, KS = ([b_[:, :].bitcast(BF16).rearrange("p (h t) -> p h t", h=H) for b_ in big[2 * i:2 * i + 2]] for i in range(2))
        KT = sb("KT", [QKM, H, P], BF16)
        VA = [sb(f"VA{i}", [P, GT, H, E + 1]) for i in range(2)]
        VL = [sb(f"VL{i}", [P, GT, H, E + 1]) for i in range(2)]
        VT = sb("VT", [P, H, E + 1])
        SB = sb("SB", [P, H, 32])
        st6 = sb("st6", [P, GT, 6])
        mv = sb("mv", [P, GT, 2])
        mvh = sb("mvh", [P, GT, 2])
        rstdh = sb("rstdh", [P, GT])[:, :]
        rstd = sb("rstd", [P, GT])[:, :]
        rstd2 = sb("rstd2", [P, GT])[:, :]
        lg = sb("lg", [P, 2 * GT, EX])[:, :, :]
        mx4 = sb("mx4", [P, 2 * GT])[:, :]
        t8 = sb("t8", [P, 2 * GT, EX])
        i8 = sb("i8", [P, 2 * GT, EX], U32)
        idf = sb("idf", [P, 2 * GT, 2])[:, :, :]
        oh = sb("oh", [P, 2, 2 * GT, EX])
        eps_col = sb("eps_col", [P, 1])
        arena = sb("arena", [P, ARENA])
        used = [0]

        def carve(*shape, dt=F32):
            n = 1
            for d in shape:
                n *= d
            w = n if dt == F32 else (n + 1) // 2
            a = arena[:, used[0]:used[0] + w]
            used[0] += w
            assert used[0] <= ARENA, used[0]
            if dt != F32:
                a = a.bitcast(dt)
            if len(shape) == 2:
                a = a.rearrange("p (a b) -> p a b", a=shape[0])
            if len(shape) == 3:
                a = a.rearrange("p (a b c) -> p a b c", a=shape[0], b=shape[1])
            return a

        wraw = [carve(3 * D) for _ in range(2)]
        braw = [carve(3 * D) for _ in range(2)]
        wsq = carve(8, D)
        idv = carve(P)
        btmp = carve(4, D)
        bo_row = carve(D)

        used[0] = 0
        XIN = [carve(GT, P) for _ in range(2)]
        XN = [carve(GT, P) for _ in range(2)]
        XH = carve(GT, P)
        X1 = carve(GT, P)
        HN = X1
        xnT = carve(GC)
        xhT = carve(GC)
        hT = carve(GC)
        parts = carve(2, 3, GC, dt=BF16)
        res = carve(2, GC)
        Y32 = carve(2, GC)
        QF = [carve(GC) for _ in range(2)]
        kraw = carve(GT, P)
        eb = carve(2, GC)
        kexp = eb[:, 0, :].rearrange("p (j f) -> p j f", j=GT)
        KST = [carve(GT, P) for _ in range(2)]
        PB = [carve(4, 2, P) for _ in range(2)]
        AB = [carve(8, P) for _ in range(2)]
        OAs = xhT.rearrange("p (j f) -> p j f", j=GT)
        OLs = carve(GT, P)
        ATM = carve(2, P)
        AST = carve(2, P)
        rec = carve(2, H)
        SU = carve(H, E + 1)
        mmax = carve(GT, H)
        mres = carve(GT, H)
        MS = carve(GT, 3 * H, dt=BF16)
        MT = carve(GC, dt=BF16)

        used[0] = 0
        YN = [carve(GT, P) for _ in range(2)]
        xT = carve(L + 4)
        DF = carve(2, GC)
        MX = [big[1][:, i * 4 * GC:(i + 1) * 4 * GC].rearrange("p (c t) -> p c t", c=4) for i in range(2)]
        SG = carve(2, GC)
        KK = carve(2, GC)
        KV = carve(GC)
        ACC = carve(2, GC)
        WK = carve(GC)
        RW = carve(GC)
        SQ = carve(GC)
        CS = carve(2, GC)
        RS = carve(2, GC)
        OT = carve(2, GC)
        fx = [[carve(GC) for _ in range(2)] for _ in range(2)]
        cwg = carve(GT, EX + 1)
        cwT = carve(GC)
        assert used[0] <= ARENA, used

        ring = [ctx.enter_context(nc.psum_tensor(f"ring{i}", [P, 2, GC], F32)) for i in range(2)]
        psA = ctx.enter_context(nc.psum_tensor("psA", [P, GT, P], F32))
        psL = ctx.enter_context(nc.psum_tensor("psL", [P, GT, P], F32))
        psT = ctx.enter_context(nc.psum_tensor("psT", [P, GT, P], F32))
        psY = ctx.enter_context(nc.psum_tensor("psY", [P, GC], F32))

        SETUP = 5
        N_CONSTS = 34

        START = 64
        counters = []

        def counter(name):
            counters.append(sem(name))
            return counters[-1]

        class S:
            amask = counter("amask")
            ast = counter("ast")
            at = counter("at")
            cen = counter("cen")
            cs = counter("cs")
            cwT = counter("cwT")
            cwT_turn = counter("cwT_turn")
            cwg = counter("cwg")
            diff = counter("diff")
            exps = counter("exps")
            grkv = counter("grkv")
            hT = counter("hT")
            hT_turn = counter("hT_turn")
            high = counter("high")
            kexp = counter("kexp")
            kk = counter("kk")
            kmax = counter("kmax")
            kmin = counter("kmin")
            kst = counter("kst")
            kv = counter("kv")
            lin_exp = counter("lin_exp")
            lin_min = counter("lin_min")
            lin_qk = counter("lin_qk")
            lin_res = counter("lin_res")
            lin_sum = counter("lin_sum")
            lin_y = counter("lin_y")
            lnc = counter("lnc")
            lnc_rstd = counter("lnc_rstd")
            lne = counter("lne")
            lne_rstd = counter("lne_rstd")
            lnp = counter("lnp")
            lnp_rstd = counter("lnp_rstd")
            lnv = counter("lnv")
            logit_turn = counter("logit_turn")
            logits = counter("logits")
            logits1 = counter("logits1")
            low = counter("low")
            lt = counter("lt")
            mT = counter("mT")
            mT_turn = counter("mT_turn")
            mid = counter("mid")
            mix = counter("mix")
            mixed = counter("mixed")
            mo = counter("mo")
            mparts = counter("mparts")
            mred = counter("mred")
            oas = counter("oas")
            ol_half = counter("ol_half")
            ol = counter("ol")
            ols = counter("ols")
            ot = counter("ot")
            pv = counter("pv")
            rcp = counter("rcp")
            resid = counter("resid")
            rs = counter("rs")
            rt0 = counter("rt0")
            rt0_exp = counter("rt0_exp")
            rt1 = counter("rt1")
            rt1_exp = counter("rt1_exp")
            rw = counter("rw")
            sb = counter("sb")
            scan = counter("scan")
            sg = counter("sg")
            sq = counter("sq")
            state = counter("state")
            su = counter("su")
            t1 = counter("t1")
            t2 = counter("t2")
            tails = counter("tails")
            tailv = counter("tailv")
            tm = counter("tm")
            turn_attend = counter("turn_attend")
            turn_max = counter("turn_max")
            turn_prep = counter("turn_prep")
            var = counter("var")
            wkv = counter("wkv")
            x1 = counter("x1")
            xT = counter("xT")
            xT0 = counter("xT0")
            xT_turn = counter("xT_turn")
            xhT = counter("xhT")
            xnT = counter("xnT")
            xo = counter("xo")
            xsum = counter("xsum")
            y = counter("y")
            yT_out = counter("yT_out")
            facc = [counter("facc0"), counter("facc1")]
            fact = [counter("fact0"), counter("fact1")]
            fdown = [counter("fdown0"), counter("fdown1")]
            fup = [counter("fup0"), counter("fup1")]
            hT_out = [counter("hT_out0"), counter("hT_out1")]
            mrow = [counter("mrow0"), counter("mrow1")]
            sent = [counter("sent0"), counter("sent1")]
            xin = [counter("xin0"), counter("xin1")]
            xnT_out = [counter("xnT_out0"), counter("xnT_out1")]
            fx = [[counter("fx00"), counter("fx01")], [counter("fx10"), counter("fx11")]]
            stack = [[counter("stack00"), counter("stack01")], [counter("stack10"), counter("stack11")]]
            loaded = sem("loaded")
            consts = sem("consts")
            wT = sem("wT")
            wTc = sem("wTc")
            bperm = sem("bperm")
            bsum = sem("bsum")
            wmixed = sem("wmixed")
            actset = sem("actset")
            dveset = sem("dveset")
            setup = sem("setup")
            out = sem("out")
            waits_alone = sem("waits_alone")
            ffnw = [sem("ffnw0"), sem("ffnw1")]

        def h_e(ap):
            return ap.rearrange("p (h e) -> p h e", e=E)

        N2 = NG // 2

        def attention_order(prep, late, attend, mx, norm, finish, eng):
            norm(0, 0)
            prep(0, 0)
            late(0, 0)
            mx(0, 0, False, True)
            with eng.Fori(0, N2 - 1) as b:
                for par in range(2):
                    attend(b, par, False)
                    mx(b + par, 1 - par, True, True)
            attend(N2 - 1, 0, False)
            mx(N2 - 1, 1, True, False)
            attend(N2 - 1, 1, True)
            finish(N2 - 1, 1)

        w_up = [big[0][:, 0:EX * F0].rearrange("p (e f) -> p e f", e=EX), big[2][:, :].rearrange("p (e f) -> p e f", e=EX)]
        w_dn = [big[0][:, EX * F0:2 * EX * F0].rearrange("p (e c d) -> p e c d", e=EX, c=C0),
                big[3][:, :].rearrange("p (e c d) -> p e c d", e=EX, c=C1)]
        HS = [big[1][:, i * 4 * GC:(i + 1) * 4 * GC].rearrange("p (c t) -> p c t", c=4) for i in range(2)]
        psO = [psA, psL]
        UNITS = [[("mlp", CM)] + [(e, C0) for e in range(EX)], [(e, C1) for e in range(EX)]]
        TURNS_F = [sum(c for _, c in u) // 2 for u in UNITS]

        def unit_turns(layer, n):
            first = sum(c for _, c in UNITS[layer][:n]) // 2
            return first, UNITS[layer][n][1] // 2

        def ffn_sp(sp, layer):
            features_d = xnT_d if layer == 0 else yT_d
            if layer == 0:
                for q in range(2):
                    sp.wait_ge(S.xnT_out[q], 16 * N2 + START)
                    sp.sem_inc(S.waits_alone, 1)
                    sp.wait_ge(S.hT_out[q], 16 * N2 + START)
                    sp.sem_inc(S.waits_alone, 1)
            else:
                sp.wait_ge(S.yT_out, 16 * NG + START)
                sp.sem_inc(S.waits_alone, 1)

            def load(g, par, used_units):
                sp.wait_ge(S.fdown[layer], used_units + START)
                sp.sem_inc(S.waits_alone, 1)
                sp.dma_start(fx[0][par], features_d[g]).then_inc(S.fx[layer][par], 16)
                if layer == 0:
                    sp.dma_start(fx[1][par], hT_d[g]).then_inc(S.fx[layer][par], 16)

            def store(g):
                sp.wait_ge(S.facc[1], 32 * (g + 1) + START)
                sp.sem_inc(S.waits_alone, 1)
                sp.dma_start(out_d[g], X[:, bass.ds(g * GT, GT), :]).then_inc(S.out, 16)

            nu = len(UNITS[layer])
            load(0, 0, 0)
            with sp.Fori(0, N2 - 1) as b:
                load(2 * b + 1, 1, nu * 2 * b)
                load(2 * b + 2, 0, nu * (2 * b + 1))
                if layer == 1:
                    store(2 * b)
                    store(2 * b + 1)
            load(NG - 1, 1, nu * (NG - 2))
            if layer == 0:
                sp.dma_start(w_up[1], I["L1_ffn_w1"].rearrange("e d f -> d e f")).then_inc(S.ffnw[1], 16)
                sp.dma_start(w_dn[1], I["L1_ffn_w2"].rearrange("e (c f) d -> f e c d", c=C1)).then_inc(S.ffnw[1], 16)
            else:
                store(NG - 2)
                store(NG - 1)
                sp.wait_ge(S.out, 16 * NG)

        def ffn_pe(pe, layer):
            T = nc.tensor
            units, nt = UNITS[layer], TURNS_F[layer]
            nu = len(units)
            pe.wait_ge(S.ffnw[layer], 32)

            def up(g, par, n):
                e, chunks = units[n]
                first, turns = unit_turns(layer, n)
                for i in range(turns):
                    k = first + i
                    slot = (nt * par + k) % 2
                    pe.wait_ge(S.fact[layer], 2 * (nt * g + k - 1) + START)
                    for c in range(2):
                        w = W1[:, 2 * i + c, :] if e == "mlp" else w_up[layer][:, e, (2 * i + c) * P:(2 * i + c + 1) * P]
                        m = T.matmul(ring[slot][:, c, :], w, fx[1 if e == "mlp" else 0][par], start=True, stop=True)
                    m.then_inc(S.fup[layer], 1)

            def down(g, par, n):
                e, chunks = units[n]
                first, turns = unit_turns(layer, n)
                o = (nu * par + n)
                hs = HS[o % 2]
                pe.wait_ge(S.fact[layer], 2 * (nt * g + first + turns) + START)
                pe.wait_ge(S.facc[layer], facc_at(layer, g, n - 2) + START)
                for j in range(GT):
                    for c in range(chunks):
                        w = W2[:, c, :] if e == "mlp" else w_dn[layer][:, e, c, :]
                        last = c == chunks - 1 and e != "mlp"
                        m = T.matmul(psO[o % 2][:, j, :], hs[:, c, j * P:(j + 1) * P], w, start=(c == 0), stop=last)
                    if e == "mlp":
                        m = T.matmul(psO[o % 2][:, j, :], cwT[0:EX + 1, j * P:(j + 1) * P], b2x[:, :], start=False, stop=True)
                m.then_inc(S.fdown[layer], 1)

            def group(b, par, follows):
                g = 2 * b + par
                pe.wait_ge(S.fx[layer][par], (32 if layer == 0 else 16) * (b + 1) + START)
                for n in range(nu):
                    up(g, par, n)
                    if n == 0 and follows:
                        down(g - 1, 1 - par, nu - 1)
                    if n == 0 and layer == 0:
                        pe.wait_ge(S.cwg, g + 1 + START)
                        for j in range(GT):
                            m = T.transpose(psT[0:EX + 1, j, :], cwg[:, j, :], ident[:, :])
                        m.then_inc(S.cwT_turn, 1)
                    if n == 1 and layer == 0:
                        pe.wait_ge(S.cwT, g + 1 + START)
                    if n > 0:
                        down(g, par, n - 1)

            group(0, 0, False)
            group(0, 1, True)
            with pe.Fori(1, N2) as b:
                group(b, 0, True)
                group(b, 1, True)
            down(NG - 1, 1, nu - 1)

        def facc_at(layer, g, n):
            per = 33 if layer == 0 else 32
            if n < 0:
                return per * g + 4 * (n + 1)
            return per * g + (4 * n + 1 if layer == 0 else 4 * n + 4)

        def ffn_act(act, layer):
            V = nc.scalar
            units, nt = UNITS[layer], TURNS_F[layer]
            nu = len(units)
            func = ACT.Relu if layer == 0 else ACT.Gelu
            act.wait_ge(S.ffnw[layer], 32)
            with act.Fori(0, N2) as b:
                for par in range(2):
                    g = 2 * b + par
                    for n, (e, chunks) in enumerate(units):
                        if n == 1 and layer == 0:
                            act.wait_ge(S.cwT_turn, g + 1 + START)
                            act.wait_ge(S.fdown[0], 9 * g + START)
                            V.activation(cwT[0:EX + 1, :], psT[0:EX + 1, :, :].rearrange("p a b -> p (a b)"), ACT.Copy).then_inc(S.cwT, 1)
                        first, turns = unit_turns(layer, n)
                        hs = HS[(nu * par + n) % 2]
                        act.wait_ge(S.fdown[layer], nu * g + n - 1 + START)
                        for i in range(turns):
                            k = first + i
                            slot = (nt * par + k) % 2
                            act.wait_ge(S.fup[layer], nt * g + k + 1 + START)
                            for c in range(2):
                                if layer == 0:
                                    bias = b1m[:, 2 * i + c:2 * i + c + 1] if e == "mlp" else fb1[:, e, 2 * i + c:2 * i + c + 1]
                                    f = ACT.Gelu if e == "mlp" else func
                                    V.activation(hs[:, 2 * i + c, :], ring[slot][:, c, :], f, bias=bias).then_inc(S.fact[0], 1)
                                else:
                                    V.activation(hs[:, 2 * i + c, :], ring[slot][:, c, :], func).then_inc(S.fact[1], 1)

        def ffn_dve(dve, layer):
            V = nc.vector
            units = UNITS[layer]
            nu = len(units)
            cw = (cw0, cw1)[layer]
            if layer == 0:
                dve.wait_ge(S.rt0, 22 * NG + START)
                V.tensor_copy(cwg, cw0[:, 0:GT, :]).then_inc(S.cwg, 1)
            with dve.Fori(0, N2) as b:
                for par in range(2):
                    g = 2 * b + par
                    for n, (e, chunks) in enumerate(units):
                        o = psO[(nu * par + n) % 2]
                        if layer == 0 and n == nu - 1:
                            dve.wait_ge(S.cwT_turn, g + 1 + START)
                            V.tensor_copy(cwg, cw0[:, bass.ds((g + 1) * GT, GT), :]).then_inc(S.cwg, 1)
                        dve.wait_ge(S.fdown[layer], nu * g + n + 1 + START)
                        dve.wait_ge(S.facc[layer], facc_at(layer, g, n - 1) + START)
                        if e == "mlp":
                            xg = X[:, bass.ds(g * GT, GT), :]
                            V.tensor_tensor(xg, o[:, :, :], xg, ALU.add).then_inc(S.facc[0], 1)
                            continue
                        for j in range(GT):
                            xt = X[:, bass.ds(g * GT + j, 1), :].rearrange("p a d -> p (a d)")
                            V.scalar_tensor_tensor(out=xt, in0=o[:, j, :], scalar=cw[:, bass.ds(g * GT + j, 1), e], in1=xt,
                                                   op0=ALU.mult, op1=ALU.add).then_inc(S.facc[layer], 1)

        psAf = psA[:, :, :].rearrange("p a b -> p (a b)")
        psLf = psL[:, :, :].rearrange("p a b -> p (a b)")
        psTf = psT[:, :, :].rearrange("p a b -> p (a b)")

        def mixer_sp(sp):
            with sp.Fori(0, B) as b:
                for q in range(2):
                    sp.wait_ge(S.xT, 2 * b + q + 1 + START)
                    sp.sem_inc(S.waits_alone, 1)
                    sp.wait_ge(S.yT_out, 16 * (2 * b + q) + START)
                    sp.sem_inc(S.waits_alone, 1)
                    sp.dma_start(yT_d[2 * b + q], xT[:, 1 + q * GC:1 + (q + 1) * GC]).then_inc(S.yT_out, 16)

        def mixer_order(eng, prologue, batch):
            prologue()
            batch(0, False, True)
            with eng.Fori(1, B - 1) as b:
                batch(b, True, True)
            batch(B - 1, True, False)

        def mixer_pool(pool):
            V = nc.gpsimd

            def rstd_of(n):
                pool.wait_ge(S.lnc, 12 * n + 8 + START)
                pool.sem_inc(S.waits_alone, 1)
                V.tensor_scalar(rstd, mv[:, :, 1], EPS, 1.0, ALU.add, ALU.mult).then_inc(S.lnc_rstd, 1)
                pool.wait_ge(S.lnc_rstd, 2 * n + 1 + START)
                pool.sem_inc(S.waits_alone, 1)
                V.tensor_tensor(rstd, rstd, half[:, :], ALU.pow).then_inc(S.lnc_rstd, 1)

            def differences(b):
                pool.wait_ge(S.xT, 2 * b + 2 + START)
                pool.sem_inc(S.waits_alone, 1)
                pool.wait_ge(S.xT0, b + 1 + START)
                pool.sem_inc(S.waits_alone, 1)
                for q in range(2):
                    V.tensor_tensor(DF[:, q, :], xT[:, 1 + q * GC:1 + (q + 1) * GC], xT[:, q * GC:(q + 1) * GC], ALU.subtract)\
                        .then_inc(S.diff, 1)

            def gate(n, q):
                pool.wait_ge(S.cs, n + 1 + START)
                pool.sem_inc(S.waits_alone, 1)
                pool.wait_ge(S.rs, n + 2 - q + START)
                pool.sem_inc(S.waits_alone, 1)
                pool.wait_ge(S.mo, n - 1 + START)
                pool.sem_inc(S.waits_alone, 1)
                V.tensor_tensor(OT[:, q, :], CS[:, q, :], RS[:, q, :], ALU.mult).then_inc(S.ot, 1)

            def prologue():
                rstd_of(0)
                rstd_of(1)
                differences(0)

            def batch(b, follows, more):
                if more:
                    rstd_of(2 * b + 2)
                    rstd_of(2 * b + 3)
                    differences(b + 1)
                gate(2 * b, 0)
                gate(2 * b + 1, 1)

            mixer_order(pool, prologue, batch)

        def mixer_act(act):
            V = nc.scalar

            def features(n, q):
                act.wait_ge(S.xT_turn, n + 1 + START)
                act.wait_ge(S.yT_out, 16 * (n - q) + START)
                act.wait_ge(S.mixed, 4 * (n - q) + START)
                V.activation(xT[:, 1 + q * GC:1 + (q + 1) * GC], psTf, ACT.Copy).then_inc(S.xT, 1)
                if q == 1:
                    act.wait_ge(S.xT, n + 1 + START)
                    V.activation(xT[:, 0:1], xT[:, L:L + 1], ACT.Copy).then_inc(S.xT0, 1)

            def router_exp(b):
                act.wait_ge(S.rt1, 30 * b + 2 + START)
                V.activation(lg, lg, ACT.Exp).then_inc(S.rt1_exp, 1)

            def project(n, q):
                act.wait_ge(S.grkv, 2 * n + 1 + START)
                act.wait_ge(S.cs, n - 1 + START)
                V.activation(SG[:, q, :], ring[0][:, 0, :], ACT.Sigmoid, bias=l1b[:, 0:1]).then_inc(S.sg, 1)
                act.wait_ge(S.grkv, 2 * n + 2 + START)
                V.activation(KK[:, q, :], ring[1][:, 0, :], ACT.Identity, bias=l1b[:, 2:3]).then_inc(S.kk, 1)

            def square(n):
                act.wait_ge(S.cen, n + 1 + START)
                V.activation(SQ, psAf, ACT.Square).then_inc(S.sq, 1)

            def variance(n, q):
                act.wait_ge(S.var, n + 1 + START)
                act.wait_ge(S.ot, n - 1 + START)
                V.activation(RS[:, q, :], psLf, ACT.Ln, bias=eps_col[:, 0:1]).then_inc(S.lnv, 1)

            def prologue():
                for q in range(2):
                    features(q, q)

            def batch(b, follows, more):
                n = 2 * b
                project(n, 0)
                if more:
                    features(n + 2, 0)
                square(n)
                project(n + 1, 1)
                variance(n, 0)
                if more:
                    features(n + 3, 1)
                square(n + 1)
                variance(n + 1, 1)
                act.wait_ge(S.lnv, n + 2 + START)
                V.activation(RS, RS, ACT.Exp, scale=-0.5).then_inc(S.rs, 2)
                router_exp(b)

            mixer_order(act, prologue, batch)

        def mixer_dve(dve):
            V = nc.vector

            def norm_stats(n):
                for j in range(GT):
                    V.bn_stats(st6[:, j, :], X[:, bass.ds(n * GT + j, 1), :].rearrange("p a d -> p (a d)")).then_inc(S.lnc, 1)
                dve.wait_ge(S.lnc, 12 * n + 4 + START)
                dve.sem_inc(S.waits_alone, 1)
                for j in range(GT):
                    V.bn_aggr(mv[:, j, :], st6[:, j, :]).then_inc(S.lnc, 1)

            def norm_apply(n, q):
                dve.wait_ge(S.lnc_rstd, 2 * n + 2 + START)
                dve.wait_ge(S.xT_turn, n - 1 + START)
                for j in range(GT):
                    V.tensor_scalar(YN[q][:, j, :], X[:, bass.ds(n * GT + j, 1), :].rearrange("p a d -> p (a d)"), mv[:, j, 0:1],
                                    rstd[:, j:j + 1], ALU.subtract, ALU.mult).then_inc(S.lnc, 1)

            def router_start(b):
                dve.wait_ge(S.logit_turn, 2 * b + 2 + START)
                route_start(dve, S.rt1, S.logits1, b, psY[:, 0:2 * GT * EX].rearrange("p (a b) -> p a b", b=EX), 1)

            def router_end(b):
                route_end(dve, S.rt1, S.rt1_exp, b, 1, cw1)

            def mix(n, q):
                dve.wait_ge(S.diff, n - q + 2 + START)
                dve.wait_ge(S.grkv, 2 * n - 2 + START)
                for i in range(4):
                    V.scalar_tensor_tensor(out=MX[q][:, i, :], in0=DF[:, q, :], scalar=l1m[:, i:i + 1],
                                           in1=xT[:, q * GC:(q + 1) * GC], op0=ALU.mult, op1=ALU.add).then_inc(S.mixed, 1)

            def project(n, q):
                dve.wait_ge(S.kk, n + 1 + START)
                V.scalar_tensor_tensor(out=KV, in0=ring[1][:, 1, :], scalar=l1b[:, 3:4], in1=KK[:, q, :], op0=ALU.add, op1=ALU.mult)\
                    .then_inc(S.kv, 1)
                dve.wait_ge(S.kv, n + 1 + START)
                dve.wait_ge(S.scan, n + START)
                V.tensor_tensor_scan(ACC[:, q, :], l1w[:, 3:4].to_broadcast([P, GC]), KV, 0.0 if q == 0 else ACC[:, 0, GC - 1:GC],
                                     ALU.mult, ALU.add).then_inc(S.scan, 1)
                dve.wait_ge(S.scan, n + 1 + START)
                V.scalar_tensor_tensor(out=WK, in0=KV, scalar=l1w[:, 1:2], in1=ACC[:, q, :], op0=ALU.mult, op1=ALU.add)\
                    .then_inc(S.wkv, 1)
                dve.wait_ge(S.wkv, n + 1 + START)
                V.scalar_tensor_tensor(out=RW, in0=ring[0][:, 1, :], scalar=l1b[:, 1:2], in1=WK, op0=ALU.add, op1=ALU.mult)\
                    .then_inc(S.rw, 1)

            def centred(n, q):
                dve.wait_ge(S.sq, n + 1 + START)
                dve.wait_ge(S.ot, n - 1 + START)
                V.tensor_tensor(CS[:, q, :], psAf, SG[:, q, :], ALU.mult).then_inc(S.cs, 1)

            def add(n):
                dve.wait_ge(S.mo, n + 1 + START)
                xg = X[:, bass.ds(n * GT, GT), :]
                V.tensor_tensor(xg, psT[:, :, :], xg, ALU.add).then_inc(S.xo, 1)

            def prologue():
                dve.wait_ge(S.facc[0], 33 * NG + START)
                for q in range(2):
                    norm_stats(q)
                    norm_apply(q, q)
                mix(0, 0)

            def batch(b, follows, more):
                n = 2 * b
                mix(n + 1, 1)
                if more:
                    norm_stats(n + 2)
                if follows:
                    add(n - 2)
                project(n, 0)
                if follows:
                    add(n - 1)
                if more:
                    norm_apply(n + 2, 0)
                    norm_stats(n + 3)
                if follows:
                    router_end(b - 1)
                router_start(b)
                centred(n, 0)
                if more:
                    norm_apply(n + 3, 1)
                project(n + 1, 1)
                centred(n + 1, 1)
                if more:
                    mix(n + 2, 0)

            mixer_order(dve, prologue, batch)
            add(2 * B - 2)
            router_end(B - 1)
            add(2 * B - 1)

        def mixer_pe(pe):
            T = nc.tensor

            def features(n, q):
                pe.wait_ge(S.lnc, 12 * n + 12 + START)
                pe.wait_ge(S.xT, n + START)
                pe.wait_ge(S.xo, n - 2 - q + START)
                for j in range(GT):
                    m = T.transpose(psT[:, j, :], YN[q][:, j, :], ident[:, :])
                m.then_inc(S.xT_turn, 1)

            def router(n, q, b):
                pe.wait_ge(S.xT, n + 1 + START)
                pe.wait_ge(S.logits1, b + START)
                for j in range(GT):
                    c = 1 + q * GC + j * P
                    m = T.matmul(psY[:, (q * GT + j) * EX:(q * GT + j + 1) * EX], xT[:, c:c + P], rw1[:, :], start=True, stop=True)
                m.then_inc(S.logit_turn, 1)

            def project(n, q):
                pe.wait_ge(S.mixed, 4 * n + 4 + START)
                pe.wait_ge(S.sg, n + START)
                pe.wait_ge(S.rw, n + START)
                for i in range(2):
                    for k in range(2):
                        m = T.matmul(ring[i][:, k, :], wsqT[:, 3 + 2 * i + k, :], MX[q][:, 2 * i + k, :], start=True, stop=True)
                    m.then_inc(S.grkv, 1)

            def centre(n):
                pe.wait_ge(S.rw, n + 1 + START)
                pe.wait_ge(S.cs, n + START)
                T.matmul(psAf, cen[:, :], RW, start=True, stop=True).then_inc(S.cen, 1)

            def variance(n):
                pe.wait_ge(S.sq, n + 1 + START)
                pe.wait_ge(S.lnv, n + START)
                T.matmul(psLf, avg[:, :], SQ, start=True, stop=True).then_inc(S.var, 1)

            def output(n, q, more=True):
                pe.wait_ge(S.ot, n + 1 + START)
                pe.wait_ge(S.xo, n + START)
                pe.wait_ge(S.xT, n - q + 4 + START if more else n - q + 2 + START)
                for j in range(GT):
                    T.matmul(psT[:, j, :], OT[:, q, j * P:(j + 1) * P], wsqT[:, 7, :], start=True, stop=False)
                    m = T.matmul(psT[:, j, :], ones_row[:, :], wob_row[:, :], start=False, stop=True)
                m.then_inc(S.mo, 1)

            def prologue():
                pe.wait_ge(S.cwT, NG + START)
                pe.wait_ge(S.facc[0], 33 * NG + START)
                for q in range(2):
                    features(q, q)
                for q in range(2):
                    router(q, q, 0)

            def batch(b, follows, more):
                n = 2 * b
                project(n, 0)
                if follows:
                    output(n - 2, 0)
                    output(n - 1, 1)
                if more:
                    features(n + 2, 0)
                centre(n)
                project(n + 1, 1)
                variance(n)
                if more:
                    features(n + 3, 1)
                centre(n + 1)
                if more:
                    router(n + 2, 0, b + 1)
                    router(n + 3, 1, b + 1)
                variance(n + 1)

            mixer_order(pe, prologue, batch)
            output(2 * B - 2, 0, False)
            output(2 * B - 1, 1, False)

        def sp_rest(sp):
            ffn_sp(sp, 0)
            mixer_sp(sp)
            ffn_sp(sp, 1)

        def pool_rest(pool):
            mixer_pool(pool)

        def act_rest(act):
            ffn_act(act, 0)
            mixer_act(act)
            ffn_act(act, 1)

        def dve_rest(dve):
            ffn_dve(dve, 0)
            mixer_dve(dve)
            ffn_dve(dve, 1)

        def pe_rest(pe):
            ffn_pe(pe, 0)
            mixer_pe(pe)
            ffn_pe(pe, 1)

        def nothing(*group):
            pass

        block = ctx.enter_context(nc.Block())
        n_load = [0]

        @block.sync
        def _(sp):
            def load(dst, src, scattered=False):
                sp.dma_start(dst, src, allow_slow_non_contiguous=scattered).then_inc(S.loaded, 16)
                n_load[0] += 16

            bq = [I["L0_attn_bqkv_a"], I["L0_attn_bqkv_s"]]
            for a, w in enumerate(("L0_attn_Wqkv_a", "L0_attn_Wqkv_s")):
                load(wraw[a], I[w])
                load(braw[a], bq[a].partition_broadcast(P))
            for i, w in enumerate(("L0_attn_Wp_a", "L0_attn_Wo_s", "L0_attn_Wo", "L1_attn_Wg_w", "L1_attn_Wr_w", "L1_attn_Wk_w",
                                   "L1_attn_Wv_w", "L1_attn_Wo_w")):
                load(wsq[:, i, :], I[w])

            def col(dst, name):
                load(dst, I[name].rearrange("(p o) -> p o", o=1))

            for i, w in enumerate(("L0_attn_g1", "L0_attn_b1", "L0_attn_gm", "L0_attn_bm")):
                col(gb[:, i:i + 1], w)
            col(bcol[:, 0:1], "L0_attn_bp_a")
            col(bcol[:, 1:2], "L0_attn_bo_s")
            for i, w in enumerate("grkv"):
                col(l1b[:, i:i + 1], f"L1_attn_W{w}_b")
                col(l1m[:, i:i + 1], f"L1_attn_m{w}")
            load(l1w[:, 0:1], I["L1_attn_w"].rearrange("h (e o) -> (h e) o", o=1))
            load(l1w[:, 1:2], I["L1_attn_u"].rearrange("h (e o) -> (h e) o", o=1))
            load(bo_row[0:1, :], I["L0_attn_bo"].rearrange("(o n) -> o n", o=1))
            load(wob_row[:, :], I["L1_attn_Wo_b"].rearrange("(o n) -> o n", o=1))
            load(rw0[:, :], I["L0_ffn_router_w"])
            load(rb[:, 0, :], I["L0_ffn_router_b"].partition_broadcast(P))
            load(rw1r[:, :], I["L1_ffn_router_w"])
            load(W1[:, :, :], I["L0_attn_W1"].rearrange("d (c f) -> d c f", c=CM))
            load(W2[:, :, :], I["L0_attn_W2"].rearrange("(c f) d -> f c d", c=CM))
            load(b1m[:, :], I["L0_attn_b1m"].rearrange("(c f) -> f c", c=CM), scattered=True)
            load(b2x[0:EX, :], I["L0_ffn_b2"])
            load(b2x[EX:EX + 1, :], I["L0_attn_b2m"].rearrange("(o n) -> o n", o=1))
            load(fb1[:, :, :], I["L0_ffn_b1"].rearrange("e (c f) -> f e c", c=C0), scattered=True)
            for c in counters:
                sp.sem_inc(c, START)
            sp.sem_inc(S.setup, 1)
            sp.wait_ge(S.setup, SETUP)

            def first_norm(h, par):
                norm(0, 0)
                norm(0, 1)

            def norm(h, par):
                g = 2 * h + par
                sp.wait_ge(S.xsum, g - 1 + START)
                sp.sem_inc(S.waits_alone, 1)
                sp.dma_start(XIN[par], x_d[g]).then_inc(S.xin[par], 16)

            def send_parts(h, par, pair):
                g = 2 * h + par
                sp.wait_ge(S.low, 2 * g + pair + 1 + START)
                sp.sem_inc(S.waits_alone, 1)
                for i in range(2):
                    sp.wait_ge(S.stack[pair][par], 144 * h + START)
                    sp.sem_inc(S.waits_alone, 1)
                    sp.dma_start(part_d[par][2 * pair + i].rearrange("c p t -> p c t"), parts[:, i]).then_inc(S.sent[pair], 16)
                sp.wait_ge(S.sent[pair], 32 * (g + 1) + START)
                sp.sem_inc(S.waits_alone, 1)
                sp.wait_ge(S.amask, 8 * (g - 1) + START)
                sp.sem_inc(S.waits_alone, 1)
                sp.wait_ge(S.tails, 16 * h + START)
                sp.sem_inc(S.waits_alone, 1)
                r0 = LR if pair else 0
                q_d, k_d = part_d[par][2 * pair], part_d[par][2 * pair + 1]
                row = 0
                for n in (3, 2, 1):
                    sp.dma_start(QS[par][r0 + row:r0 + row + E * n, :, :],
                                 q_d[0:n].rearrange("c (e h) t -> (c e) h t", h=H)).then_inc(S.stack[pair][par], 16)
                    for i in range(n):
                        sp.dma_start(KS[par][r0 + row + E * i:r0 + row + E * i + E, :, :],
                                     k_d[3 - n].rearrange("(e h) t -> e h t", h=H)).then_inc(S.stack[pair][par], 16)
                    row += E * n

            def prep(h, par, minus=None):
                g = 2 * h + par
                if par == 1:
                    sp.wait_ge(S.stack[0][0], 144 * (h + 1) + START)
                    sp.sem_inc(S.waits_alone, 1)
                    sp.wait_ge(S.exps, 32 * h + START)
                    sp.sem_inc(S.waits_alone, 1)
                    sp.dma_start(KT[:, :, :], KS[0][0:QKM, :, GC - P:GC]).then_inc(S.tails, 16)
                sp.wait_ge(S.xnT, g + 1 + START)
                sp.sem_inc(S.waits_alone, 1)
                sp.dma_start(xnT_d[g], xnT).then_inc(S.xnT_out[par], 16)
                if minus is not None:
                    minus_rows(*minus)
                send_parts(h, par, 0)
                send_parts(h, par, 1)

            def minus_rows(h, par):
                g = 2 * h + par
                sp.wait_ge(S.mT, g + 1 + START)
                sp.sem_inc(S.waits_alone, 1)
                for c in range(3):
                    sp.dma_start(QS[par][QK + c:QK + c + 1, :, :], MT[c * H:(c + 1) * H, :]).then_inc(S.mrow[par], 16)

            def store_hidden(h, par):
                g = 2 * h + par
                sp.wait_ge(S.hT, g + 1 + START)
                sp.sem_inc(S.waits_alone, 1)
                sp.dma_start(hT_d[g], hT).then_inc(S.hT_out[par], 16)

            def mx(h, par, follows, more):
                if more and follows:
                    norm(h + par, 1 - par)
                if follows:
                    store_hidden(h - 1 + par, 1 - par)
                if more:
                    prep(h + par, 1 - par, (h, par))
                else:
                    minus_rows(h, par)

            def attend(h, par, last):
                if last:
                    sp.wait_ge(S.exps, 16 * (NG - 1) + START)
                    sp.sem_inc(S.waits_alone, 1)
                    sp.wait_ge(S.amask, 8 * (NG - 1) + START)
                    sp.sem_inc(S.waits_alone, 1)
                    sp.dma_start(w_up[0], I["L0_ffn_w1"].rearrange("e d f -> d e f")).then_inc(S.ffnw[0], 16)
                    sp.dma_start(w_dn[0], I["L0_ffn_w2"].rearrange("e (c f) d -> f e c d", c=C0)).then_inc(S.ffnw[0], 16)

            attention_order(prep, nothing, attend, mx, first_norm, store_hidden, sp)
            sp_rest(sp)

        @block.gpsimd
        def _(pool):
            V = nc.gpsimd
            done = 0
            zero = [(ident[:, :], 0.0), (identb[:, :], 0.0), (mkey[:, :, :, :], 0.0), (mqry[:, :, :, :], 0.0), (tri[:, :], 1.0),
                    (avg[:, :], 1.0 / E), (half[:, :], -0.5), (ones_row[:, :], 1.0), (SB[:, :, :], 0.0), (rb[:, 1, :], 0.0),
                    (cw0[:, :, EX:EX + 1], 1.0), (cw0[:, TILES:TILES + GT, 0:EX], 0.0)]
            zero += [(v[:, :, :, E:E + 1], 1.0) for v in VA + VL] + [(k[32:64, :, :], 1.0) for k in KS]
            for ap, value in zero:
                V.memset(ap, value).then_inc(S.consts, 1)
                done += 1
                pool.wait_ge(S.consts, done)
            V.iota(iou[:, :], pattern=[[1, EX]], base=0, channel_multiplier=0).then_inc(S.consts, 1)
            pool.wait_ge(S.consts, done + 1)
            V.tensor_copy(iot[:, :], iou[:, :]).then_inc(S.consts, 1)
            done += 2
            picks = [(ident[:, :], ALU.not_equal, 1.0, 0, [[-1, P]], 1), (identb[:, :], ALU.not_equal, 1.0, 0, [[-1, P]], 1),
                     (tri[:, :], ALU.is_ge, 0.0, 0, [[1, P]], -1)]
            for i in range(2):
                picks += [(mkey[:, i, 0, :], ALU.is_gt, MASKED, 0, [[-1, P]], 1),
                          (mkey[:, i, 1, :], ALU.is_ge, MASKED, 0, [[1, P]], -1),
                          (mqry[:, i, 0, :], ALU.is_gt, MASKED, 0, [[1, P]], -1),
                          (mqry[:, i, 1, :], ALU.is_ge, MASKED, 0, [[-1, P]], 1)]
            picks += [(h_e(avg[:, :]), ALU.is_ge, 0.0, 0, [[-E, H], [0, E]], 1),
                      (h_e(avg[:, :]), ALU.is_ge, 0.0, E - 1, [[E, H], [0, E]], -1)]
            for ap, compare, fill, base, pattern, mult in picks:
                pool.wait_ge(S.consts, done)
                V.affine_select(out=ap, in_=ap, compare_op=compare, fill=fill, base=base, pattern=pattern, channel_multiplier=mult)\
                    .then_inc(S.consts, 1)
                done += 1
            pool.wait_ge(S.consts, done)
            V.tensor_tensor(cen[:, :], ident[:, :], avg[:, :], ALU.subtract).then_inc(S.consts, 1)
            done += 1
            assert done == N_CONSTS, done
            pool.wait_ge(S.consts, done)
            V.memset(idv[0:1, 0:1], 0.0).then_inc(S.setup, 1)
            pool.wait_ge(S.setup, SETUP)

            def norm(h, par):
                g = 2 * h + par
                pool.wait_ge(S.lnp, 16 * g + 8 + START)
                pool.sem_inc(S.waits_alone, 1)
                V.tensor_scalar(rstd, mv[:, :, 1], EPS, 1.0, ALU.add, ALU.mult).then_inc(S.lnp_rstd, 1)
                pool.wait_ge(S.lnp_rstd, 6 * g + 1 + START)
                pool.sem_inc(S.waits_alone, 1)
                V.tensor_tensor(rstd, rstd, half[:, :], ALU.pow).then_inc(S.lnp_rstd, 1)
                pool.wait_ge(S.lnp_rstd, 6 * g + 2 + START)
                pool.sem_inc(S.waits_alone, 1)
                V.tensor_tensor(rstd2, rstd, rstd, ALU.mult).then_inc(S.lnp_rstd, 1)
                pool.wait_ge(S.lnp_rstd, 6 * g + 3 + START)
                pool.sem_inc(S.waits_alone, 1)
                V.tensor_tensor(rstd2, rstd2, mv[:, :, 1], ALU.mult).then_inc(S.lnp_rstd, 1)
                pool.wait_ge(S.lnp_rstd, 6 * g + 4 + START)
                pool.sem_inc(S.waits_alone, 1)
                V.tensor_scalar(rstd2, rstd2, EPS, 1.0, ALU.add, ALU.mult).then_inc(S.lnp_rstd, 1)
                pool.wait_ge(S.lnp_rstd, 6 * g + 5 + START)
                pool.sem_inc(S.waits_alone, 1)
                V.tensor_tensor(rstd2, rstd2, half[:, :], ALU.pow).then_inc(S.lnp_rstd, 1)

            def prep(h, par):
                g = 2 * h + par
                pool.wait_ge(S.resid, 2 * g + 2 + START)
                pool.sem_inc(S.waits_alone, 1)
                pool.wait_ge(S.sent[1], 32 * g + START)
                pool.sem_inc(S.waits_alone, 1)
                V.tensor_copy(parts[:, :, 1, :], res).then_inc(S.mid, 1)
                pool.wait_ge(S.mid, 2 * g + 1 + START)
                pool.sem_inc(S.waits_alone, 1)
                V.tensor_tensor(parts[:, :, 2, :], res, parts[:, :, 1, :], ALU.subtract).then_inc(S.low, 1)
                pool.wait_ge(S.lin_y, 2 * g + 2 + START)
                pool.sem_inc(S.waits_alone, 1)
                pool.wait_ge(S.lin_sum, g + START)
                pool.sem_inc(S.waits_alone, 1)
                V.tensor_scalar(eb, Y32, 0.0, MASKED, ALU.min, ALU.max).then_inc(S.lin_min, 1)
                pool.wait_ge(S.lin_sum, g + 1 + START)
                pool.sem_inc(S.waits_alone, 1)
                pool.wait_ge(S.tm, 12 * g + 12 + START)
                pool.sem_inc(S.waits_alone, 1)
                V.tensor_scalar(kexp, kraw, 0.0, MASKED, ALU.min, ALU.max).then_inc(S.kmin, 1)
                pool.wait_ge(S.ol, 4 * (g - 1) + START)
                pool.sem_inc(S.waits_alone, 1)
                V.tensor_scalar(QF[par], Y32[:, 0, :], 1e-4, 1.0, ALU.add, ALU.mult).then_inc(S.lin_qk, 1)
                V.tensor_scalar(Y32[:, 1, :], Y32[:, 1, :], 1e-4, 1.0, ALU.add, ALU.mult).then_inc(S.lin_qk, 1)
                pool.wait_ge(S.high, 4 * g + 4 + START)
                pool.sem_inc(S.waits_alone, 1)
                pool.wait_ge(S.low, 2 * g + 1 + START)
                pool.sem_inc(S.waits_alone, 1)
                V.tensor_tensor(res[:, 0, :], QF[par], parts[:, 0, 0, :], ALU.subtract).then_inc(S.lin_res, 1)
                V.tensor_tensor(res[:, 1, :], Y32[:, 1, :], parts[:, 1, 0, :], ALU.subtract).then_inc(S.lin_res, 1)
                pool.wait_ge(S.lin_res, 2 * g + 2 + START)
                pool.sem_inc(S.waits_alone, 1)
                V.tensor_copy(parts[:, :, 1, :], res).then_inc(S.mid, 1)
                pool.wait_ge(S.mid, 2 * g + 2 + START)
                pool.sem_inc(S.waits_alone, 1)
                V.tensor_tensor(parts[:, :, 2, :], res, parts[:, :, 1, :], ALU.subtract).then_inc(S.low, 1)
                pool.wait_ge(S.kmin, g + 1 + START)
                pool.sem_inc(S.waits_alone, 1)
                V.tensor_scalar(kraw, kraw, 0.0, 1e-4, ALU.max, ALU.add).then_inc(S.kmax, 1)
                pool.wait_ge(S.kmax, g + 1 + START)
                pool.sem_inc(S.waits_alone, 1)
                pool.wait_ge(S.kexp, g + 1 + START)
                pool.sem_inc(S.waits_alone, 1)
                V.tensor_tensor(KST[par], kraw, kexp, ALU.add).then_inc(S.kst, 1)
                if par == 1:
                    pool.wait_ge(S.tm, 12 * g + START)
                    pool.sem_inc(S.waits_alone, 1)
                    pool.wait_ge(S.pv, 32 * h + START)
                    pool.sem_inc(S.waits_alone, 1)
                    V.tensor_copy(VT[:, :, :], VA[0][:, GT - 1, :, :]).then_inc(S.tailv, 1)

            def finish(h, par):
                g = 2 * h + par
                pool.wait_ge(S.x1, 4 * g + 4 + START)
                pool.sem_inc(S.waits_alone, 1)
                V.tensor_tensor(X[:, bass.ds(g * GT, GT), :], X1, XIN[par], ALU.add).then_inc(S.xsum, 1)
                pool.wait_ge(S.lne, 12 * g + 8 + START)
                pool.sem_inc(S.waits_alone, 1)
                V.tensor_scalar(rstdh, mvh[:, :, 1], EPS, 1.0, ALU.add, ALU.mult).then_inc(S.lne_rstd, 1)
                pool.wait_ge(S.lne_rstd, 2 * g + 1 + START)
                pool.sem_inc(S.waits_alone, 1)
                V.tensor_tensor(rstdh, rstdh, half[:, :], ALU.pow).then_inc(S.lne_rstd, 1)
                pool.wait_ge(S.lne_rstd, 2 * g + 2 + START)
                pool.sem_inc(S.waits_alone, 1)
                pool.wait_ge(S.xsum, g + 1 + START)
                pool.sem_inc(S.waits_alone, 1)
                for j in range(GT):
                    V.tensor_scalar(HN[:, j, :], X1[:, j, :], mvh[:, j, 0:1], rstdh[:, j:j + 1], ALU.subtract, ALU.mult)\
                        .then_inc(S.lne, 1)

            def mx(h, par, follows, more):
                if follows:
                    finish(h - 1 + par, 1 - par)
                if more:
                    norm(h + par, 1 - par)
                    prep(h + par, 1 - par)

            attention_order(prep, nothing, nothing, mx, norm, finish, pool)
            pool_rest(pool)

        @block.scalar
        def _(act):
            V = nc.scalar
            act.wait_ge(S.loaded, n_load[0])
            act.wait_ge(S.wT, 1)
            for i in range(2):
                V.activation(wsqT[:, 4 * i:4 * i + 4, :].rearrange("p a b -> p (a b)"), ring[i][:, 0, :], ACT.Copy).then_inc(S.wTc, 1)
            act.wait_ge(S.wmixed, 1)
            V.activation(wmix[:, :, :], psT[:, 0:2, :], ACT.Copy).then_inc(S.actset, 1)
            V.activation(rw1[:, :], psY[:, 0:EX], ACT.Copy).then_inc(S.actset, 1)
            V.activation(bfm[:, :], psY[:, 16:20], ACT.Copy).then_inc(S.actset, 1)
            V.activation(l1w[:, 2:3], l1w[:, 0:1], ACT.Exp).then_inc(S.actset, 1)
            act.wait_ge(S.actset, 4)
            V.activation(l1w[:, 3:4], l1w[:, 2:3], ACT.Exp, scale=-1.0).then_inc(S.actset, 1)
            act.wait_ge(S.actset, 5)
            V.activation(bcol[:, 2:3], l1w[:, 2:3], ACT.Copy).then_inc(S.setup, 1)
            act.wait_ge(S.setup, SETUP)

            def prep(h, par, minus=None):
                g = 2 * h + par
                r = lambda k: ring[k % 2]
                act.wait_ge(S.lnp, 16 * g + 12 + START)
                act.wait_ge(S.turn_prep, 6 * (g - 1) + 2 + START)
                for j in range(GT):
                    V.activation(XH[:, j, :], XN[par][:, j, :], ACT.Copy, scale=rstd2[:, j:j + 1]).then_inc(S.lnp, 1)
                act.wait_ge(S.turn_prep, 6 * g + 1 + START)
                act.wait_ge(S.xnT_out[1 - par], 16 * (h if par == 0 else h + 1) + START)
                V.activation(xnT, r(0)[:, 0, :], ACT.Copy).then_inc(S.xnT, 1)
                act.wait_ge(S.turn_prep, 6 * g + 2 + START)
                V.activation(xhT, r(1)[:, 0, :], ACT.Identity, scale=gb[:, 0:1], bias=gb[:, 1:2]).then_inc(S.xhT, 1)
                act.wait_ge(S.turn_prep, 6 * g + 3 + START)
                act.wait_ge(S.sent[1], 32 * g + START)
                for i in range(2):
                    V.activation(parts[:, i, 0, :], r(2)[:, i, :], ACT.Identity, bias=bfm[:, i:i + 1]).then_inc(S.high, 1)
                act.wait_ge(S.rt0, 22 * g + 2 + START)
                V.activation(lg[:, 0:GT, :], lg[:, 0:GT, :], ACT.Exp).then_inc(S.rt0_exp, 1)
                if minus is not None:
                    minus_rows(*minus)

            def late_exp(h, par):
                g = 2 * h + par
                act.wait_ge(S.lin_min, g + 1 + START)
                V.activation(eb, eb, ACT.Exp).then_inc(S.lin_exp, 1)

            def late_high(h, par):
                g = 2 * h + par
                act.wait_ge(S.lin_qk, 2 * g + 2 + START)
                act.wait_ge(S.sent[0], 32 * (g + 1) + START)
                V.activation(parts[:, 0, 0, :], QF[par], ACT.Copy).then_inc(S.high, 1)
                V.activation(parts[:, 1, 0, :], Y32[:, 1, :], ACT.Copy).then_inc(S.high, 1)
                act.wait_ge(S.kmin, g + 1 + START)
                V.activation(kexp, kexp, ACT.Exp).then_inc(S.kexp, 1)

            def late(h, par):
                late_exp(h, par)
                late_high(h, par)

            def minus_rows(h, par):
                g = 2 * h + par
                act.wait_ge(S.mT_turn, g + 1 + START)
                act.wait_ge(S.mrow[1 - par], 48 * (h + par) + START)
                V.activation(MT[0:3 * H, :], psY[:, 256:512].bitcast(BF16)[0:3 * H, :], ACT.Copy).then_inc(S.mT, 1)

            def copy_attended(u):
                act.wait_ge(S.y, u + 1 + START)
                V.activation(AST, psT[:, 0:2, :], ACT.Copy).then_inc(S.ast, 1)

            def copy_hidden(h, par):
                g = 2 * h + par
                act.wait_ge(S.hT_turn, g + 1 + START)
                act.wait_ge(S.hT_out[1 - par], 16 * (h + par) + START)
                V.activation(hT, psT[:, :, :].rearrange("p a b -> p (a b)"), ACT.Identity, scale=gb[:, 2:3],
                             bias=gb[:, 3:4]).then_inc(S.hT, 1)

            def finish(h, par):
                copy_attended(GT * (2 * h + par) + GT - 1)
                copy_hidden(h, par)

            def mx(h, par, follows, more):
                if follows:
                    finish(h - 1 + par, 1 - par)
                if more:
                    prep(h + par, 1 - par, (h, par))
                else:
                    minus_rows(h, par)

            def attend(h, par, last):
                g = 2 * h + par
                for j in range(GT):
                    t = GT * g + j
                    for q in range(4):
                        if q == 3 and j > 0:
                            copy_attended(t - 1)
                        act.wait_ge(S.turn_attend, 24 * g + 6 * j + q + 3 + START)
                        act.wait_ge(S.pv, 4 * t + max(q - 1, 0) + START)
                        n = 256 if par == 0 and j == 0 else 512
                        V.activation(PB[q % 2].rearrange("p a b c -> p (a b c)")[:, 0:2 * n].rearrange("p (a n) -> p a n", a=2),
                                     ring[q % 2][:, :, 0:n], ACT.Exp, scale=RSQ).then_inc(S.exps, 1)
                    act.wait_ge(S.pv, 4 * t + 4 + START)
                    act.wait_ge(S.t1, t + START)
                    V.activation(OAs, psA[:, :, :], ACT.Copy).then_inc(S.oas, 1)
                    act.wait_ge(S.ol, t + 1 + START)
                    act.wait_ge(S.t2, t + START)
                    V.activation(OLs, psL[:, :, :], ACT.Copy).then_inc(S.ols, 1)
                    if j == 0 and not last:
                        late_exp(h + par, 1 - par)
                    if j == 2 and not last:
                        late_high(h + par, 1 - par)

            attention_order(prep, late, attend, mx, nothing, finish, act)
            act_rest(act)

        def layernorm(eng, steps, rstds, n, src, dst, free=None, value=None):
            V = nc.vector
            for j in range(GT):
                V.bn_stats(st6[:, j, :], src(j)).then_inc(steps, 1)
            eng.wait_ge(steps, 12 * n + 4 + START)
            eng.sem_inc(S.waits_alone, 1)
            for j in range(GT):
                V.bn_aggr(mv[:, j, :], st6[:, j, :]).then_inc(steps, 1)
            eng.wait_ge(rstds, 2 * n + 2 + START)
            if free is not None:
                eng.wait_ge(free, value)
            for j in range(GT):
                V.tensor_scalar(dst(j), src(j), mv[:, j, 0:1], rstd[:, j:j + 1], ALU.subtract, ALU.mult).then_inc(steps, 1)

        def route_start(eng, steps, read, n, logits, layer):
            V = nc.vector
            tiles = (1 + layer) * GT
            base = (14 + 2 * tiles) * n + START
            lg_, mx_ = lg[:, 0:tiles, :], mx4[:, 0:tiles]
            V.tensor_tensor(lg_, logits, rb[:, layer, :].unsqueeze(1).to_broadcast([P, tiles, EX]), ALU.add).then_inc(read, 1)
            eng.wait_ge(read, n + 1 + START)
            V.tensor_reduce(mx_, lg_, AX_X, ALU.max).then_inc(steps, 1)
            eng.wait_ge(steps, base + 1)
            V.tensor_tensor(lg_, lg_, mx_.unsqueeze(2).to_broadcast([P, tiles, EX]), ALU.subtract).then_inc(steps, 1)

        def route_end(eng, steps, exps, n, layer, cw):
            V = nc.vector
            tiles = (1 + layer) * GT
            base = (14 + 2 * tiles) * n + START
            lg_, mx_, first, both = lg[:, 0:tiles, :], mx4[:, 0:tiles], oh[:, 0, 0:tiles], oh[:, :, 0:tiles]
            eng.wait_ge(exps, n + 1 + START)
            V.tensor_reduce(mx_, lg_, AX_X, ALU.add).then_inc(steps, 1)
            eng.wait_ge(steps, base + 3)
            V.reciprocal(mx_, mx_).then_inc(steps, 1)
            eng.wait_ge(steps, base + 4)
            V.tensor_tensor(lg_, lg_, mx_.unsqueeze(2).to_broadcast([P, tiles, EX]), ALU.mult).then_inc(steps, 1)
            eng.wait_ge(steps, base + 5)
            eng.sem_inc(S.waits_alone, 1)
            for j in range(tiles):
                V.max(t8[:, j, :], lg[:, j, :]).then_inc(steps, 1)
            eng.wait_ge(steps, base + 5 + tiles)
            eng.sem_inc(S.waits_alone, 1)
            for j in range(tiles):
                V.max_index(i8[:, j, :], t8[:, j, :], lg[:, j, :]).then_inc(steps, 1)
            eng.wait_ge(steps, base + 5 + 2 * tiles)
            V.tensor_copy(idf[:, 0:tiles], i8[:, 0:tiles, 0:2]).then_inc(steps, 1)
            eng.wait_ge(steps, base + 6 + 2 * tiles)
            for k in range(2):
                V.tensor_tensor(both[:, k], iot[:, :].unsqueeze(1).to_broadcast([P, tiles, EX]),
                                idf[:, 0:tiles, k].unsqueeze(2).to_broadcast([P, tiles, EX]), ALU.is_equal).then_inc(steps, 1)
            V.tensor_tensor(mx_, t8[:, 0:tiles, 0], t8[:, 0:tiles, 1], ALU.add).then_inc(steps, 1)
            eng.wait_ge(steps, base + 9 + 2 * tiles)
            V.tensor_tensor(first, first, both[:, 1], ALU.add).then_inc(steps, 1)
            V.tensor_scalar(mx_, mx_, 1e-9 * layer, None, ALU.add).then_inc(steps, 1)
            eng.wait_ge(steps, base + 11 + 2 * tiles)
            V.reciprocal(mx_, mx_).then_inc(steps, 1)
            V.tensor_tensor(first, first, lg_, ALU.mult).then_inc(steps, 1)
            eng.wait_ge(steps, base + 13 + 2 * tiles)
            V.tensor_tensor(cw[:, bass.ds(n * tiles, tiles), 0:EX], first, mx_.unsqueeze(2).to_broadcast([P, tiles, EX]), ALU.mult)\
                .then_inc(steps, 1)

        @block.vector
        def _(dve):
            V = nc.vector
            V.memset(psA[:, :, :], 0.0).then_inc(S.dveset, 1)
            V.memset(psL[:, :, :], 0.0).then_inc(S.dveset, 1)
            V.memset(eps_col[:, :], EPS).then_inc(S.dveset, 1)
            dve.wait_ge(S.loaded, n_load[0])
            for i, (a, o) in enumerate(((0, 0), (0, 1), (1, 0), (1, 1))):
                V.tensor_copy(wfm[:, i, :].rearrange("p (e h) -> p h e", e=E), h_e(wraw[a][:, o * D:o * D + D])).then_inc(S.dveset, 1)
                V.tensor_copy(btmp[0:1, i, :].rearrange("p (e h) -> p h e", e=E), h_e(braw[a][0:1, o * D:o * D + D])).then_inc(S.bperm, 1)
            for dst, src in ((wtm, wraw), (btm, braw)):
                V.tensor_copy(dst[:, 0, :], src[0][:, 2 * D:3 * D]).then_inc(S.dveset, 1)
                V.tensor_copy(dst[:, 1, :], src[1][:, 2 * D:3 * D]).then_inc(S.dveset, 1)
                V.tensor_copy(dst[:, 2, :].rearrange("p (e h) -> p h e", e=E), h_e(src[1][:, D:2 * D])).then_inc(S.dveset, 1)
            V.tensor_tensor(bcol[:, 2:3], bcol[:, 0:1], bcol[:, 1:2], ALU.add).then_inc(S.bsum, 1)
            dve.wait_ge(S.actset, 3)
            V.tensor_tensor(bc_row[:, :], psY[0:1, 32:32 + D], bo_row[0:1, :], ALU.add).then_inc(S.dveset, 1)
            dve.wait_ge(S.consts, N_CONSTS)
            V.tensor_reduce(bd[:, :], ident[:, :].rearrange("p (e h) -> p h e", e=E), AX_X, ALU.add).then_inc(S.dveset, 1)
            dve.wait_ge(S.dveset, 15)
            V.memset(st6[:, :, :], 0.0).then_inc(S.setup, 1)
            dve.wait_ge(S.setup, SETUP)

            heads = psT[:, :, :].rearrange("p a (b e) -> p (a b) e", e=32)

            def norm_stats(h, par, j):
                dve.wait_ge(S.xin[par], 16 * (h + 1) + START)
                dve.wait_ge(S.lne, 12 * (2 * h + par - 2) + 8 + START)
                V.bn_stats(st6[:, j, :], XIN[par][:, j, :]).then_inc(S.lnp, 1)

            def norm_aggregate(h, par):
                dve.wait_ge(S.lnp, 16 * (2 * h + par) + 4 + START)
                dve.sem_inc(S.waits_alone, 1)
                for j in range(GT):
                    V.bn_aggr(mv[:, j, :], st6[:, j, :]).then_inc(S.lnp, 1)

            def norm_apply(h, par, j):
                dve.wait_ge(S.lnp_rstd, 6 * (2 * h + par) + 6 + START)
                V.tensor_scalar(XN[par][:, j, :], XIN[par][:, j, :], mv[:, j, 0:1], rstd[:, j:j + 1], ALU.subtract, ALU.mult)\
                    .then_inc(S.lnp, 1)

            def norm(h, par):
                for j in range(GT):
                    norm_stats(h, par, j)
                norm_aggregate(h, par)
                for j in range(GT):
                    norm_apply(h, par, j)

            def attended_softmax(u):
                dve.wait_ge(S.t1, u + 1 + START)
                V.reciprocal(rec[:, 0, :], heads[:, :, E]).then_inc(S.rcp, 1)
                dve.wait_ge(S.rcp, 3 * u + 1 + START)
                dve.wait_ge(S.y, u + START)
                V.tensor_tensor(h_e(ATM[:, 0, :]), heads[:, :, 0:E], rec[:, 0, :].unsqueeze(2).to_broadcast([P, H, E]),
                                ALU.mult).then_inc(S.at, 1)

            def attended_linear(u):
                dve.wait_ge(S.t2, u + 1 + START)
                V.tensor_scalar(rec[:, 1, :], heads[:, :, E], 1e-6, None, ALU.add).then_inc(S.rcp, 1)
                dve.wait_ge(S.rcp, 3 * u + 2 + START)
                V.reciprocal(rec[:, 1, :], rec[:, 1, :]).then_inc(S.rcp, 1)
                dve.wait_ge(S.rcp, 3 * u + 3 + START)
                V.tensor_tensor(h_e(ATM[:, 1, :]), heads[:, :, 0:E], rec[:, 1, :].unsqueeze(2).to_broadcast([P, H, E]),
                                ALU.mult).then_inc(S.lt, 1)

            def add_mixed(g, par, j):
                dve.wait_ge(S.mix, GT * g + j + 1 + START)
                dve.wait_ge(S.hT_turn, g + START)
                V.tensor_tensor(X1[:, j, :], psT[:, 2, :], XN[par][:, j, :], ALU.add).then_inc(S.x1, 1)

            def hidden_stats(g, j):
                dve.wait_ge(S.x1, 4 * g + j + 1 + START)
                V.bn_stats(st6[:, j, :], X1[:, j, :]).then_inc(S.lne, 1)

            def hidden_aggregate(g):
                dve.wait_ge(S.lne, 12 * g + 4 + START)
                dve.sem_inc(S.waits_alone, 1)
                for j in range(GT):
                    V.bn_aggr(mvh[:, j, :], st6[:, j, :]).then_inc(S.lne, 1)

            def finish(h, par):
                g = 2 * h + par
                attended_softmax(GT * g + GT - 1)
                attended_linear(GT * g + GT - 1)
                add_mixed(g, par, GT - 1)
                hidden_stats(g, GT - 1)
                hidden_aggregate(g)

            def prep_logits(h, par):
                g = 2 * h + par
                dve.wait_ge(S.turn_prep, 6 * g + 2 + START)
                route_start(dve, S.rt0, S.logits, g, ring[1][:, 1, 0:GT * EX].rearrange("p (a b) -> p a b", a=GT), 0)

            def prep_residues(h, par):
                g = 2 * h + par
                dve.wait_ge(S.turn_prep, 6 * g + 3 + START)
                dve.wait_ge(S.low, 2 * g + START)
                for i in range(2):
                    dve.wait_ge(S.high, 4 * g + i + 1 + START)
                    V.scalar_tensor_tensor(out=res[:, i, :], in0=ring[0][:, i, :], scalar=bfm[:, i:i + 1], in1=parts[:, i, 0, :],
                                           op0=ALU.add, op1=ALU.subtract).then_inc(S.resid, 1)
                dve.wait_ge(S.turn_prep, 6 * g + 4 + START)
                for i in range(2):
                    V.tensor_scalar(Y32[:, i, :], ring[1][:, i, :], bfm[:, 2 + i:3 + i], (RSQ, 1.0)[i], ALU.add, ALU.mult)\
                        .then_inc(S.lin_y, 1)

            def prep_values(h, par):
                g = 2 * h + par
                dve.wait_ge(S.pv, 16 * (g - 1) + START)
                dve.wait_ge(S.ol, 4 * (g - 1) + START)
                dve.wait_ge(S.kst, g + START)
                if par == 0:
                    dve.wait_ge(S.tailv, h + START)
                for j in range(GT):
                    dve.wait_ge(S.turn_prep, 6 * g + 5 + j // 2 + START)
                    src = ring[j // 2][:, j % 2, 0:3 * D].rearrange("p (a n) -> p a n", a=3)
                    for i, dst in enumerate((VA[par][:, j, :, 0:E], VL[par][:, j, :, 0:E], h_e(kraw[:, j, :]))):
                        V.tensor_tensor(dst, h_e(src[:, i, :]), h_e(btm[:, i, :]), ALU.add).then_inc(S.tm, 1)

            def prep(h, par):
                prep_logits(h, par)
                prep_residues(h, par)
                prep_values(h, par)

            def mx(h, par, follows, more):
                g = 2 * h + par
                after = h + par, 1 - par
                for k in range(4 * GT):
                    if follows and k == 0:
                        attended_softmax(GT * g - 1)
                    if follows and k == 1:
                        attended_linear(GT * g - 1)
                    if follows and k == 3:
                        add_mixed(g - 1, 1 - par, GT - 1)
                        hidden_stats(g - 1, GT - 1)
                    if follows and k == 4:
                        hidden_aggregate(g - 1)
                    if more and k == 7:
                        norm_stats(*after, 0)
                        norm_stats(*after, 1)
                    if more and k == 8:
                        norm_stats(*after, 2)
                        norm_stats(*after, 3)
                        norm_aggregate(*after)
                    if more and k == 11:
                        norm_apply(*after, 0)
                        norm_apply(*after, 1)
                    if more and k == 12:
                        norm_apply(*after, 2)
                        norm_apply(*after, 3)
                    if more and k == 14:
                        prep_logits(*after)
                    dve.wait_ge(S.turn_max, 16 * g + k + 1 + START)
                    n = P if par == 0 and k < 4 else 2 * P
                    j, q = divmod(k, 4)
                    V.tensor_reduce(mmax[:, j, 4 * q:4 * q + 4].rearrange("p (a b) -> p a b", a=2),
                                    ring[q % 2][:, :, 0:2 * n].rearrange("p a (b n) -> p a b n", b=2), AX_X, ALU.max)\
                        .then_inc(S.mred, 1)
                dve.wait_ge(S.mred, 16 * g + 16 + START)
                dve.wait_ge(S.mT_turn, g + START)
                V.tensor_scalar(MS[:, :, 0:H], mmax, -1.0, None, ALU.mult).then_inc(S.mparts, 1)
                dve.wait_ge(S.mparts, 4 * g + 1 + START)
                V.scalar_tensor_tensor(out=mres, in0=mmax, scalar=-1.0, in1=MS[:, :, 0:H], op0=ALU.mult, op1=ALU.subtract)\
                    .then_inc(S.mparts, 1)
                dve.wait_ge(S.mparts, 4 * g + 2 + START)
                V.tensor_copy(MS[:, :, H:2 * H], mres).then_inc(S.mparts, 1)
                dve.wait_ge(S.mparts, 4 * g + 3 + START)
                V.tensor_tensor(MS[:, :, 2 * H:3 * H], mres, MS[:, :, H:2 * H], ALU.subtract).then_inc(S.mparts, 1)
                if more:
                    prep_residues(*after)
                    prep_values(*after)

            def late_router(h, par):
                route_end(dve, S.rt0, S.rt0_exp, 2 * h + par, 0, cw0)

            def late_sum(h, par):
                g = 2 * h + par
                dve.wait_ge(S.lin_exp, g + 1 + START)
                V.scalar_tensor_tensor(out=Y32.rearrange("p a b -> p (a b)"), in0=Y32.rearrange("p a b -> p (a b)"), scalar=0.0,
                                       in1=eb.rearrange("p a b -> p (a b)"), op0=ALU.max, op1=ALU.add).then_inc(S.lin_sum, 1)

            def late(h, par):
                late_router(h, par)
                late_sum(h, par)

            def attend(h, par, last):
                g = 2 * h + par
                for j in range(GT):
                    t = GT * g + j
                    for i in range(2):
                        dve.wait_ge(S.turn_attend, 24 * g + 6 * j + i + 1 + START)
                        dve.wait_ge(S.ol_half if i == 0 else S.ol, t + START)
                        V.tensor_tensor(AB[i], ring[i][:, :, :].rearrange("p a (b c) -> p (a b) c", c=P),
                                        tri[:, :].unsqueeze(1).to_broadcast([P, 8, P]), ALU.mult).then_inc(S.amask, 1)
                    n = 7 * h + GT * par + j
                    if not (par == 0 and j == 0):
                        if par == 0 and j == 1:
                            dve.wait_ge(S.su, n + START)
                            V.tensor_copy(SB[:, :, 0:E + 1], SU).then_inc(S.sb, 1)
                        else:
                            dve.wait_ge(S.sb, n - 1 + START)
                            dve.wait_ge(S.su, n + START)
                            V.tensor_tensor(SB[:, :, 0:E + 1], SB[:, :, 0:E + 1], SU, ALU.add).then_inc(S.sb, 1)
                    if j > 0:
                        attended_softmax(t - 1)
                        attended_linear(t - 1)
                    if j == 0 and not last:
                        late_router(h + par, 1 - par)
                    if j == 1 and not last:
                        late_sum(h + par, 1 - par)
                    if j > 0:
                        add_mixed(g, par, j - 1)
                        hidden_stats(g, j - 1)
                    if not (par == 1 and j == GT - 1):
                        dve.wait_ge(S.state, n + 1 + START)
                        dve.wait_ge(S.sb, n + START)
                        V.tensor_tensor(SU, psY[:, 0:H * (E + 1)].rearrange("p (h e) -> p h e", h=H),
                                        bd[:, :].unsqueeze(2).to_broadcast([P, H, E + 1]), ALU.mult).then_inc(S.su, 1)

            attention_order(prep, late, attend, mx, norm, finish, dve)
            dve_rest(dve)

        @block.tensor
        def _(pe):
            T = nc.tensor
            pe.wait_ge(S.loaded, n_load[0])
            pe.wait_ge(S.consts, N_CONSTS)
            for i in range(8):
                m = T.transpose(ring[i // 4][:, 0, :].rearrange("p (a b) -> p a b", a=GT)[:, i % 4, :], wsq[:, i, :], ident[:, :])
            m.then_inc(S.wT, 1)
            T.transpose(psY[:, 0:EX], rw1r[:, :], ident[0:EX, 0:EX])
            pe.wait_ge(S.bperm, 4)
            for i in range(4):
                T.matmul(psY[:, 16 + i:17 + i], btmp[0:1, i, :], ones_row[0:1, 0:1], start=True, stop=True)
            pe.wait_ge(S.wTc, 2)
            pe.wait_ge(S.bsum, 1)
            T.matmul(psY[0:1, 32:32 + D], bcol[:, 2:3], wsq[:, 2, :], start=True, stop=True)
            T.matmul(psT[:, 0, :], wsqT[:, 0, :], wsq[:, 2, :], start=True, stop=True)
            T.matmul(psT[:, 1, :], wsqT[:, 1, :], wsq[:, 2, :], start=True, stop=True).then_inc(S.wmixed, 1)
            pe.wait_ge(S.actset, 5)
            pe.wait_ge(S.dveset, 15)
            T.transpose(psY[:, 0:EX], rw1r[:, :], ident[0:EX, 0:EX]).then_inc(S.setup, 1)
            pe.wait_ge(S.setup, SETUP)

            def tile(j):
                return slice(j * P, (j + 1) * P)

            def prep_part(h, par, k):
                g = 2 * h + par
                last = 16 * (g - 1) + START
                bank = ring[k % 2]
                if k == 0:
                    pe.wait_ge(S.mred, last + 13)
                    pe.wait_ge(S.lnp, 16 * g + 12 + START)
                    for j in range(GT):
                        m = T.transpose(bank[:, 0, tile(j)], XN[par][:, j, :], ident[:, :])
                elif k == 1:
                    pe.wait_ge(S.mred, last + 14)
                    pe.wait_ge(S.lnp, 16 * g + 16 + START)
                    for j in range(GT):
                        T.transpose(bank[:, 0, tile(j)], XH[:, j, :], ident[:, :])
                    pe.wait_ge(S.xnT, g + 1 + START)
                    for j in range(GT):
                        m = T.matmul(bank[:, 1, j * EX:(j + 1) * EX], xnT[:, tile(j)], rw0[:, :], start=True, stop=True)
                elif k < 4:
                    pe.wait_ge(S.xhT, g + 1 + START)
                    pe.wait_ge(S.logits, g + 1 + START)
                    pe.wait_ge(S.mred, last + 13 + k)
                    for i in range(2):
                        m = T.matmul(bank[:, i, :], wfm[:, 2 * (k - 2) + i, :], xhT, start=True, stop=True)
                else:
                    pe.wait_ge(S.resid if k == 4 else S.lin_y, 2 * g + 2 + START)
                    for i in range(2):
                        m = T.matmul(bank[:, i, 0:3 * D], xhT[:, tile(2 * (k - 4) + i)], wtm[:, :, :].rearrange("p a b -> p (a b)"),
                                     start=True, stop=True)
                m.then_inc(S.turn_prep, 1)

            def prep(h, par):
                for k in range(6):
                    prep_part(h, par, k)

            def scores(j, par, q, mask, rows, by_key):
                for a in range(2):
                    first = par == 0 and j == 0
                    bank = ring[q % 2][:, a, :]
                    if first:
                        T.matmul(bank[:, 0:2 * P].rearrange("p (b n) -> p b n", b=2), identb[:, :], mask[:, :, 1, :], start=True, stop=True)
                    else:
                        T.matmul(bank, identb[:, :], mask[:, :, :, :].rearrange("p a b c -> p (a b c)"), start=True, stop=True)
                for a in range(2):
                    for b in range(2):
                        hd = 4 * q + 2 * a + b
                        own = KS[par][0:rows, hd, tile(j)]
                        before = KS[par][0:rows, hd, tile(j - 1)] if j > 0 else KT[0:rows, hd, :]
                        blocks = [own] if first else [before, own]
                        for n, keys in enumerate(blocks):
                            c = (len(blocks) * b + n) * P
                            query = QS[par][0:rows, hd, tile(j)]
                            lhsT, rhs = (keys, query) if by_key else (query, keys)
                            m = T.matmul(ring[q % 2][:, a, c:c + P], lhsT, rhs, start=False, stop=True,
                                         skip_group_check=True)
                return m

            def hidden_turn(g):
                pe.wait_ge(S.lne, 12 * g + 12 + START)
                for j in range(GT):
                    m = T.transpose(psT[:, j, :], HN[:, j, :], ident[:, :])
                m.then_inc(S.hT_turn, 1)

            def minus_rows(h, par):
                g = 2 * h + par
                pe.wait_ge(S.mparts, 4 * g + 4 + START)
                pe.wait_ge(S.su, 7 * h + GT * par + START)
                pe.wait_ge(S.mT, g + START)
                pe.sem_inc(S.waits_alone, 1)
                for j in range(GT):
                    m = T.transpose(psY[:, 256:512].bitcast(BF16)[0:3 * H, tile(j)], MS[:, j, :], identb[:, :])
                m.then_inc(S.mT_turn, 1)

            def finish_part(u, g, part):
                if part == 0:
                    pe.wait_ge(S.oas, u + 1 + START)
                    pe.wait_ge(S.x1, u + START)
                    pe.wait_ge(S.hT, g + START)
                    for a in range(4):
                        m = T.transpose(psT[:, a, :], OAs[:, a, :], ident[:, :])
                    m.then_inc(S.t1, 1)
                elif part == 1:
                    pe.wait_ge(S.ols, u + 1 + START)
                    pe.wait_ge(S.at, u + 1 + START)
                    for a in range(4):
                        m = T.transpose(psT[:, a, :], OLs[:, a, :], ident[:, :])
                    m.then_inc(S.t2, 1)
                elif part == 2:
                    pe.wait_ge(S.lt, u + 1 + START)
                    for a in range(2):
                        m = T.transpose(psT[:, a, :], ATM[:, a, :], ident[:, :])
                    m.then_inc(S.y, 1)
                else:
                    pe.wait_ge(S.ast, u + 1 + START)
                    T.matmul(psT[:, 2, :], AST[:, 0, :], wmix[:, 0, :], start=True, stop=False)
                    T.matmul(psT[:, 2, :], AST[:, 1, :], wmix[:, 1, :], start=False, stop=False)
                    T.matmul(psT[:, 2, :], ones_row[:, :], bc_row[:, :], start=False, stop=True).then_inc(S.mix, 1)

            def finish(h, par):
                g = 2 * h + par
                for part in range(4):
                    finish_part(GT * g + GT - 1, g, part)
                hidden_turn(g)

            def mx(h, par, follows, more):
                g = 2 * h + par
                after = h + par, 1 - par
                pe.wait_ge(S.stack[0][par], 144 * (h + 1) + START)
                if par == 1:
                    pe.wait_ge(S.tails, 16 * (h + 1) + START)
                for k in range(4 * GT):
                    if k < 2:
                        pe.wait_ge(S.tm, 12 * g + 6 * (k + 1) + START)
                        pe.wait_ge(S.exps, 16 * g + START)
                    elif more and k == 14:
                        pe.wait_ge(S.xnT, g + 2 + START)
                    elif more and k == 15:
                        pe.wait_ge(S.xhT, g + 2 + START)
                        pe.wait_ge(S.logits, g + 2 + START)
                    else:
                        pe.wait_ge(S.mred, 16 * g + k - 1 + START)
                    scores(k // 4, par, k % 4, mqry, QK, False).then_inc(S.turn_max, 1)
                    if follows and k < 4:
                        finish_part(GT * g - 1, g - 1, k)
                    if follows and k == 11:
                        hidden_turn(g - 1)
                    if more and k == 13:
                        prep_part(*after, 0)
                        prep_part(*after, 1)
                if more:
                    prep_part(*after, 2)
                minus_rows(h, par)
                if more:
                    for k in range(3, 6):
                        prep_part(*after, k)

            def attend(h, par, last):
                g = 2 * h + par

                def values(j, q):
                    t = GT * g + j
                    pe.wait_ge(S.exps, 4 * t + q + 1 + START)
                    if q == 0:
                        pe.wait_ge(S.oas, t + START)
                        if j == 0 and par == 1:
                            pe.wait_ge(S.tailv, h + 1 + START)
                    first = par == 0 and j == 0
                    for a in range(4):
                        hd = 4 * q + a
                        before = VA[par][:, j - 1, hd, :] if j > 0 else VT[:, hd, :]
                        blocks = [VA[par][:, j, hd, :]] if first else [before, VA[par][:, j, hd, :]]
                        flat = PB[q % 2].rearrange("p a b c -> p (a b c)")
                        for n, v in enumerate(blocks):
                            c = (len(blocks) * a + n) * P
                            m = T.matmul(psA[32 * a:32 * a + E + 1, q, :], v, flat[:, c:c + P], start=(n == 0), stop=(n == len(blocks) - 1),
                                         skip_group_check=True)
                    m.then_inc(S.pv, 1)

                def products(j, i):
                    for k in range(8):
                        hd = 8 * i + k
                        m = T.matmul(ring[i][:, k // 4, (k % 4) * P:(k % 4 + 1) * P], KS[par][LR:LR + QK, hd, tile(j)],
                                     QS[par][LR:LR + QK, hd, tile(j)], start=True, stop=True)
                    m.then_inc(S.turn_attend, 1)

                pe.wait_ge(S.stack[1][par], 144 * (h + 1) + START)
                pe.wait_ge(S.mrow[par], 48 * (h + 1) + START)
                for j in range(GT):
                    t = GT * g + j
                    if j == 0:
                        for i in range(2):
                            if last:
                                pe.wait_ge(S.mred, 16 * g + 15 + i + START)
                            else:
                                pe.wait_ge(S.tm, 12 * (g + 1) + 6 * (i + 1) + START)
                            products(0, i)
                    if j > 0:
                        finish_part(t - 1, g, 0)
                    for q in range(4):
                        if q < 2:
                            pe.wait_ge(S.amask, 8 * g + 2 * j + q + 1 + START)
                        else:
                            pe.wait_ge(S.exps, 16 * g + 4 * j + q - 1 + START)
                        scores(j, par, q, mkey, QKM, True).then_inc(S.turn_attend, 1)
                        if q > 0:
                            values(j, q - 1)
                            if j > 0:
                                finish_part(t - 1, g, q)
                    values(j, 3)
                    n = 7 * h + GT * par + j
                    if not (par == 1 and j == GT - 1):
                        pe.wait_ge(S.kst, g + 1 + START)
                        pe.wait_ge(S.su, n + START)
                        pe.wait_ge(S.mT, g + 1 + START)
                        T.matmul(psY[:, 0:H * (E + 1)], KST[par][:, j, :], VL[par][:, j, :, :].rearrange("p h e -> p (h e)"),
                                 start=True, stop=True).then_inc(S.state, 1)
                    pe.wait_ge(S.lin_qk, 2 * g + 1 + START)
                    pe.wait_ge(S.ols, t + START)
                    pe.wait_ge(S.sb, n + START)
                    first = par == 0 and j == 0
                    for q in range(4):
                        if q % 2 == 0 and j < GT - 1:
                            pe.wait_ge(S.exps, 16 * g + 4 * j + 3 + q // 2 + START)
                            products(j + 1, q // 2)
                        if not first:
                            T.matmul(psL[:, q, :], SB[:, 4 * q:4 * q + 4, :].rearrange("p h e -> p (h e)"), QF[par][:, tile(j)],
                                     start=True, stop=True)
                        for a in range(4):
                            hd = 4 * q + a
                            m = T.matmul(psL[32 * a:32 * a + E + 1, q, :], VL[par][:, j, hd, :], AB[hd // 8][:, hd % 8, :],
                                         start=first, stop=True, skip_group_check=True)
                        if q == 1:
                            m.then_inc(S.ol_half, 1)
                    m.then_inc(S.ol, 1)

            attention_order(prep, nothing, attend, mx, nothing, finish, pe)
            pe_rest(pe)


_OUTS = [((8, 1024, 128), 'float32')]


def kernel(**inputs):
    import numpy as _np
    import concourse.bacc as _bacc
    from concourse import mybir as _mybir
    from concourse.bass_utils import run_bass_kernel_spmd as _run

    nc = _bacc.Bacc("TRN2", target_bir_lowering=False, num_devices=1)
    arrays, I = {}, {}
    for name in inputs:
        a = _np.ascontiguousarray(inputs[name])
        arrays[f"in_{name}_dram"] = a
        I[name] = nc.dram_tensor(f"in_{name}_dram", a.shape, _mybir.dt.from_np(a.dtype), kind="ExternalInput").ap()
    shape, dtype = _OUTS[0]
    out = nc.dram_tensor("out_0_dram", shape, _mybir.dt.from_np(_np.dtype(dtype)), kind="ExternalOutput").ap()
    build(nc, I, out)
    r = _run(nc, [arrays], core_ids=[0])
    return r.results[0]["out_0_dram"]
```
